# Optimizing a Trainium2 kernel written in Bass

```python
import numpy as np
import jax
import jax.numpy as jnp

def _softmax(x, axis=-1):
    return jax.nn.softmax(x, axis=axis)

def _gelu(x):
    return jax.nn.gelu(x, approximate=True)

def _silu(x):
    return jax.nn.silu(x)

def _sigmoid(x):
    return jax.nn.sigmoid(x)

def _layernorm(x, axis=-1, eps=1e-05):
    m = jnp.mean(x, axis=axis, keepdims=True)
    v = jnp.var(x, axis=axis, keepdims=True)
    return (x - m) / jnp.sqrt(v + eps)

def _scatter_add(tgt, idx, src, axis=0):
    return tgt.at[idx].add(src)

def _segment_sum(src, seg, n):
    return jax.ops.segment_sum(src, seg, n)
kernel_name = 'mk_xattn_seq_d2_seqx_r8_dd153b'

def setup_inputs(seed: int=0):
    np.random.seed(seed)
    _w = jnp.asarray

    def _rec_inputs():
        import jax
        import jax.numpy as jnp
        _rk = jax.random.key(seed)
        x = 7.22e-05 + 1 * jax.random.normal(jax.random.fold_in(_rk, 1), (16, 128, 128), jnp.float32)
        _lenS = 128 - jax.random.randint(jax.random.fold_in(_rk, 7), (16,), 0, max(1, 128 // 4) + 1, jnp.int32)
        _lenS2 = 128 - jax.random.randint(jax.random.fold_in(_rk, 8), (16,), 0, max(1, 128 // 4) + 1, jnp.int32)
        _ctx_1024P = jax.random.normal(jax.random.fold_in(_rk, 11), (16, 16, 128), jnp.float32)
        _ctx_1024c = jax.random.dirichlet(jax.random.fold_in(_rk, 511), 0.3 * jnp.ones((16,), jnp.float32), (16, 128))
        _ctx_1024t = jnp.einsum('bsk,bkd->bsd', _ctx_1024c, _ctx_1024P)
        _ctx_1024t = _ctx_1024t * jax.lax.rsqrt(jnp.mean(jnp.square(_ctx_1024t)) + 1e-12) * 0.953939
        ctx_1024 = 4.13588e-05 + 0.999923 * (_ctx_1024t + 0.3 * jax.random.normal(jax.random.fold_in(_rk, 611), (16, 128, 128), jnp.float32))
        _validS = jnp.arange(128)[None, :] < _lenS[:, None]
        _validS2 = jnp.arange(128)[None, :] < _lenS2[:, None]
        _causal = jnp.tril(jnp.ones((128, 128), dtype=bool))
        mask_BxSxS_ik0 = jnp.where(jnp.broadcast_to(_validS[:, None, :], (16, 128, 128)), 0, 1).astype(jnp.int32)
        mask_BxSxS2_if1 = jnp.where(jnp.ones((16, 128, 128), dtype=bool), 1, 0).astype(jnp.int32)
        return (x, ctx_1024, mask_BxSxS_ik0, mask_BxSxS2_if1)
    x, ctx_1024, mask_BxSxS_ik0, mask_BxSxS2_if1 = _rec_inputs()

    def _L0_xattn_setup():
        import jax, jax.numpy as jnp
        import numpy as np
        B, S, D, H, E, HID, K = (4, 256, 128, 16, 8, 512, 2)
        EPS = 1e-05

        def _layernorm(x, g, b):
            mu = jnp.mean(x, -1, keepdims=True)
            var = jnp.var(x, -1, keepdims=True)
            return (x - mu) * jax.lax.rsqrt(var + EPS) * g + b

        def _mha(q_in, k_in, v_in, wq, bq, wk, bk, wv, bv, wo, bo):
            Bq, Sq, Dm = q_in.shape
            hd = Dm // H
            q = (q_in @ wq + bq).reshape(Bq, Sq, H, hd)
            k = (k_in @ wk + bk).reshape(Bq, -1, H, hd)
            v = (v_in @ wv + bv).reshape(Bq, -1, H, hd)
            scores = jnp.einsum('bqhd,bkhd->bhqk', q, k) / np.sqrt(hd).astype(q.dtype)
            attn = jax.nn.softmax(scores, axis=-1)
            out = jnp.einsum('bhqk,bkhd->bqhd', attn, v).reshape(Bq, Sq, Dm)
            return out @ wo + bo

        def _moe(x, r_w, r_b, e_w1, e_b1, e_w2, e_b2):
            xf = x.reshape(-1, D)
            T = xf.shape[0]
            probs = jax.nn.softmax(xf @ r_w + r_b, axis=-1)
            vals, idx = jax.lax.top_k(probs, K)
            vals = vals / jnp.sum(vals, -1, keepdims=True)
            cw = jnp.zeros((T, E), dtype=x.dtype).at[jnp.arange(T)[:, None], idx].add(vals)
            out = jnp.zeros_like(xf)
            for e in range(E):
                y = jax.nn.relu(xf @ e_w1[e] + e_b1[e]) @ e_w2[e] + e_b2[e]
                out = out + cw[:, e:e + 1] * y
            return out.reshape(x.shape)
        key = jax.random.key(seed)
        ks = jax.random.split(key, 24)
        sc = 0.02
        p = {'tgt': jax.random.normal(ks[0], (B, S, D), jnp.float32), 'memory': jax.random.normal(ks[1], (B, S, D), jnp.float32), 'sa_wq': jax.random.normal(ks[2], (D, D)) * sc, 'sa_bq': jnp.zeros((D,)), 'sa_wk': jax.random.normal(ks[3], (D, D)) * sc, 'sa_bk': jnp.zeros((D,)), 'sa_wv': jax.random.normal(ks[4], (D, D)) * sc, 'sa_bv': jnp.zeros((D,)), 'sa_wo': jax.random.normal(ks[5], (D, D)) * sc, 'sa_bo': jnp.zeros((D,)), 'ca_wq': jax.random.normal(ks[6], (D, D)) * sc, 'ca_bq': jnp.zeros((D,)), 'ca_wk': jax.random.normal(ks[7], (D, D)) * sc, 'ca_bk': jnp.zeros((D,)), 'ca_wv': jax.random.normal(ks[8], (D, D)) * sc, 'ca_bv': jnp.zeros((D,)), 'ca_wo': jax.random.normal(ks[9], (D, D)) * sc, 'ca_bo': jnp.zeros((D,)), 'r_w': jax.random.normal(ks[10], (D, E)) * sc, 'r_b': jnp.zeros((E,)), 'e_w1': jax.random.normal(ks[11], (E, D, HID)) * sc, 'e_b1': jnp.zeros((E, HID)), 'e_w2': jax.random.normal(ks[12], (E, HID, D)) * sc, 'e_b2': jnp.zeros((E, D)), 'n1_g': jnp.ones((D,)), 'n1_b': jnp.zeros((D,)), 'n2_g': jnp.ones((D,)), 'n2_b': jnp.zeros((D,)), 'n3_g': jnp.ones((D,)), 'n3_b': jnp.zeros((D,))}
        return p
    _L0_xattn_all = _L0_xattn_setup()
    _L0_xattn_in = {k: v for k, v in _L0_xattn_all.items() if k in ('sa_wq', 'sa_bq', 'sa_wk', 'sa_bk', 'sa_wv', 'sa_bv', 'sa_wo', 'sa_bo', 'ca_wq', 'ca_bq', 'ca_wk', 'ca_bk', 'ca_wv', 'ca_bv', 'ca_wo', 'ca_bo', 'r_w', 'r_b', 'e_w1', 'e_b1', 'e_w2', 'e_b2', 'n1_g', 'n1_b', 'n2_g', 'n2_b', 'n3_g', 'n3_b')}
    del _L0_xattn_all

    def _L1_xattn_setup():
        import jax, jax.numpy as jnp
        import numpy as np
        B, T, S_ENC, D, H, E, K = (4, 128, 64, 128, 16, 8, 2)
        DK = D // H
        HID = 4 * D
        NEG = -65504.0
        EPS = 1e-05

        def rmsnorm(x, w):
            return w * (x * jax.lax.rsqrt(jnp.mean(x * x, axis=-1, keepdims=True) + EPS))

        def mha(xq, xk, xv, mask, wq, wk, wv, wo):
            q = jnp.einsum('bsd,ed->bse', xq, wq).reshape(xq.shape[0], -1, H, DK).transpose(0, 2, 1, 3)
            k = jnp.einsum('bsd,ed->bse', xk, wk).reshape(xk.shape[0], -1, H, DK).transpose(0, 2, 1, 3)
            v = jnp.einsum('bsd,ed->bse', xv, wv).reshape(xv.shape[0], -1, H, DK).transpose(0, 2, 1, 3)
            scores = jnp.einsum('bhqd,bhkd->bhqk', q, k) / jnp.sqrt(jnp.float32(DK))
            scores = jnp.where(mask[:, None, :, :] == 0, NEG, scores)
            attn = jax.nn.softmax(scores, axis=-1)
            out = jnp.einsum('bhqk,bhkd->bhqd', attn, v)
            out = out.transpose(0, 2, 1, 3).reshape(xq.shape[0], -1, D)
            return jnp.einsum('bsd,ed->bse', out, wo)

        def moe_ffn(x, gate_w, exp_w1, exp_w2, sh_w1, sh_w2):
            b, s, d = x.shape
            xf = x.reshape(-1, d)
            sh = jnp.einsum('nd,hd->nh', xf, sh_w1)
            sh = jax.nn.silu(sh)
            sh = jnp.einsum('nh,dh->nd', sh, sh_w2)
            logits = jnp.einsum('nd,ed->ne', xf, gate_w)
            topk_vals, topk_idx = jax.lax.top_k(logits, K)
            topk_gates = jax.nn.softmax(topk_vals, axis=-1)
            n = xf.shape[0]
            gates = jnp.zeros((n, E), dtype=xf.dtype).at[jnp.arange(n)[:, None], topk_idx].set(topk_gates)
            h = jnp.einsum('nd,ehd->neh', xf, exp_w1)
            h = jax.nn.silu(h)
            eo = jnp.einsum('neh,edh->ned', h, exp_w2)
            sel = jnp.einsum('ned,ne->nd', eo, gates)
            return (sh + sel).reshape(b, s, d)
        key = jax.random.key(seed)
        ks = jax.random.split(key, 16)
        sd = 1.0 / np.sqrt(D)
        inp = {'x': jax.random.normal(ks[0], (B, T, D), jnp.float32), 'encoder_output': jax.random.normal(ks[1], (B, S_ENC, D), jnp.float32), 'tgt_mask': jnp.tril(jnp.ones((T, T), jnp.int32))[None].repeat(B, 0), 'src_mask': jnp.ones((B, T, S_ENC), jnp.int32), 'norm1_w': jnp.ones((D,), jnp.float32), 'norm2_w': jnp.ones((D,), jnp.float32), 'norm3_w': jnp.ones((D,), jnp.float32), 'sa_wq': jax.random.normal(ks[2], (D, D), jnp.float32) * sd, 'sa_wk': jax.random.normal(ks[3], (D, D), jnp.float32) * sd, 'sa_wv': jax.random.normal(ks[4], (D, D), jnp.float32) * sd, 'sa_wo': jax.random.normal(ks[5], (D, D), jnp.float32) * sd, 'ca_wq': jax.random.normal(ks[6], (D, D), jnp.float32) * sd, 'ca_wk': jax.random.normal(ks[7], (D, D), jnp.float32) * sd, 'ca_wv': jax.random.normal(ks[8], (D, D), jnp.float32) * sd, 'ca_wo': jax.random.normal(ks[9], (D, D), jnp.float32) * sd, 'gate_w': jax.random.normal(ks[10], (E, D), jnp.float32) * 0.02, 'exp_w1': jax.random.normal(ks[11], (E, HID, D), jnp.float32) * sd, 'exp_w2': jax.random.normal(ks[12], (E, D, HID), jnp.float32) / np.sqrt(HID), 'sh_w1': jax.random.normal(ks[13], (HID, D), jnp.float32) * sd, 'sh_w2': jax.random.normal(ks[14], (D, HID), jnp.float32) / np.sqrt(HID)}
        return inp
    _L1_xattn_all = _L1_xattn_setup()
    _L1_xattn_in = {k: v for k, v in _L1_xattn_all.items() if k in ('norm1_w', 'norm2_w', 'norm3_w', 'sa_wq', 'sa_wk', 'sa_wv', 'sa_wo', 'ca_wq', 'ca_wk', 'ca_wv', 'ca_wo', 'gate_w', 'exp_w1', 'exp_w2', 'sh_w1', 'sh_w2')}
    del _L1_xattn_all
    return {'x': x, 'ctx_1024': ctx_1024, 'mask_BxSxS_ik0': mask_BxSxS_ik0, 'mask_BxSxS2_if1': mask_BxSxS2_if1, 'L0_xattn_sa_wq': _L0_xattn_in['sa_wq'], 'L0_xattn_sa_bq': _L0_xattn_in['sa_bq'], 'L0_xattn_sa_wk': _L0_xattn_in['sa_wk'], 'L0_xattn_sa_bk': _L0_xattn_in['sa_bk'], 'L0_xattn_sa_wv': _L0_xattn_in['sa_wv'], 'L0_xattn_sa_bv': _L0_xattn_in['sa_bv'], 'L0_xattn_sa_wo': _L0_xattn_in['sa_wo'], 'L0_xattn_sa_bo': _L0_xattn_in['sa_bo'], 'L0_xattn_ca_wq': _L0_xattn_in['ca_wq'], 'L0_xattn_ca_bq': _L0_xattn_in['ca_bq'], 'L0_xattn_ca_wk': _L0_xattn_in['ca_wk'], 'L0_xattn_ca_bk': _L0_xattn_in['ca_bk'], 'L0_xattn_ca_wv': _L0_xattn_in['ca_wv'], 'L0_xattn_ca_bv': _L0_xattn_in['ca_bv'], 'L0_xattn_ca_wo': _L0_xattn_in['ca_wo'], 'L0_xattn_ca_bo': _L0_xattn_in['ca_bo'], 'L0_xattn_r_w': _L0_xattn_in['r_w'], 'L0_xattn_r_b': _L0_xattn_in['r_b'], 'L0_xattn_e_w1': _L0_xattn_in['e_w1'], 'L0_xattn_e_b1': _L0_xattn_in['e_b1'], 'L0_xattn_e_w2': _L0_xattn_in['e_w2'], 'L0_xattn_e_b2': _L0_xattn_in['e_b2'], 'L0_xattn_n1_g': _L0_xattn_in['n1_g'], 'L0_xattn_n1_b': _L0_xattn_in['n1_b'], 'L0_xattn_n2_g': _L0_xattn_in['n2_g'], 'L0_xattn_n2_b': _L0_xattn_in['n2_b'], 'L0_xattn_n3_g': _L0_xattn_in['n3_g'], 'L0_xattn_n3_b': _L0_xattn_in['n3_b'], 'L1_xattn_norm1_w': _L1_xattn_in['norm1_w'], 'L1_xattn_norm2_w': _L1_xattn_in['norm2_w'], 'L1_xattn_norm3_w': _L1_xattn_in['norm3_w'], 'L1_xattn_sa_wq': _L1_xattn_in['sa_wq'], 'L1_xattn_sa_wk': _L1_xattn_in['sa_wk'], 'L1_xattn_sa_wv': _L1_xattn_in['sa_wv'], 'L1_xattn_sa_wo': _L1_xattn_in['sa_wo'], 'L1_xattn_ca_wq': _L1_xattn_in['ca_wq'], 'L1_xattn_ca_wk': _L1_xattn_in['ca_wk'], 'L1_xattn_ca_wv': _L1_xattn_in['ca_wv'], 'L1_xattn_ca_wo': _L1_xattn_in['ca_wo'], 'L1_xattn_gate_w': _L1_xattn_in['gate_w'], 'L1_xattn_exp_w1': _L1_xattn_in['exp_w1'], 'L1_xattn_exp_w2': _L1_xattn_in['exp_w2'], 'L1_xattn_sh_w1': _L1_xattn_in['sh_w1'], 'L1_xattn_sh_w2': _L1_xattn_in['sh_w2']}

def reference(x, ctx_1024, mask_BxSxS_ik0, mask_BxSxS2_if1, L0_xattn_sa_wq, L0_xattn_sa_bq, L0_xattn_sa_wk, L0_xattn_sa_bk, L0_xattn_sa_wv, L0_xattn_sa_bv, L0_xattn_sa_wo, L0_xattn_sa_bo, L0_xattn_ca_wq, L0_xattn_ca_bq, L0_xattn_ca_wk, L0_xattn_ca_bk, L0_xattn_ca_wv, L0_xattn_ca_bv, L0_xattn_ca_wo, L0_xattn_ca_bo, L0_xattn_r_w, L0_xattn_r_b, L0_xattn_e_w1, L0_xattn_e_b1, L0_xattn_e_w2, L0_xattn_e_b2, L0_xattn_n1_g, L0_xattn_n1_b, L0_xattn_n2_g, L0_xattn_n2_b, L0_xattn_n3_g, L0_xattn_n3_b, L1_xattn_norm1_w, L1_xattn_norm2_w, L1_xattn_norm3_w, L1_xattn_sa_wq, L1_xattn_sa_wk, L1_xattn_sa_wv, L1_xattn_sa_wo, L1_xattn_ca_wq, L1_xattn_ca_wk, L1_xattn_ca_wv, L1_xattn_ca_wo, L1_xattn_gate_w, L1_xattn_exp_w1, L1_xattn_exp_w2, L1_xattn_sh_w1, L1_xattn_sh_w2):
    import jax
    import jax.numpy as jnp

    def _L0_xattn_ref(tgt, memory, sa_wq, sa_bq, sa_wk, sa_bk, sa_wv, sa_bv, sa_wo, sa_bo, ca_wq, ca_bq, ca_wk, ca_bk, ca_wv, ca_bv, ca_wo, ca_bo, r_w, r_b, e_w1, e_b1, e_w2, e_b2, n1_g, n1_b, n2_g, n2_b, n3_g, n3_b):
        import jax, jax.numpy as jnp
        import numpy as np
        B, S, D, H, E, HID, K = (4, 256, 128, 16, 8, 512, 2)
        EPS = 1e-05

        def _layernorm(x, g, b):
            mu = jnp.mean(x, -1, keepdims=True)
            var = jnp.var(x, -1, keepdims=True)
            return (x - mu) * jax.lax.rsqrt(var + EPS) * g + b

        def _mha(q_in, k_in, v_in, wq, bq, wk, bk, wv, bv, wo, bo):
            Bq, Sq, Dm = q_in.shape
            hd = Dm // H
            q = (q_in @ wq + bq).reshape(Bq, Sq, H, hd)
            k = (k_in @ wk + bk).reshape(Bq, -1, H, hd)
            v = (v_in @ wv + bv).reshape(Bq, -1, H, hd)
            scores = jnp.einsum('bqhd,bkhd->bhqk', q, k) / np.sqrt(hd).astype(q.dtype)
            attn = jax.nn.softmax(scores, axis=-1)
            out = jnp.einsum('bhqk,bkhd->bqhd', attn, v).reshape(Bq, Sq, Dm)
            return out @ wo + bo

        def _moe(x, r_w, r_b, e_w1, e_b1, e_w2, e_b2):
            xf = x.reshape(-1, D)
            T = xf.shape[0]
            probs = jax.nn.softmax(xf @ r_w + r_b, axis=-1)
            vals, idx = jax.lax.top_k(probs, K)
            vals = vals / jnp.sum(vals, -1, keepdims=True)
            cw = jnp.zeros((T, E), dtype=x.dtype).at[jnp.arange(T)[:, None], idx].add(vals)
            out = jnp.zeros_like(xf)
            for e in range(E):
                y = jax.nn.relu(xf @ e_w1[e] + e_b1[e]) @ e_w2[e] + e_b2[e]
                out = out + cw[:, e:e + 1] * y
            return out.reshape(x.shape)
        t2 = _mha(tgt, tgt, tgt, sa_wq, sa_bq, sa_wk, sa_bk, sa_wv, sa_bv, sa_wo, sa_bo)
        x = _layernorm(tgt + t2, n1_g, n1_b)
        t2 = _mha(x, memory, memory, ca_wq, ca_bq, ca_wk, ca_bk, ca_wv, ca_bv, ca_wo, ca_bo)
        x = _layernorm(x + t2, n2_g, n2_b)
        t2 = _moe(x, r_w, r_b, e_w1, e_b1, e_w2, e_b2)
        x = _layernorm(x + t2, n3_g, n3_b)
        return x

    def _L1_xattn_ref(x, encoder_output, tgt_mask, src_mask, norm1_w, norm2_w, norm3_w, sa_wq, sa_wk, sa_wv, sa_wo, ca_wq, ca_wk, ca_wv, ca_wo, gate_w, exp_w1, exp_w2, sh_w1, sh_w2):
        import jax, jax.numpy as jnp
        import numpy as np
        B, T, S_ENC, D, H, E, K = (4, 128, 64, 128, 16, 8, 2)
        DK = D // H
        HID = 4 * D
        NEG = -65504.0
        EPS = 1e-05

        def rmsnorm(x, w):
            return w * (x * jax.lax.rsqrt(jnp.mean(x * x, axis=-1, keepdims=True) + EPS))

        def mha(xq, xk, xv, mask, wq, wk, wv, wo):
            q = jnp.einsum('bsd,ed->bse', xq, wq).reshape(xq.shape[0], -1, H, DK).transpose(0, 2, 1, 3)
            k = jnp.einsum('bsd,ed->bse', xk, wk).reshape(xk.shape[0], -1, H, DK).transpose(0, 2, 1, 3)
            v = jnp.einsum('bsd,ed->bse', xv, wv).reshape(xv.shape[0], -1, H, DK).transpose(0, 2, 1, 3)
            scores = jnp.einsum('bhqd,bhkd->bhqk', q, k) / jnp.sqrt(jnp.float32(DK))
            scores = jnp.where(mask[:, None, :, :] == 0, NEG, scores)
            attn = jax.nn.softmax(scores, axis=-1)
            out = jnp.einsum('bhqk,bhkd->bhqd', attn, v)
            out = out.transpose(0, 2, 1, 3).reshape(xq.shape[0], -1, D)
            return jnp.einsum('bsd,ed->bse', out, wo)

        def moe_ffn(x, gate_w, exp_w1, exp_w2, sh_w1, sh_w2):
            b, s, d = x.shape
            xf = x.reshape(-1, d)
            sh = jnp.einsum('nd,hd->nh', xf, sh_w1)
            sh = jax.nn.silu(sh)
            sh = jnp.einsum('nh,dh->nd', sh, sh_w2)
            logits = jnp.einsum('nd,ed->ne', xf, gate_w)
            topk_vals, topk_idx = jax.lax.top_k(logits, K)
            topk_gates = jax.nn.softmax(topk_vals, axis=-1)
            n = xf.shape[0]
            gates = jnp.zeros((n, E), dtype=xf.dtype).at[jnp.arange(n)[:, None], topk_idx].set(topk_gates)
            h = jnp.einsum('nd,ehd->neh', xf, exp_w1)
            h = jax.nn.silu(h)
            eo = jnp.einsum('neh,edh->ned', h, exp_w2)
            sel = jnp.einsum('ned,ne->nd', eo, gates)
            return (sh + sel).reshape(b, s, d)
        xn = rmsnorm(x, norm1_w)
        h = x + mha(xn, xn, xn, tgt_mask, sa_wq, sa_wk, sa_wv, sa_wo)
        hn = rmsnorm(h, norm2_w)
        h = h + mha(hn, encoder_output, encoder_output, src_mask, ca_wq, ca_wk, ca_wv, ca_wo)
        hn = rmsnorm(h, norm3_w)
        return h + moe_ffn(hn, gate_w, exp_w1, exp_w2, sh_w1, sh_w2)
    x = _L0_xattn_ref(x, ctx_1024, L0_xattn_sa_wq, L0_xattn_sa_bq, L0_xattn_sa_wk, L0_xattn_sa_bk, L0_xattn_sa_wv, L0_xattn_sa_bv, L0_xattn_sa_wo, L0_xattn_sa_bo, L0_xattn_ca_wq, L0_xattn_ca_bq, L0_xattn_ca_wk, L0_xattn_ca_bk, L0_xattn_ca_wv, L0_xattn_ca_bv, L0_xattn_ca_wo, L0_xattn_ca_bo, L0_xattn_r_w, L0_xattn_r_b, L0_xattn_e_w1, L0_xattn_e_b1, L0_xattn_e_w2, L0_xattn_e_b2, L0_xattn_n1_g, L0_xattn_n1_b, L0_xattn_n2_g, L0_xattn_n2_b, L0_xattn_n3_g, L0_xattn_n3_b)
    x = _L1_xattn_ref(x, ctx_1024, mask_BxSxS_ik0, mask_BxSxS2_if1, L1_xattn_norm1_w, L1_xattn_norm2_w, L1_xattn_norm3_w, L1_xattn_sa_wq, L1_xattn_sa_wk, L1_xattn_sa_wv, L1_xattn_sa_wo, L1_xattn_ca_wq, L1_xattn_ca_wk, L1_xattn_ca_wv, L1_xattn_ca_wo, L1_xattn_gate_w, L1_xattn_exp_w1, L1_xattn_exp_w2, L1_xattn_sh_w1, L1_xattn_sh_w2)
    return x

_drawn_inputs = setup_inputs


def setup_inputs(seed=0):
    import zlib

    import numpy as np

    out = dict(_drawn_inputs(seed))
    spreads = {'L0_xattn_sa_bq': (0.0, 0.8),
     'L0_xattn_sa_bk': (0.0, 0.8),
     'L0_xattn_sa_bv': (0.0, 0.1),
     'L0_xattn_sa_bo': (0.0, 0.1),
     'L0_xattn_ca_bq': (0.0, 0.8),
     'L0_xattn_ca_bk': (0.0, 0.8),
     'L0_xattn_ca_bv': (0.0, 0.1),
     'L0_xattn_ca_bo': (0.0, 0.1),
     'L0_xattn_r_b': (0.0, 0.1),
     'L0_xattn_e_b1': (0.0, 0.1),
     'L0_xattn_e_b2': (0.0, 0.1),
     'L0_xattn_n1_g': (1.0, 0.2),
     'L0_xattn_n1_b': (0.0, 0.1),
     'L0_xattn_n2_g': (1.0, 0.2),
     'L0_xattn_n2_b': (0.0, 0.1),
     'L0_xattn_n3_g': (1.0, 0.2),
     'L0_xattn_n3_b': (0.0, 0.1),
     'L1_xattn_norm1_w': (1.0, 0.2),
     'L1_xattn_norm2_w': (1.0, 0.2),
     'L1_xattn_norm3_w': (1.0, 0.2)}
    factors = {'L0_xattn_sa_wq': 8.0,
     'L0_xattn_sa_wk': 8.0,
     'L0_xattn_sa_wv': 3.295,
     'L0_xattn_ca_wq': 8.0,
     'L0_xattn_ca_wk': 8.0}
    for name, (base, spread) in spreads.items():
        noise = np.random.default_rng([zlib.crc32(name.encode()), seed]).standard_normal(out[name].shape)
        drawn = base * np.exp(spread * noise) if base else spread * noise
        out[name] = jnp.asarray(drawn.astype(out[name].dtype))
    for name, factor in factors.items():
        out[name] = (out[name] * factor).astype(out[name].dtype)
    return out
```

```python
from contextlib import ExitStack

import concourse.bass as bass
from concourse import mybir

F32 = mybir.dt.float32
BF16 = mybir.dt.bfloat16
I32 = mybir.dt.int32
ALU = mybir.AluOpType
ACT = mybir.ActivationFunctionType
AX = mybir.AxisListType

B, S, D = 16, 128, 128
H, HD = 16, 8
E0, E1, HID = 8, 9, 512
NE = 8
GB = 4
GROUPS = B // GB
T = GB * S
HC = HID // 128
HALF = H // 2
SR = 32
KR = HALF * HD + SR
STEPS = 16
LSTEPS = STEPS // 2
SCALE = float(HD) ** -0.5
EPS = 1e-5
NEG = -65504.0
BIG = 1e30

ROWS = ["sa_bv", "ca_bv", "sa_bo", "ca_bo", "n1_g", "n1_b", "n2_g", "n2_b", "n3_g", "n3_b"]
COLS = ["n1_g", "n1_b", "n2_g", "n2_b", "norm1_w", "norm2_w", "norm3_w"]


class Signal:

    def __init__(self, sem, per):
        self.sem, self.per = sem, per

    def at(self, turn, k):
        return turn * self.per + k


def two_layers(nc, x_tok, x_feat, ctx_feat, m_self, m_selfT, m_cross, m_crossT, att_w, w1_0, w2_0,
               w1_1, w2_1, gate_w, rows, cols, cols64, b1c, b2, ident, identb, hmask, shift_ones,
               before, out):
    ctx = ExitStack()
    with ctx:
        def sb(name, shape, dt=F32):
            return ctx.enter_context(nc.sbuf_tensor(name, shape, dt))

        def sig(name, per):
            return Signal(ctx.enter_context(nc.semaphore(name)), per)

        WA = sb("WA", [128, 16, 128])
        W1 = [sb("W1a", [128, E0, HID]), sb("W1b", [128, E1, HID])]
        W2 = [sb("W2a", [128, E0, HC, D]), sb("W2b", [128, E1, HC, D])]
        GW = sb("GW", [128, 2, NE])
        RV = sb("RV", [128, len(ROWS) * D + NE])
        CV = sb("CV", [128, len(COLS)])
        C64 = sb("C64", [64, 8])
        QB = sb("QB", [64, 4])
        B1 = sb("B1", [128, E0, HC])
        B2 = sb("B2", [NE, D])
        ID = sb("ID", [128, 128])
        IDB = sb("IDB", [128, 128], BF16)
        HM = sb("HM", [64, HALF])
        BEF = sb("BEF", [128, NE, NE])
        BS = sb("BS", [128, 2, D])
        EXPN = sb("EXPN", [128, 3])
        TICK = sb("TICK", [128, 2])
        Xin = sb("Xin", [128, GB, D])
        XFin = sb("XFin", [128, T])
        CF = sb("CF", [128, T])
        X = sb("X", [128, GB, D])
        XA = sb("XA", [128, T])
        XB = sb("XB", [128, T])
        XC = sb("XC", [128, T])
        MI = sb("MI", [128, 4, GB, S], I32)
        MA = sb("MA", [128, 4, GB, S], BF16)
        MZ = sb("MZ", [128, 2, GB, S])
        MF = sb("MF", [128, 2, GB, 4])
        K9 = sb("K9", [64, 2, 2, S])
        KX = [sb(f"KX{i}", [KR, H, S]) for i in range(4)]
        KB = [sb(f"KB{i}", [KR, H, S], BF16) for i in range(2)]
        Q9 = [sb(f"Q9{i}", [KR, 2, S]) for i in range(4)]
        QS = [sb(f"QS{i}", [KR, 2, S], BF16) for i in range(4)]
        VA = [sb(f"VA{i}", [128, H, HD + 1]) for i in range(4)]
        MX = sb("MX", [128, 2, H])
        NM = sb("NM", [128, 2, 2, SR])
        PT = sb("PT", [128, 4, 4, S])
        CA = sb("CA", [128, 2, H])
        CE = sb("CE", [128, 2, H])
        OT = sb("OT", [128, 2, 4, S])
        CW = sb("CW", [128, H, HD + 1])
        OW = sb("OW", [128, H, HD + 1])
        RS = sb("RS", [128, 2, H])
        AN = sb("AN", [128, 2, D])
        AT = sb("AT", [128, 2, S])
        RR = sb("RR", [128, 2, D])
        BN = sb("BN", [128, 2, 6])
        MV = sb("MV", [128, 2, 2])
        SQ = sb("SQ", [128, D])
        SS = sb("SS", [128, 2])
        RE = sb("RE", [128, 2])
        RD = sb("RD", [128, 2])
        YN = sb("YN", [128, 2, D])
        YG = sb("YG", [128, D])
        HT = sb("HT", [128, 2, HC, T])
        LG = sb("LG", [128, GB, NE])
        LM = sb("LM", [128, GB])
        LZ = sb("LZ", [128, GB, NE])
        LE = sb("LE", [128, GB, NE])
        GT = sb("GT", [128, GB, NE, NE])
        EQ = sb("EQ", [128, GB, NE, NE])
        RK = sb("RK", [128, GB, NE])
        GE = sb("GE", [128, GB, NE])
        GS = sb("GS", [128, GB])
        GR = sb("GR", [128, GB])
        G = sb("G", [128, GB, NE])
        GTT = sb("GTT", [NE, GB, 128])

        bank = [ctx.enter_context(nc.psum_tensor(f"bank{i}", [128, 512], F32)) for i in range(8)]
        S1B, S2B, OB, TB, PB, MB = bank[0:2], bank[2:4], bank[4], bank[5], bank[6], bank[7]
        HB, YB = bank[0:4], bank[4:6]
        PK, PV, PQ = PB[0:64, 0:256], PB[:, 256:384], PB[0:64, 0:256]

        w_in = sig("w_in", 0)
        moe_w = [sig("moe_w0", 0), sig("moe_w1", 0)]
        x_in = sig("x_in", 16)
        xf_in = sig("xf_in", 16)
        c_in = sig("c_in", 16)
        m_in = sig("m_in", 64)
        out_done = sig("out_done", 16)
        c_zero = sig("c_zero", 0)
        c_qb = sig("c_qb", 0)
        c_bs = sig("c_bs", 0)
        kx_ones = sig("kx_ones", 0)
        kb_ones = sig("kb_ones", 0)
        pk = sig("pk", 16)
        pq = sig("pq", 16)
        s1 = sig("s1", 64)
        nmt = sig("nmt", 16)
        s2 = sig("s2", 64)
        av = sig("av", 64)
        wz = sig("wz", 8)
        ott = sig("ott", 16)
        ant = sig("ant", 16)
        zo = sig("zo", 16)
        xtt = sig("xtt", 20)
        lgt = sig("lgt", 2)
        gtt = sig("gtt", 1)
        b2t = sig("b2t", 1)
        ht = sig("ht", 4 * (E0 + E1))
        yt = sig("yt", E0 + E1)
        k9 = sig("k9", 16)
        va = sig("va", 16)
        kb = sig("kb", 16)
        mx = sig("mx", 64)
        nm = sig("nm", 16)
        ca = sig("ca", 8)
        cw = sig("cw", 8)
        ow = sig("ow", 8)
        rs = sig("rs", 16)
        an = sig("an", 16)
        rr = sig("rr", 16)
        bns = sig("bns", 12)
        mv = sig("mv", 12)
        ss = sig("ss", 12)
        yn = sig("yn", 24)
        lg = sig("lg", 2)
        lm = sig("lm", 2)
        lz = sig("lz", 2)
        lgr = sig("lgr", 8)
        ge = sig("ge", 2)
        gs = sig("gs", 2)
        gr = sig("gr", 2)
        gg = sig("gg", 2)
        xb2 = sig("xb2", 1)
        hd = sig("hd", 2 * E0)
        acc = sig("acc", E0 + E1)
        mf = sig("mf", 3)
        q9 = sig("q9", 16)
        qs = sig("qs", 16)
        nmc = sig("nmc", 16)
        ce = sig("ce", 8)
        ex = sig("ex", 64)
        otc = sig("otc", 16)
        atc = sig("atc", 16)
        xtc = sig("xtc", 20)
        le = sig("le", 2)
        gtc = sig("gtc", 1)
        ha = sig("ha", 2 * E0 + 4 * E1)
        x0 = sig("x0", 1)
        ma = sig("ma", 1)
        mz = sig("mz", 1)
        kx = sig("kx", 16)
        re = sig("re", 24)
        rd = sig("rd", 24)
        yg = sig("yg", 12)
        xg = sig("xg", 12)

        def norm_no(n):
            return n if n < LSTEPS else n + 2 * GB

        def xt_no(n):
            return n if n < LSTEPS else n + GB

        def row(name):
            i = ROWS.index(name)
            return RV[:, i * D:(i + 1) * D]

        def col(name):
            i = COLS.index(name)
            return CV[:, i:i + 1]

        def stage(n):
            return n // LSTEPS, n % LSTEPS // GB, n % GB

        def tok(t, b):
            return t[:, b * S:(b + 1) * S]

        def q_input(n):
            l, a, b = stage(n)
            return tok([[XFin, XB], [XA, XB]][l][a], b)

        def kv_input(n):
            l, a, b = stage(n)
            return tok(CF if a else [XFin, XA][l], b)

        def late(l, ok):
            return [s for s in range(LSTEPS) if ok(s)]

        block = ctx.enter_context(nc.Block())

        @block.sync
        def _(sp):
            sp.sem_inc(out_done.sem, 16)
            consts = [(WA, att_w), (ID, ident), (HM, hmask), (C64, cols64), (RV, None), (CV, cols),
                      (IDB, identb), (GW, gate_w), (B1, b1c), (B2, b2), (BEF, None)]

            def group_in(tile, src, at, done):
                sp.dma_start(tile, src(at)).then_inc(done.sem, 16)

            src_x = lambda g: x_tok[:, bass.ds(g * GB, GB), :]
            src_f = lambda g: x_feat[:, bass.ds(g * T, T)]
            src_c = lambda g: ctx_feat[:, bass.ds(g * T, T)]
            masks = (m_self, m_selfT, m_cross, m_crossT)

            group_in(XFin[:], src_f, 0, xf_in)
            for tile, src in consts:
                if src is None:
                    r = rows if tile is RV else before
                    src = bass.AP(r.tensor, 0, [[0, 128], [1, r.shape[1]]])
                    dst = tile[:] if tile is RV else tile[:].rearrange("p i j -> p (i j)")
                    sp.dma_start(dst, src).then_inc(w_in.sem, 16)
                else:
                    sp.dma_start(tile[:], src).then_inc(w_in.sem, 16)
            for t in KX:
                sp.dma_start(t[KR - SR:KR], shift_ones).then_inc(kx_ones.sem, 16)
            group_in(CF[:], src_c, 0, c_in)
            group_in(Xin[:], src_x, 0, x_in)
            for i, m in enumerate(masks):
                sp.dma_start(MI[:, i], m[:, 0:GB, :]).then_inc(m_in.sem, 16)
            for l, (a, b) in enumerate(((w1_0, w2_0), (w1_1, w2_1))):
                for e in range((E0, E1)[l]):
                    sp.dma_start(W1[l][:, e], a[:, e]).then_inc(moe_w[l].sem, 16)
                    sp.dma_start(W2[l][:, e], b[:, e]).then_inc(moe_w[l].sem, 16)

            def turn(it, more):
                if more:
                    sp.wait_ge(x0.sem, x0.at(it, 1))
                    group_in(Xin[:], src_x, it + 1, x_in)
                    sp.wait_ge(pk.sem, pk.at(it, GB))
                    sp.wait_ge(pq.sem, pq.at(it, GB))
                    group_in(XFin[:], src_f, it + 1, xf_in)
                    sp.wait_ge(mz.sem, mz.at(it, 1))
                    for i, m in enumerate(masks):
                        sp.dma_start(MI[:, i], m[:, bass.ds((it + 1) * GB, GB), :])\
                            .then_inc(m_in.sem, 16)
                    sp.wait_ge(pk.sem, pk.at(it, STEPS))
                    group_in(CF[:], src_c, it + 1, c_in)
                sp.wait_ge(acc.sem, acc.at(it, E0 + E1))
                sp.dma_start(out[:, bass.ds(it * GB, GB), :], X[:]).then_inc(out_done.sem, 16)

            with sp.Fori(0, GROUPS - 1) as it:
                turn(it, True)
            turn(GROUPS - 1, False)
            sp.wait_ge(out_done.sem, out_done.at(GROUPS, 16))

        N_CONST = 11

        @block.tensor
        def _(pe):
            pe.wait_ge(w_in.sem, 16 * N_CONST)
            pe.wait_ge(c_zero.sem, 1)
            pe.wait_ge(kx_ones.sem, 16 * 4)
            pe.wait_ge(kb_ones.sem, 2)

            with pe.Fori(0, GROUPS) as it:
                def proj_kv(n):
                    l, a, b = stage(n)
                    if n == 0:
                        pe.wait_ge(xf_in.sem, xf_in.at(it, 16))
                    if n == GB:
                        pe.wait_ge(c_in.sem, c_in.at(it, 16))
                    if l == 1 and a == 0:
                        pe.wait_ge(xtc.sem, xtc.at(it, LSTEPS + b + 1))
                    if n >= 1:
                        pe.wait_ge(qs.sem, qs.at(it, q_done[n]))
                        pe.wait_ge(va.sem, va.at(it, n))
                        pe.wait_ge(k9.sem, k9.at(it, n))
                        if l == 1 and w_done[n]:
                            pe.wait_ge(cw.sem, cw.at(it, w_done[n]))
                    if n == LSTEPS:
                        pe.wait_ge(lg.sem, lg.at(it, 1))
                    w = (2 * l + a) * 4
                    for h in range(2):
                        pe.matmul(PK[:, h * S:(h + 1) * S], WA[:, w + 1, h * 64:h * 64 + 64],
                                  kv_input(n), start=True, stop=True)
                    pe.matmul(PV, kv_input(n), WA[:, w + 2, :], start=True, stop=True)\
                        .then_inc(pk.sem, 1)

                def proj_q(n):
                    l, a, b = stage(n)
                    pe.wait_ge(k9.sem, k9.at(it, kv_before_q[n]))
                    pe.wait_ge(va.sem, va.at(it, kv_before_q[n]))
                    if w_before_q[n]:
                        pe.wait_ge(cw.sem, cw.at(it, w_before_q[n]))
                    if n and q_prev[n]:
                        pe.wait_ge(qs.sem, qs.at(it, n))
                    if a == 1:
                        pe.wait_ge(xtc.sem, xtc.at(it, xt_no(n - GB) + 1))
                    w = (2 * l + a) * 4
                    for h in range(2):
                        mm = pe.matmul(PQ[:, h * S:(h + 1) * S], WA[:, w, h * 64:h * 64 + 64],
                                       q_input(n), start=True, stop=True)
                    mm.then_inc(pq.sem, 1)

                def scores1(n, g):
                    l, a, b = stage(n)
                    if g == 0:
                        pe.wait_ge(kb.sem, kb.at(it, n + 1))
                        pe.wait_ge(qs.sem, qs.at(it, n + 1))
                        if n == LSTEPS:
                            pe.wait_ge(ma.sem, ma.at(it, 1))
                            pe.wait_ge(ha.sem, ha.at(it, 2 * E0))
                            pe.wait_ge(hd.sem, hd.at(it, 2 * E0))
                    q = 4 * n + g
                    if q >= 2:
                        pe.wait_ge(mx.sem, mx.at(it, q - 1))
                    o = S1B[g % 2]
                    if l:
                        pe.matmul(o[:], IDB[:], MA[:, 2 * a, b:b + 1, :].broadcast_to((128, 4, S)),
                                  start=True, stop=False, skip_group_check=True)
                    pe.matmul(o[:], QS[n % 4][:, g // 2, :], KB[n % 2][:, 4 * g:4 * g + 4, :],
                              start=not l, stop=True, skip_group_check=True).then_inc(s1.sem, 1)

                def shift_rows(n):
                    pe.wait_ge(nm.sem, nm.at(it, n + 1))
                    bank7(pe)
                    for h in range(2):
                        mm = pe.transpose(MB[0:SR, h * S:(h + 1) * S], NM[:, n % 2, h, :], ID[:])
                    mm.then_inc(nmt.sem, 1)

                def scores2(n, g):
                    l, a, b = stage(n)
                    q = 4 * n + g
                    if g == 0:
                        pe.wait_ge(kx.sem, kx.at(it, n + 1))
                        pe.wait_ge(nmc.sem, nmc.at(it, n + 1))
                    if q >= 2:
                        pe.wait_ge(ex.sem, ex.at(it, q - 1))
                    o = S2B[g % 2]
                    if l:
                        pe.matmul(o[:], IDB[:], MA[:, 2 * a + 1, b:b + 1, :].broadcast_to((128, 4, S)),
                                  start=True, stop=False, skip_group_check=True)
                    for j in range(4):
                        mm = pe.matmul(o[:, j * S:(j + 1) * S], KX[n % 4][:, 4 * g + j, :],
                                       Q9[n % 4][:, g // 2, :], start=not l, stop=True,
                                       skip_group_check=True)
                    mm.then_inc(s2.sem, 1)

                def values(n, g):
                    pe.wait_ge(ex.sem, ex.at(it, 4 * n + g + 1))
                    if g == 0:
                        pe.wait_ge(va.sem, va.at(it, n + 1))
                        if n:
                            pe.wait_ge(otc.sem, otc.at(it, n))
                        if n == LSTEPS:
                            pe.wait_ge(acc.sem, acc.at(it, E0))
                    for j in range(4):
                        mm = pe.matmul(OB[32 * j:32 * j + HD + 1, g * S:(g + 1) * S],
                                       VA[n % 4][:, 4 * g + j, :], PT[:, g, j, :],
                                       start=True, stop=True, skip_group_check=True)
                    mm.then_inc(av.sem, 1)

                def masked_values(n):
                    l, a, b = stage(n)
                    if n == LSTEPS:
                        pe.wait_ge(mz.sem, mz.at(it, 1))
                    pe.wait_ge(qs.sem, qs.at(it, q_before_w[n]))
                    pe.wait_ge(k9.sem, k9.at(it, kv_before_w[n]))
                    pe.wait_ge(va.sem, va.at(it, kv_before_w[n]))
                    pe.matmul(PB[:, 0:H * (HD + 1)], MZ[:, a, b, :],
                              VA[n % 4][:].rearrange("p h d -> p (h d)"), start=True, stop=True)\
                        .then_inc(wz.sem, 1)

                def token_major(n):
                    pe.wait_ge(otc.sem, otc.at(it, n + 1))
                    if n:
                        pe.wait_ge(an.sem, an.at(it, n))
                    if n == LSTEPS:
                        pe.wait_ge(acc.sem, acc.at(it, E0))
                    for g in range(4):
                        mm = pe.transpose(TB[:, g * 128:(g + 1) * 128], OT[:, n % 2, g, :], ID[:])
                    mm.then_inc(ott.sem, 1)

                last7 = []

                def bank7(e):
                    if last7:
                        s, k = last7[-1]
                        e.wait_ge(s.sem, s.at(it, k))

                def heads_back(n):
                    pe.wait_ge(an.sem, an.at(it, n + 1))
                    bank7(pe)
                    pe.transpose(MB[:, 0:128], AN[:, n % 2, :], ID[:]).then_inc(ant.sem, 1)
                    last7.append((atc, n + 1))

                def out_proj(n):
                    l, a, b = stage(n)
                    pe.wait_ge(atc.sem, atc.at(it, n + 1))
                    pe.matmul(MB[:, 0:128], AT[:, n % 2, :], WA[:, (2 * l + a) * 4 + 3, :],
                              start=True, stop=True).then_inc(zo.sem, 1)
                    last7.append((rr, n + 1))

                def feature_major(no_yn, slot, no_xt):
                    pe.wait_ge(yn.sem, yn.at(it, no_yn + 1))
                    bank7(pe)
                    pe.transpose(MB[:, 0:128], YN[:, slot, :], ID[:]).then_inc(xtt.sem, 1)
                    last7.append((xtc, no_xt + 1))

                q_done, w_done, kv_before_q, w_before_q, q_prev = {}, {}, {}, {}, {}
                q_before_w, kv_before_w = {}, {}
                nk = nq = nw = 0
                for l in range(2):
                    for kind, n in pb_order(l):
                        if kind == "kv":
                            q_done[n], w_done[n] = nq, nw
                            nk += 1
                        elif kind == "q":
                            kv_before_q[n], w_before_q[n], q_prev[n] = nk, nw, nq
                            nq += 1
                        else:
                            q_before_w[n], kv_before_w[n] = nq, nk
                            nw += 1

                for l in range(2):
                    n0 = l * LSTEPS
                    for kind, n in pb_prologue(l):
                        (proj_kv if kind == "kv" else proj_q)(n)
                    for g in range(4):
                        scores1(n0, g)
                    for s in range(LSTEPS + 2):
                        n = n0 + s
                        on = s < LSTEPS
                        if on:
                            shift_rows(n)
                            last7.append((nmc, n + 1))
                        if s < LSTEPS - 1:
                            scores1(n + 1, 0)
                            scores1(n + 1, 1)
                        if 1 <= s <= LSTEPS:
                            token_major(n - 1)
                        if on:
                            scores2(n, 0)
                        if 1 <= s <= LSTEPS:
                            heads_back(n - 1)
                        if s < LSTEPS - 1:
                            scores1(n + 1, 2)
                        if on:
                            scores2(n, 1)
                            values(n, 0)
                        if 1 <= s <= LSTEPS:
                            out_proj(n - 1)
                        if s < LSTEPS - 1:
                            scores1(n + 1, 3)
                        if on:
                            scores2(n, 2)
                            values(n, 1)
                        if 2 <= s:
                            feature_major(norm_no(n - 2), n % 2, xt_no(n - 2))
                        if s + 2 < LSTEPS:
                            proj_q(n + 2)
                        if on:
                            scores2(n, 3)
                            values(n, 2)
                        if s + 3 < LSTEPS:
                            proj_kv(n + 3)
                        if on:
                            values(n, 3)
                            if l:
                                masked_values(n)

                    if l == 0:
                        pe.wait_ge(moe_w[0].sem, 16 * 2 * E0)
                    else:
                        pe.wait_ge(moe_w[1].sem, 16 * 2 * E1)
                    pe.wait_ge(xtc.sem, xtc.at(it, xt_no(n0 + LSTEPS - 1) + 1))
                    pe.wait_ge(mx.sem, mx.at(it, 4 * (n0 + LSTEPS)))
                    pe.wait_ge(ex.sem, ex.at(it, 4 * (n0 + LSTEPS)))
                    n_exp = (E0, E1)[l]
                    if l:
                        pe.wait_ge(cw.sem, cw.at(it, 8))
                    pe.wait_ge(qs.sem, qs.at(it, n0 + LSTEPS))
                    pe.wait_ge(va.sem, va.at(it, n0 + LSTEPS))
                    for b in range(GB):
                        mm = pe.matmul(PB[:, b * NE:(b + 1) * NE], tok(XC, b), GW[:, l, :],
                                       start=True, stop=True)
                    mm.then_inc(lgt.sem, 1)

                    def hidden(e):
                        for c in range(HC):
                            x = l * E0 + e
                            if e:
                                if l == 0:
                                    r = ha if c % 2 == 0 else hd
                                    pe.wait_ge(r.sem, r.at(it, 2 * (e - 1) + c // 2 + 1))
                                else:
                                    pe.wait_ge(ha.sem, ha.at(it, 2 * E0 + 4 * (e - 1) + c + 1))
                            pe.matmul(HB[c][:], W1[l][:, e, c * 128:(c + 1) * 128], XC[:],
                                      start=True, stop=True).then_inc(ht.sem, 1)

                    def combine(e):
                        x = l * E0 + e
                        if e == 0:
                            pe.wait_ge(an.sem, an.at(it, n0 + LSTEPS))
                        if e >= 2:
                            pe.wait_ge(acc.sem, acc.at(it, x - 1))
                        for b in range(GB):
                            for c in range(HC):
                                if b == 0:
                                    if l == 0:
                                        r = ha if c % 2 == 0 else hd
                                        pe.wait_ge(r.sem, r.at(it, 2 * e + c // 2 + 1))
                                    else:
                                        pe.wait_ge(ha.sem, ha.at(it, 2 * E0 + 4 * e + c + 1))
                                mm = pe.matmul(YB[e % 2][:, b * 128:(b + 1) * 128],
                                               HT[:, e % 2, c, b * 128:(b + 1) * 128],
                                               W2[l][:, e, c, :], start=(c == 0), stop=(c == HC - 1),
                                               skip_group_check=True)
                        mm.then_inc(yt.sem, 1)

                    hidden(0)
                    if l == 0:
                        pe.wait_ge(gg.sem, gg.at(it, 1))
                        bank7(pe)
                        for b in range(GB):
                            mm = pe.transpose(MB[0:NE, b * 128:(b + 1) * 128], G[:, b, :], ID[:])
                        mm.then_inc(gtt.sem, 1)
                    for e in range(1, n_exp):
                        hidden(e)
                        if l == 0 and e == 1:
                            pe.wait_ge(gtc.sem, gtc.at(it, 1))
                            for b in range(GB):
                                mm = pe.matmul(MB[:, b * 128:(b + 1) * 128], GTT[:, b, :], B2[:],
                                               start=True, stop=True)
                            mm.then_inc(b2t.sem, 1)
                        combine(e - 1)
                    combine(n_exp - 1)
                    if l == 0:
                        last7.append((xb2, 1))
                        for b in range(GB):
                            feature_major(LSTEPS + 2 * b + 1, b % 2, LSTEPS + b)

        @block.scalar
        def _(act):
            act.wait_ge(w_in.sem, 16 * N_CONST)
            act.wait_ge(c_zero.sem, 1)
            for a in range(2):
                for h in range(2):
                    act.activation(QB[:, 2 * a + h:2 * a + h + 1], C64[:, 4 * a + h:4 * a + h + 1],
                                   ACT.Copy, scale=SCALE).then_inc(c_qb.sem, 1)
            act.wait_ge(c_qb.sem, 4)

            with act.Fori(0, GROUPS) as it:
                def queries(n):
                    l, a, b = stage(n)
                    act.wait_ge(pq.sem, pq.at(it, n + 1))
                    if l == 0:
                        for h in range(2):
                            i = act.activation(Q9[n % 4][0:64, h, :], PQ[:, h * S:(h + 1) * S],
                                               ACT.Identity, scale=SCALE,
                                               bias=QB[:, 2 * a + h:2 * a + h + 1])
                    else:
                        i = act.activation(Q9[n % 4][0:64, :, :].rearrange("p h t -> p (h t)"), PQ,
                                           ACT.Copy, scale=SCALE)
                    i.then_inc(q9.sem, 1)
                    act.wait_ge(q9.sem, q9.at(it, n + 1))
                    act.activation(QS[n % 4][0:64, :, :], Q9[n % 4][0:64, :, :], ACT.Copy)\
                        .then_inc(qs.sem, 1)

                def exps(n, g):
                    act.wait_ge(s2.sem, s2.at(it, 4 * n + g + 1))
                    if n:
                        act.wait_ge(av.sem, av.at(it, 4 * (n - 1) + g + 1))
                    act.activation(PT[:, g], S2B[g % 2][:], ACT.Exp).then_inc(ex.sem, 1)

                def norm_scale(no_xt, dst, scale, bias):
                    act.wait_ge(xtt.sem, xtt.at(it, no_xt + 1))
                    act.activation(dst, MB[:, 0:128], ACT.Identity, scale=scale, bias=bias)\
                        .then_inc(xtc.sem, 1)

                for l in range(2):
                    n0 = l * LSTEPS
                    if l:
                        for b in range(GB):
                            norm_scale(LSTEPS + b, tok(XA, b), col("norm1_w"), 0.0)
                    for kind, n in pb_prologue(l):
                        if kind == "q":
                            queries(n)
                    for s in range(LSTEPS + 2):
                        n = n0 + s
                        on = s < LSTEPS
                        if on:
                            act.wait_ge(nmt.sem, nmt.at(it, n + 1))
                            act.activation(Q9[n % 4][64:96, :, :],
                                           MB[0:SR, 0:2 * S].rearrange("p (h t) -> p h t", h=2),
                                           ACT.Copy).then_inc(nmc.sem, 1)
                        if 1 <= s <= LSTEPS:
                            act.wait_ge(av.sem, av.at(it, 4 * n))
                            if n >= 3:
                                act.wait_ge(ott.sem, ott.at(it, n - 2))
                            act.activation(OT[:, (n - 1) % 2].rearrange("p g t -> p (g t)"), OB[:],
                                           ACT.Copy).then_inc(otc.sem, 1)
                        if on:
                            exps(n, 0)
                            if l:
                                act.wait_ge(ca.sem, ca.at(it, n - n0 + 1))
                                act.activation(CE[:, n % 2], CA[:, n % 2], ACT.Exp)\
                                    .then_inc(ce.sem, 1)
                        if 1 <= s <= LSTEPS:
                            act.wait_ge(ant.sem, ant.at(it, n))
                            act.activation(AT[:, (n - 1) % 2, :], MB[:, 0:128], ACT.Copy)\
                                .then_inc(atc.sem, 1)
                        if on:
                            exps(n, 1)
                            exps(n, 2)
                        if s >= 2:
                            m = n - 2
                            _, a, b = stage(m)
                            names = [["n1", "n2"], ["norm2", "norm3"]][l][a]
                            norm_scale(xt_no(m), tok((XB, XC)[a], b),
                                       col(names + ("_w" if l else "_g")),
                                       0.0 if l else col(names + "_b"))
                        if s + 2 < LSTEPS:
                            queries(n + 2)
                        if on:
                            exps(n, 3)
                    act.wait_ge(lz.sem, lz.at(it, l + 1))
                    act.activation(LE[:], LZ[:], ACT.Exp).then_inc(le.sem, 1)
                    if l == 0:
                        for e in range(E0):
                            for c in (0, 2):
                                act.wait_ge(ht.sem, ht.at(it, 4 * e + c + 1))
                                if e >= 2:
                                    act.wait_ge(yt.sem, yt.at(it, e - 1))
                                act.activation(HT[:, e % 2, c, :], HB[c][:], ACT.Relu,
                                               bias=B1[:, e, c:c + 1]).then_inc(ha.sem, 1)
                            if e == 0:
                                act.wait_ge(gtt.sem, gtt.at(it, 1))
                                act.activation(GTT[:].rearrange("p b t -> p (b t)"), MB[0:NE, :],
                                               ACT.Copy).then_inc(gtc.sem, 1)
                    else:
                        for e in range(E1):
                            for c in range(HC):
                                act.wait_ge(ht.sem, ht.at(it, 4 * (E0 + e) + c + 1))
                                if e >= 2:
                                    act.wait_ge(yt.sem, yt.at(it, E0 + e - 1))
                                act.activation(HT[:, e % 2, c, :], HB[c][:], ACT.Silu)\
                                    .then_inc(ha.sem, 1)

        @block.vector
        def _(dve):
            dve.memset(NM[:], 0.0)
            dve.memset(OB[:], 0.0)
            for t in Q9:
                dve.memset(t[64:96], 0.0)
            for t in VA:
                dve.memset(t[:, :, HD:HD + 1], 1.0)
            for t in QS:
                i = dve.memset(t[64:96], 0.0)
            i.then_inc(c_zero.sem, 1)
            dve.wait_ge(kx_ones.sem, 16 * 4)
            for i in range(2):
                dve.tensor_copy(KB[i][64:96], KX[i][64:96]).then_inc(kb_ones.sem, 1)
            dve.wait_ge(w_in.sem, 16 * N_CONST)
            dve.tensor_tensor(BS[:, 0], row("n1_b"), row("ca_bo"), ALU.add).then_inc(c_bs.sem, 1)
            dve.tensor_copy(BS[:, 1], row("n2_b")).then_inc(c_bs.sem, 1)

            with dve.Fori(0, GROUPS) as it:
                def keys_values(n):
                    l, a, b = stage(n)
                    dve.wait_ge(pk.sem, pk.at(it, n + 1))
                    if n >= 2:
                        dve.wait_ge(kx.sem, kx.at(it, n - 1))
                    if l == 0:
                        for h in range(2):
                            i = dve.tensor_scalar(K9[:, n % 2, h, :], PK[:, h * S:(h + 1) * S],
                                                  C64[:, 4 * a + 2 + h:4 * a + 3 + h], None, ALU.add)
                    else:
                        i = dve.tensor_copy(K9[:, n % 2].rearrange("p h t -> p (h t)"), PK)
                    i.then_inc(k9.sem, 1)
                    v = PV.rearrange("p (h d) -> p h d", h=H)
                    if l == 0:
                        i = dve.tensor_tensor(VA[n % 4][:, :, 0:HD], v,
                                              row(("sa_bv", "ca_bv")[a]).rearrange(
                                                  "p (h d) -> p h d", h=H), ALU.add)
                    else:
                        i = dve.tensor_copy(VA[n % 4][:, :, 0:HD], v)
                    i.then_inc(va.sem, 1)

                def keys_bf16(n):
                    dve.wait_ge(kx.sem, kx.at(it, n + 1))
                    dve.tensor_copy(KB[n % 2][0:64], KX[n % 4][0:64]).then_inc(kb.sem, 1)

                def row_max(n, g):
                    dve.wait_ge(s1.sem, s1.at(it, 4 * n + g + 1))
                    dve.tensor_reduce(MX[:, n % 2, 4 * g:4 * g + 4],
                                      S1B[g % 2][:].rearrange("p (j k) -> p j k", j=4),
                                      AX.X, ALU.max).then_inc(mx.sem, 1)

                def shift(n):
                    l, a, b = stage(n)
                    dve.wait_ge(mx.sem, mx.at(it, 4 * n + 4))
                    src = MX[:, n % 2].rearrange("p (a h) -> p a h", a=2)
                    dst = NM[:, n % 2, :, 0:HALF]
                    if l == 0:
                        dve.tensor_scalar(dst, src, -1.0, None, ALU.mult).then_inc(nm.sem, 1)
                    else:
                        dve.tensor_scalar(dst, src, MF[:, a, b, 3:4], -1.0, ALU.max, ALU.mult)\
                            .then_inc(nm.sem, 1)
                        dve.wait_ge(nm.sem, nm.at(it, n + 1))
                        dve.tensor_scalar(CA[:, n % 2].rearrange("p (a h) -> p a h", a=2), dst,
                                          NEG, 0.0, ALU.add, ALU.min).then_inc(ca.sem, 1)

                def normalise(n):
                    l, a, b = stage(n)
                    dve.wait_ge(ott.sem, ott.at(it, n + 1))
                    o = TB[:].rearrange("p (h r) -> p h r", h=H)
                    if l:
                        m = n - LSTEPS
                        dve.wait_ge(wz.sem, wz.at(it, m + 1))
                        dve.wait_ge(ce.sem, ce.at(it, m + 1))
                        w = PB[:, 0:H * (HD + 1)].rearrange("p (h d) -> p h d", h=H)
                        c = CE[:, n % 2].rearrange("p (h o) -> p h o", o=1)\
                            .broadcast_to((128, H, HD + 1))
                        dve.tensor_tensor(CW[:], w, c, ALU.mult).then_inc(cw.sem, 1)
                        dve.wait_ge(cw.sem, cw.at(it, m + 1))
                        dve.tensor_tensor(OW[:], o[:, :, 0:HD + 1], CW[:], ALU.add)\
                            .then_inc(ow.sem, 1)
                        dve.wait_ge(ow.sem, ow.at(it, m + 1))
                        o = OW[:]
                    dve.reciprocal(RS[:, n % 2].rearrange("p (h o) -> p h o", o=1), o[:, :, HD:HD + 1])\
                        .then_inc(rs.sem, 1)
                    dve.wait_ge(rs.sem, rs.at(it, n + 1))
                    r = RS[:, n % 2].rearrange("p (h o) -> p h o", o=1).broadcast_to((128, H, HD))
                    dve.tensor_tensor(AN[:, n % 2].rearrange("p (h d) -> p h d", h=H),
                                      o[:, :, 0:HD], r, ALU.mult).then_inc(an.sem, 1)

                def layer_norm_stats(src, slot, k):
                    dve.bn_stats(BN[:, slot], src).then_inc(bns.sem, 1)
                    dve.wait_ge(bns.sem, bns.at(it, k + 1))
                    dve.tensor_copy(TICK[:, 1:2], BN[:, slot, 0:1])
                    dve.bn_aggr(MV[:, slot], BN[:, slot]).then_inc(mv.sem, 1)

                def rms_stats(src, slot, k):
                    dve.scalar_tensor_tensor(SQ[:], src, 1.0, src, ALU.mult, ALU.mult,
                                             accum_out=SS[:, slot:slot + 1]).then_inc(ss.sem, 1)

                def residual(n):
                    l, a, b = stage(n)
                    dve.wait_ge(zo.sem, zo.at(it, n + 1))
                    if l == 0:
                        if a == 0 and b == 0:
                            dve.wait_ge(x0.sem, x0.at(it, 1))
                        if a == 1:
                            dve.wait_ge(xg.sem, xg.at(it, n - GB + 1))
                        dve.tensor_tensor(RR[:, n % 2], MB[:, 0:128], X[:, b], ALU.add)\
                            .then_inc(rr.sem, 1)
                        dve.wait_ge(rr.sem, rr.at(it, n + 1))
                        layer_norm_stats(RR[:, n % 2], n % 2, n)
                    else:
                        dve.tensor_tensor(X[:, b], MB[:, 0:128], X[:, b], ALU.add)\
                            .then_inc(rr.sem, 1)
                        dve.wait_ge(rr.sem, rr.at(it, n + 1))
                        rms_stats(X[:, b], n % 2, n - LSTEPS + GB)

                def norm_out(n):
                    l, a, b = stage(n)
                    k = norm_no(n)
                    dve.wait_ge(rd.sem, rd.at(it, k + 1))
                    if n % LSTEPS >= 2:
                        dve.wait_ge(xtt.sem, xtt.at(it, xt_no(n - 2) + 1))
                    if l == 0:
                        dve.tensor_scalar(YN[:, n % 2], RR[:, n % 2], MV[:, n % 2, 0:1],
                                          RD[:, n % 2:n % 2 + 1], ALU.subtract, ALU.mult)\
                            .then_inc(yn.sem, 1)
                    else:
                        dve.tensor_scalar(YN[:, n % 2], X[:, b], RD[:, n % 2:n % 2 + 1],
                                          float(D) ** 0.5, ALU.mult, ALU.mult).then_inc(yn.sem, 1)

                for l in range(2):
                    n0 = l * LSTEPS
                    if l:
                        dve.wait_ge(ma.sem, ma.at(it, 1))
                        for a in range(2):
                            i = dve.tensor_reduce(MF[:, a, :, 0:1].rearrange("p b o -> p (b o)"),
                                                  MA[:, 2 * a], AX.X, ALU.min)
                        i.then_inc(mf.sem, 1)
                        dve.wait_ge(mf.sem, mf.at(it, 1))
                        dve.tensor_scalar(MF[:, :, :, 1], MF[:, :, :, 0], 0.0, -BIG,
                                          ALU.is_ge, ALU.mult)
                        dve.tensor_scalar(MF[:, :, :, 2], MF[:, :, :, 0], 0.0, NEG,
                                          ALU.is_lt, ALU.mult).then_inc(mf.sem, 1)
                        dve.wait_ge(mf.sem, mf.at(it, 2))
                        dve.tensor_tensor(MF[:, :, :, 3], MF[:, :, :, 1], MF[:, :, :, 2], ALU.add)\
                            .then_inc(mf.sem, 1)
                        dve.wait_ge(mf.sem, mf.at(it, 3))
                    for kind, n in pb_prologue(l):
                        if kind == "kv":
                            keys_values(n)
                    keys_bf16(n0)
                    keys_bf16(n0 + 1)
                    for g in range(4):
                        row_max(n0, g)
                    shift(n0)
                    for s in range(LSTEPS + 2):
                        n = n0 + s
                        if s < LSTEPS - 1:
                            row_max(n + 1, 0)
                            row_max(n + 1, 1)
                        if 1 <= s <= LSTEPS:
                            normalise(n - 1)
                        if s >= 2:
                            norm_out(n - 2)
                        if s < LSTEPS - 1:
                            row_max(n + 1, 2)
                            row_max(n + 1, 3)
                            shift(n + 1)
                        if s + 2 < LSTEPS:
                            keys_bf16(n + 2)
                        if 1 <= s <= LSTEPS:
                            residual(n - 1)
                        if s + 3 < LSTEPS:
                            keys_values(n + 3)

                    dve.wait_ge(lgt.sem, lgt.at(it, l + 1))
                    lgp = PB[:, 0:GB * NE].rearrange("p (b e) -> p b e", b=GB)
                    if l == 0:
                        rb = RV[:, len(ROWS) * D:].rearrange("p (o e) -> p o e", o=1)
                        i = dve.tensor_tensor(LG[:], lgp, rb.broadcast_to((128, GB, NE)), ALU.add)
                    else:
                        i = dve.tensor_copy(LG[:], lgp)
                    i.then_inc(lg.sem, 1)
                    dve.wait_ge(lg.sem, lg.at(it, l + 1))
                    dve.tensor_reduce(LM[:], LG[:], AX.X, ALU.max).then_inc(lm.sem, 1)
                    dve.wait_ge(lm.sem, lm.at(it, l + 1))
                    lmb = LM[:].rearrange("p (b o) -> p b o", o=1).broadcast_to((128, GB, NE))
                    dve.tensor_tensor(LZ[:], LG[:], lmb, ALU.subtract).then_inc(lz.sem, 1)
                    for b in range(GB):
                        other = LG[:, b:b + 1, :].broadcast_to((128, NE, NE))
                        own = LG[:, b, :].rearrange("p (i o) -> p i o", o=1)\
                            .broadcast_to((128, NE, NE))
                        dve.tensor_tensor(GT[:, b], other, own, ALU.is_gt)
                        i = dve.tensor_tensor(EQ[:, b], other, own, ALU.is_equal)
                    i.then_inc(lgr.sem, 1)
                    dve.wait_ge(lgr.sem, lgr.at(it, 4 * l + 1))
                    for b in range(GB):
                        i = dve.tensor_tensor(EQ[:, b], EQ[:, b], BEF[:], ALU.mult)
                    i.then_inc(lgr.sem, 1)
                    dve.wait_ge(lgr.sem, lgr.at(it, 4 * l + 2))
                    dve.tensor_tensor(GT[:], GT[:], EQ[:], ALU.add).then_inc(lgr.sem, 1)
                    dve.wait_ge(lgr.sem, lgr.at(it, 4 * l + 3))
                    dve.tensor_reduce(RK[:], GT[:], AX.X, ALU.add).then_inc(lgr.sem, 1)
                    dve.wait_ge(lgr.sem, lgr.at(it, 4 * l + 4))
                    dve.wait_ge(le.sem, le.at(it, l + 1))
                    dve.scalar_tensor_tensor(GE[:], RK[:], 1.5, LE[:], ALU.is_lt, ALU.mult)\
                        .then_inc(ge.sem, 1)
                    dve.wait_ge(ge.sem, ge.at(it, l + 1))
                    dve.tensor_reduce(GS[:], GE[:], AX.X, ALU.add).then_inc(gs.sem, 1)
                    dve.wait_ge(gs.sem, gs.at(it, l + 1))
                    dve.reciprocal(GR[:], GS[:]).then_inc(gr.sem, 1)
                    dve.wait_ge(gr.sem, gr.at(it, l + 1))
                    grb = GR[:].rearrange("p (b o) -> p b o", o=1).broadcast_to((128, GB, NE))
                    dve.tensor_tensor(G[:], GE[:], grb, ALU.mult).then_inc(gg.sem, 1)
                    dve.wait_ge(gg.sem, gg.at(it, l + 1))

                    def relu(e):
                        for c in (1, 3):
                            dve.wait_ge(ht.sem, ht.at(it, 4 * e + c + 1))
                            if e >= 2:
                                dve.wait_ge(yt.sem, yt.at(it, e - 1))
                            dve.tensor_scalar(HT[:, e % 2, c, :], HB[c][:], B1[:, e, c:c + 1], 0.0,
                                              ALU.add, ALU.max).then_inc(hd.sem, 1)

                    def add_expert(e):
                        x = l * E0 + e
                        dve.wait_ge(yt.sem, yt.at(it, x + 1))
                        if l == 0 and e == 0:
                            dve.wait_ge(xb2.sem, xb2.at(it, 1))
                        if e:
                            dve.wait_ge(acc.sem, acc.at(it, x))
                        if l and e == NE:
                            dve.tensor_tensor(X[:].rearrange("p b d -> p (b d)"), YB[e % 2][:],
                                              X[:].rearrange("p b d -> p (b d)"), ALU.add)\
                                .then_inc(acc.sem, 1)
                            return
                        for b in range(GB):
                            i = dve.scalar_tensor_tensor(
                                X[:, b], YB[e % 2][:, b * 128:(b + 1) * 128], G[:, b, e:e + 1],
                                X[:, b], ALU.mult, ALU.add)
                        i.then_inc(acc.sem, 1)

                    if l == 0:
                        relu(0)
                        relu(1)
                        dve.wait_ge(b2t.sem, b2t.at(it, 1))
                        dve.wait_ge(xg.sem, xg.at(it, LSTEPS))
                        dve.tensor_tensor(X[:].rearrange("p b d -> p (b d)"), MB[:],
                                          X[:].rearrange("p b d -> p (b d)"), ALU.add)\
                            .then_inc(xb2.sem, 1)
                        add_expert(0)
                        for e in range(2, E0):
                            relu(e)
                            add_expert(e - 1)
                        add_expert(E0 - 1)
                        dve.wait_ge(acc.sem, acc.at(it, E0))
                        for b in range(GB):
                            layer_norm_stats(X[:, b], b % 2, LSTEPS + b)
                            dve.wait_ge(rd.sem, rd.at(it, LSTEPS + 2 * b + 1))
                            dve.tensor_scalar(YN[:, b % 2], X[:, b], MV[:, b % 2, 0:1],
                                              RD[:, 0:1], ALU.subtract, ALU.mult)\
                                .then_inc(yn.sem, 1)
                            dve.wait_ge(xg.sem, xg.at(it, LSTEPS + b + 1))
                            rms_stats(X[:, b], 1, b)
                            dve.wait_ge(rd.sem, rd.at(it, LSTEPS + 2 * b + 2))
                            dve.tensor_scalar(YN[:, b % 2], X[:, b], RD[:, 1:2],
                                              float(D) ** 0.5, ALU.mult, ALU.mult)\
                                .then_inc(yn.sem, 1)
                            dve.wait_ge(xtt.sem, xtt.at(it, LSTEPS + b + 1))
                    else:
                        for e in range(E1):
                            add_expert(e)

        @block.gpsimd
        def _(pool):
            pool.memset(EXPN[:, 0:1], -0.5)
            pool.memset(EXPN[:, 1:2], EPS)
            pool.memset(EXPN[:, 2:3], D * EPS).then_inc(c_bs.sem, 1)
            pool.wait_ge(w_in.sem, 16 * N_CONST)
            pool.wait_ge(c_bs.sem, 3)

            with pool.Fori(0, GROUPS) as it:
                def spread(n):
                    pool.wait_ge(k9.sem, k9.at(it, n + 1))
                    if n >= 4:
                        pool.wait_ge(s2.sem, s2.at(it, 4 * (n - 3)))
                        pool.wait_ge(kb.sem, kb.at(it, n - 3))
                    dst = KX[n % 4][0:64].rearrange("p (a h) t -> p a h t", a=2)
                    pool.tensor_tensor(dst[:, :, 0, :], K9[:, n % 2],
                                       HM[:, 0:1].rearrange("p (a o) -> p a o", a=1)
                                       .broadcast_to((64, 2, S)), ALU.mult)
                    for h in range(1, HALF):
                        i = pool.tensor_scalar(dst[:, :, h, :], K9[:, n % 2], HM[:, h:h + 1], 1.0,
                                               ALU.mult, ALU.mult)
                    i.then_inc(kx.sem, 1)

                def inverse_root(src, eps, slot, k):
                    pool.tensor_tensor(RE[:, slot:slot + 1], src, EXPN[:, eps:eps + 1], ALU.add)\
                        .then_inc(re.sem, 1)
                    pool.wait_ge(re.sem, re.at(it, k + 1))
                    pool.tensor_tensor(RD[:, slot:slot + 1], RE[:, slot:slot + 1], EXPN[:, 0:1],
                                       ALU.pow).then_inc(rd.sem, 1)

                def affine(src, b, k, g, bias):
                    pool.tensor_tensor(YG[:], src, g, ALU.mult).then_inc(yg.sem, 1)
                    pool.wait_ge(yg.sem, yg.at(it, k + 1))
                    pool.tensor_tensor(X[:, b], YG[:], bias, ALU.add).then_inc(xg.sem, 1)

                pool.wait_ge(x_in.sem, x_in.at(it, 16))
                pool.wait_ge(out_done.sem, out_done.at(it, 16))
                bo = row("sa_bo").rearrange("p (o d) -> p o d", o=1).broadcast_to((128, GB, D))
                pool.tensor_tensor(X[:], Xin[:], bo, ALU.add).then_inc(x0.sem, 1)
                for l in range(2):
                    n0 = l * LSTEPS
                    for kind, n in pb_prologue(l):
                        if kind == "kv":
                            spread(n)
                    if l == 0:
                        pool.wait_ge(m_in.sem, m_in.at(it, 64))
                        pool.tensor_tensor(TICK[:, 0:1], EXPN[:, 0:1], EXPN[:, 0:1], ALU.mult)
                        pool.tensor_scalar(MA[:].rearrange("p m b t -> p (m b t)"),
                                           MI[:].rearrange("p m b t -> p (m b t)"), 0.0, -BIG,
                                           ALU.is_equal, ALU.mult).then_inc(ma.sem, 1)
                        pool.tensor_scalar(MZ[:], MI[:, 1::2], 0.0, 1.0,
                                           ALU.is_equal, ALU.mult).then_inc(mz.sem, 1)
                    for s in range(LSTEPS + 2):
                        n = n0 + s
                        if l == 0 and s >= 2:
                            m = n - 2
                            _, a, b = stage(m)
                            pool.wait_ge(yn.sem, yn.at(it, m + 1))
                            affine(YN[:, m % 2], b, m, row(("n1_g", "n2_g")[a]), BS[:, a])
                        if 1 <= s <= LSTEPS:
                            m = n - 1
                            k = norm_no(m)
                            if l == 0:
                                pool.wait_ge(mv.sem, mv.at(it, m + 1))
                                inverse_root(MV[:, m % 2, 1:2], 1, m % 2, k)
                            else:
                                pool.wait_ge(ss.sem, ss.at(it, m - LSTEPS + GB + 1))
                                inverse_root(SS[:, m % 2:m % 2 + 1], 2, m % 2, k)
                        if s + 3 < LSTEPS:
                            spread(n + 3)
                    if l == 0:
                        for b in range(GB):
                            k = LSTEPS + 2 * b
                            pool.wait_ge(mv.sem, mv.at(it, LSTEPS + b + 1))
                            inverse_root(MV[:, b % 2, 1:2], 1, 0, k)
                            pool.wait_ge(yn.sem, yn.at(it, k + 1))
                            affine(YN[:, b % 2], b, LSTEPS + b, row("n3_g"), row("n3_b"))
                            pool.wait_ge(ss.sem, ss.at(it, b + 1))
                            inverse_root(SS[:, 1:2], 2, 1, k + 1)


def pb_prologue(l):
    n0 = l * LSTEPS
    return [("kv", n0), ("q", n0), ("kv", n0 + 1), ("q", n0 + 1), ("kv", n0 + 2)]


def pb_order(l):
    n0 = l * LSTEPS
    order = list(pb_prologue(l))
    for s in range(LSTEPS):
        if s + 2 < LSTEPS:
            order.append(("q", n0 + s + 2))
        if s + 3 < LSTEPS:
            order.append(("kv", n0 + s + 3))
        if l:
            order.append(("w", n0 + s))
    return order


def kernel(**inputs):
    import ml_dtypes
    import numpy as np
    import concourse.bacc as bacc
    from concourse.bass_utils import run_bass_kernel_spmd as run

    a = {k: np.asarray(v) for k, v in inputs.items()}
    p0 = lambda k: a["L0_xattn_" + k]
    p1 = lambda k: a["L1_xattn_" + k]
    c = np.ascontiguousarray
    x, ctx = a["x"], a["ctx_1024"]
    ms, mc = a["mask_BxSxS_ik0"], a["mask_BxSxS2_if1"]
    att = [p0(f"{s}_w{m}") for s in ("sa", "ca") for m in "qkvo"]
    att += [p1(f"{s}_w{m}").T for s in ("sa", "ca") for m in "qkvo"]
    w1_1 = np.concatenate([p1("exp_w1"), p1("sh_w1")[None]])
    w2_1 = np.concatenate([p1("exp_w2"), p1("sh_w2")[None]])
    half = lambda v: v.reshape(2, 64).T
    eye = np.eye(128, dtype=np.float32)
    ones = np.zeros((SR, H, S), np.float32)
    for h in range(H):
        ones[h % HALF, h] = 1.0
    head = np.zeros((64, HALF), np.float32)
    for h in range(HALF):
        head[h * HD:(h + 1) * HD, h] = 1.0
    arrays = {
        "x_tok": x.transpose(1, 0, 2),
        "x_feat": x.transpose(2, 0, 1).reshape(D, B * S),
        "ctx_feat": ctx.transpose(2, 0, 1).reshape(D, B * S),
        "m_self": ms.transpose(1, 0, 2), "m_selfT": ms.transpose(2, 0, 1),
        "m_cross": mc.transpose(1, 0, 2), "m_crossT": mc.transpose(2, 0, 1),
        "att_w": np.stack(att, 1),
        "w1_0": p0("e_w1").transpose(1, 0, 2),
        "w2_0": p0("e_w2").reshape(E0, HC, 128, D).transpose(2, 0, 1, 3),
        "w1_1": w1_1.transpose(2, 0, 1),
        "w2_1": w2_1.reshape(E1, D, HC, 128).transpose(3, 0, 2, 1),
        "gate_w": np.stack([p0("r_w"), p1("gate_w").T], 1),
        "rows": np.concatenate([p0(r) for r in ROWS] + [p0("r_b")])[None],
        "cols": np.stack([p0(v) for v in COLS[:4]] + [p1(v) for v in COLS[4:]], 1),
        "cols64": np.concatenate([half(p0(f"{s}_b{m}")) for s in ("sa", "ca") for m in "qk"], 1),
        "b1c": p0("e_b1").reshape(E0, HC, 128).transpose(2, 0, 1),
        "b2": p0("e_b2"),
        "ident": eye, "identb": eye.astype(ml_dtypes.bfloat16),
        "hmask": head, "shift_ones": ones,
        "before": np.tril(np.ones((NE, NE), np.float32), -1).reshape(1, NE * NE),
    }
    nc = bacc.Bacc("TRN2", target_bir_lowering=False, num_devices=1)
    feed, args = {}, []
    for name, v in arrays.items():
        v = c(v)
        feed[name] = v
        args.append(nc.dram_tensor(name, v.shape, mybir.dt.from_np(v.dtype),
                                   kind="ExternalInput").ap())
    out = nc.dram_tensor("out", (S, B, D), F32, kind="ExternalOutput").ap()
    two_layers(nc, *args, out)
    r = run(nc, [feed], core_ids=[0])
    return r.results[0]["out"].transpose(1, 0, 2)
```

```python
from contextlib import ExitStack

import concourse.bass as bass
from concourse import mybir

F32 = mybir.dt.float32
BF16 = mybir.dt.bfloat16
I32 = mybir.dt.int32
ALU = mybir.AluOpType
ACT = mybir.ActivationFunctionType
AX = mybir.AxisListType

B, S, D = 16, 128, 128
H, HD = 16, 8
E0, E1, HID = 8, 9, 512
NE = 8
GB = 4
GROUPS = B // GB
T = GB * S
HC = HID // 128
HALF = H // 2
SR = 32
KR = HALF * HD + SR
LSTEPS = 2 * GB
PHASES = 4
STEPS = PHASES * LSTEPS
TURNS = GROUPS // 2
SCALE = float(HD) ** -0.5
EPS = 1e-5
NEG = -65504.0
BIG = 1e30

ROWS = ["sa_bv", "ca_bv", "sa_bo", "ca_bo", "n1_g", "n1_b", "n2_g", "n2_b", "n3_g", "n3_b"]
COLS = ["n1_g", "n1_b", "n2_g", "n2_b", "norm1_w", "norm2_w", "norm3_w"]


class Signal:

    def __init__(self, sem, per):
        self.sem, self.per = sem, per

    def at(self, turn, k):
        return turn * self.per + k


def moe_first(m):
    return sum((E0, E1)[j // 2] for j in range(m))


def moe_pieces(l):
    n = (E0, E1)[l]
    out = [("h", 0, c) for c in range(HC)]
    for e in range(1, n):
        h, y = [("h", e, c) for c in range(HC)], [("y", e - 1, b) for b in range(GB)]
        if l == 0 and e == 2:
            out += [h[0], ("gt",), h[1], ("b2",), h[2], y[0], h[3], *y[1:]]
        else:
            out += [p for pair in zip(h, y) for p in pair]
    return out + [("y", n - 1, b) for b in range(GB)]


FILL = (2, 2, 2, 2, 2, 1, 1, 1, 1)
SPREAD = 27


def moe_plan(l):
    pieces, plan = moe_pieces(l), {}
    at = 0
    for i, k in enumerate(FILL):
        plan["fill", i] = pieces[at:at + k]
        at += k
    plan["fill", 0] = [("lg",)] + plan["fill", 0]
    plan["fill", 3] = plan["fill", 3] + [("le",)]
    rest = pieces[at:]
    for i in range(SPREAD):
        lo, hi = (len(rest) * j // SPREAD for j in (i, i + 1))
        plan[i // 4, i % 4] = rest[lo:hi]
    return plan


def two_layers(nc, x_tok, x_feat, ctx_feat, m_self, m_selfT, m_cross, m_crossT, att_w, w1_0, w2_0,
               w1_1, w2_1, gate_w, rows, cols, cols64, b1c, b2, ident, identb, hmask, shift_ones,
               before, out):
    ctx = ExitStack()
    with ctx:
        def sb(name, shape, dt=F32):
            return ctx.enter_context(nc.sbuf_tensor(name, shape, dt))

        def sig(name, per):
            return Signal(ctx.enter_context(nc.semaphore(name)), per)

        WA = sb("WA", [128, 16, 128])
        W1 = [sb("W1a", [128, E0, HID]), sb("W1b", [128, E1, HID])]
        W2 = [sb("W2a", [128, E0, HC, D]), sb("W2b", [128, E1, HC, D])]
        GW = sb("GW", [128, 2, NE])
        RV = sb("RV", [128, len(ROWS) * D + NE])
        CV = sb("CV", [128, len(COLS)])
        CR = sb("CR", [128, 1])
        C64 = sb("C64", [64, 8])
        QB = sb("QB", [64, 4])
        B1 = sb("B1", [128, E0, HC])
        B2 = sb("B2", [NE, D])
        ID = sb("ID", [128, 128])
        IDB = sb("IDB", [128, 128], BF16)
        HM = sb("HM", [64, HALF])
        BEF = sb("BEF", [128, NE, NE])
        BS = sb("BS", [128, 2, D])
        EXPN = sb("EXPN", [128, 3])
        TICK = sb("TICK", [128, 3])
        Xin = sb("Xin", [128, GB, D])
        XFin = sb("XFin", [128, T])
        CF = [sb(f"CF{i}", [128, T]) for i in range(2)]
        X = [sb(f"X{i}", [128, GB, D]) for i in range(2)]
        XA = sb("XA", [128, T])
        XB = sb("XB", [128, T])
        XC = [sb(f"XC{i}", [128, T]) for i in range(2)]
        MI = sb("MI", [128, 2, GB, S], I32)
        MA = [sb(f"MA{i}", [128, 4, GB, S], BF16) for i in range(2)]
        MZ = [sb(f"MZ{i}", [128, 2, GB, S]) for i in range(2)]
        MF = sb("MF", [128, 2, GB, 4])
        K9 = sb("K9", [64, 2, 2, S])
        KX = [sb(f"KX{i}", [KR, H, S]) for i in range(3)]
        KB = [sb(f"KB{i}", [KR, H, S], BF16) for i in range(2)]
        Q9 = [sb(f"Q9{i}", [KR, 2, S]) for i in range(4)]
        QS = [sb(f"QS{i}", [KR, 2, S], BF16) for i in range(4)]
        VA = [sb(f"VA{i}", [128, H, HD + 1]) for i in range(4)]
        MX = sb("MX", [128, 2, H])
        NM = sb("NM", [128, 2, 2, SR])
        PT = sb("PT", [128, 4, 4, S])
        CA = sb("CA", [128, 2, H])
        CE = sb("CE", [128, 2, H])
        OT = sb("OT", [128, 2, 4, S])
        CW = sb("CW", [128, 2, H, HD + 1])
        OW = sb("OW", [128, H, HD + 1])
        RS = sb("RS", [128, 2, H])
        AN = sb("AN", [128, 2, D])
        AT = sb("AT", [128, 2, S])
        RR = sb("RR", [128, 2, D])
        BN = sb("BN", [128, 2, 6])
        MV = sb("MV", [128, 2, 2])
        SQ = sb("SQ", [128, D])
        SS = sb("SS", [128, 2])
        RE = sb("RE", [128, 2])
        RD = sb("RD", [128, 2])
        YN = sb("YN", [128, 2, D])
        YG = sb("YG", [128, D])
        JB = sb("JB", [128, GB, 6])
        JM = sb("JM", [128, GB, 2])
        JS = sb("JS", [128, GB])
        JE = sb("JE", [128, GB])
        JD = sb("JD", [128, 2, GB])
        JT = sb("JT", [128, GB, D])
        HT = sb("HT", [128, 2, HC, T])
        LG = sb("LG", [128, GB, NE])
        LM = sb("LM", [128, GB])
        LZ = sb("LZ", [128, GB, NE])
        LE = sb("LE", [128, GB, NE])
        GT = sb("GT", [128, GB, NE, NE])
        EQ = sb("EQ", [128, GB, NE, NE])
        RK = sb("RK", [128, GB, NE])
        GE = sb("GE", [128, GB, NE])
        GS = sb("GS", [128, GB])
        GR = sb("GR", [128, GB])
        G = sb("G", [128, GB, NE])
        GTT = JT[0:NE]

        bank = [ctx.enter_context(nc.psum_tensor(f"bank{i}", [128, 512], F32)) for i in range(8)]
        OB, TB, MB, PB = bank[2:6]
        PK, PV, PQ = PB[0:64, 0:256], PB[:, 256:384], PB[0:64, 0:256]

        def s1_bank(n, g):
            return bank[0] if n >= LSTEPS else bank[(0, 7)[g % 2]]

        def s2_bank(n, g):
            return bank[1] if n >= LSTEPS else bank[(1, 6)[g % 2]]

        def h_bank(m, c):
            return bank[(6, 0, 1, 2)[c]] if m == 3 else bank[6]

        def y_bank(m, e):
            return bank[(7, 3)[e % 2]] if m == 3 else bank[7]

        w_in = sig("w_in", 0)
        moe_w = [sig("moe_w0", 0), sig("moe_w1", 0)]
        x_in = sig("x_in", 32)
        xf_in = sig("xf_in", 32)
        c_in = [sig("c_in0", 16), sig("c_in1", 16)]
        m_in = sig("m_in", 128)
        out_done = [sig("out_done0", 16), sig("out_done1", 16)]
        c_zero = sig("c_zero", 0)
        c_qb = sig("c_qb", 0)
        c_bs = sig("c_bs", 0)
        kx_ones = sig("kx_ones", 0)
        kb_ones = sig("kb_ones", 0)
        N, N0 = STEPS, STEPS // 2
        EX = moe_first(4)
        pk = sig("pk", N)
        pq = sig("pq", N)
        s1 = sig("s1", 4 * N)
        nmt = sig("nmt", N)
        s2 = sig("s2", 4 * N)
        av = sig("av", 4 * N)
        wz = sig("wz", N0)
        ott = sig("ott", N)
        ant = sig("ant", N)
        zo = sig("zo", N)
        xtt = sig("xtt", N)
        lgt = sig("lgt", 4)
        gtt = sig("gtt", 2)
        b2t = sig("b2t", 2)
        ht = sig("ht", HC * EX)
        yt = sig("yt", EX)
        jxt = sig("jxt", 2)
        k9 = sig("k9", N)
        va = sig("va", N)
        kb = sig("kb", N)
        mx = sig("mx", 4 * N)
        nm = sig("nm", N)
        ca = sig("ca", N0)
        cw = sig("cw", N0)
        ow = sig("ow", N0)
        rs = sig("rs", N)
        an = sig("an", N)
        rr = sig("rr", N)
        bns = sig("bns", N0)
        mv = sig("mv", N0)
        ss = sig("ss", N0)
        yn = sig("yn", N)
        lg = sig("lg", 4)
        lm = sig("lm", 4)
        lz = sig("lz", 4)
        lgr = sig("lgr", 16)
        ge = sig("ge", 4)
        gs = sig("gs", 4)
        gr = sig("gr", 4)
        gg = sig("gg", 4)
        xb2 = sig("xb2", 2)
        hs = sig("hs", HC * 2 * E1)
        acc = sig("acc", EX)
        mf = sig("mf", 6)
        jb = sig("jb", 2)
        jm = sig("jm", 2)
        jt = sig("jt", 8)
        js = sig("js", 2)
        jy = sig("jy", 2)
        q9 = sig("q9", N)
        qs = sig("qs", N)
        nmc = sig("nmc", N)
        ce = sig("ce", N0)
        ex = sig("ex", 4 * N)
        otc = sig("otc", N)
        atc = sig("atc", N)
        xtc = sig("xtc", N)
        le = sig("le", 4)
        gtc = sig("gtc", 2)
        hr = sig("hr", HC * 2 * E0)
        th = sig("th", HC * 2 * E1)
        jxc = sig("jxc", 2)
        x0 = sig("x0", 2)
        ma = sig("ma", 4)
        mz = sig("mz", 4)
        kx = sig("kx", N)
        re = sig("re", N)
        rd = sig("rd", N)
        yg = sig("yg", N0)
        xg = sig("xg", N0)
        je = sig("je", 4)
        jd = sig("jd", 4)

        def row(name):
            i = ROWS.index(name)
            return RV[:, i * D:(i + 1) * D]

        def col(name):
            i = COLS.index(name)
            return CV[:, i:i + 1]

        def stage(n):
            ph, s = divmod(n, LSTEPS)
            return ph // 2, ph % 2, s // GB, s % GB

        def tok(t, b):
            return t[:, b * S:(b + 1) * S]

        def q_input(n):
            l, g, a, b = stage(n)
            return tok([[XFin, XB], [XA, XB]][l][a], b)

        def kv_input(n):
            l, g, a, b = stage(n)
            return tok(CF[g] if a else [XFin, XA][l], b)

        def hidden_done(m, k):
            return (hr, HC * E0 * (m % 2) + k) if m < 2 else (hs, HC * E1 * (m % 2) + k)

        plans = [moe_plan(l) for l in range(2)]

        def pieces(ph, *slot):
            m = ph - 1
            return [] if m < 0 else [(m, *p) for p in plans[m // 2].get(slot, ())]

        alone = [(3, "lg"), (3, *moe_pieces(1)[0]), (3, *moe_pieces(1)[1]), (3, "le"),
                 *((3, *p) for p in moe_pieces(1)[2:])]

        block = ctx.enter_context(nc.Block())

        @block.sync
        def _(sp):
            for g in range(2):
                sp.sem_inc(out_done[g].sem, 16)
            consts = [(WA, att_w), (ID, ident), (HM, hmask), (C64, cols64), (RV, None), (CV, cols),
                      (IDB, identb), (GW, gate_w), (B1, b1c), (B2, b2), (BEF, None)]

            def x_load(g):
                sp.dma_start(Xin[:], x_tok[:, bass.ds(g * GB, GB), :]).then_inc(x_in.sem, 16)

            def xf_load(g):
                sp.dma_start(XFin[:], x_feat[:, bass.ds(g * T, T)]).then_inc(xf_in.sem, 16)

            def c_load(g, half):
                sp.dma_start(CF[half][:], ctx_feat[:, bass.ds(g * T, T)])\
                    .then_inc(c_in[half].sem, 16)

            def m_load(g, a):
                for i, m in enumerate(((m_self, m_selfT), (m_cross, m_crossT))[a]):
                    sp.dma_start(MI[:, i], m[:, bass.ds(g * GB, GB), :]).then_inc(m_in.sem, 16)

            xf_load(0)
            for tile, src in consts:
                if src is None:
                    r = rows if tile is RV else before
                    src = bass.AP(r.tensor, 0, [[0, 128], [1, r.shape[1]]])
                    dst = tile[:] if tile is RV else tile[:].rearrange("p i j -> p (i j)")
                    sp.dma_start(dst, src).then_inc(w_in.sem, 16)
                else:
                    sp.dma_start(tile[:], src).then_inc(w_in.sem, 16)
            for t in KX:
                sp.dma_start(t[KR - SR:KR], shift_ones).then_inc(kx_ones.sem, 16)
            c_load(0, 0)
            x_load(0)
            m_load(0, 0)
            for l, (a, b) in enumerate(((w1_0, w2_0), (w1_1, w2_1))):
                for e in range((E0, E1)[l]):
                    sp.dma_start(W1[l][:, e], a[:, e]).then_inc(moe_w[l].sem, 16)
                    sp.dma_start(W2[l][:, e], b[:, e]).then_inc(moe_w[l].sem, 16)
                if l == 0:
                    c_load(1, 1)

            def turn(it, more):
                group = 2 * it
                sp.wait_ge(x0.sem, x0.at(it, 1))
                x_load(group + 1)
                sp.wait_ge(pk.sem, pk.at(it, GB))
                sp.wait_ge(pq.sem, pq.at(it, GB))
                xf_load(group + 1)
                sp.wait_ge(mz.sem, mz.at(it, 1))
                m_load(group, 1)
                sp.wait_ge(mz.sem, mz.at(it, 2))
                m_load(group + 1, 0)
                sp.wait_ge(mz.sem, mz.at(it, 3))
                m_load(group + 1, 1)
                if more:
                    sp.wait_ge(x0.sem, x0.at(it, 2))
                    x_load(group + 2)
                    sp.wait_ge(pk.sem, pk.at(it, LSTEPS + GB))
                    sp.wait_ge(pq.sem, pq.at(it, LSTEPS + GB))
                    xf_load(group + 2)
                    sp.wait_ge(mz.sem, mz.at(it, 4))
                    m_load(group + 2, 0)
                    sp.wait_ge(pk.sem, pk.at(it, 3 * LSTEPS))
                    c_load(group + 2, 0)
                    sp.wait_ge(pk.sem, pk.at(it, 4 * LSTEPS))
                    c_load(group + 3, 1)
                for g in range(2):
                    sp.wait_ge(acc.sem, acc.at(it, moe_first(3 + g)))
                    sp.dma_start(out[:, bass.ds((group + g) * GB, GB), :], X[g][:])\
                        .then_inc(out_done[g].sem, 16)

            with sp.Fori(0, TURNS - 1) as it:
                turn(it, True)
            turn(TURNS - 1, False)
            for g in range(2):
                sp.wait_ge(out_done[g].sem, out_done[g].at(TURNS, 16))

        N_CONST = 11

        @block.tensor
        def _(pe):
            pe.wait_ge(w_in.sem, 16 * N_CONST)
            pe.wait_ge(c_zero.sem, 1)
            pe.wait_ge(kx_ones.sem, 16 * 3)
            pe.wait_ge(kb_ones.sem, 2)

            with pe.Fori(0, TURNS) as it:
                def w_of(n):
                    l, g, a, b = stage(n)
                    return (2 * l + a) * 4

                def proj_kv(n):
                    l, g, a, b = stage(n)
                    if l == 0 and a == 0 and b == 0:
                        pe.wait_ge(xf_in.sem, xf_in.at(it, 16 * (g + 1)))
                    if l == 0 and a == 1 and b == 0:
                        pe.wait_ge(c_in[g].sem, c_in[g].at(it, 16))
                    if l == 1 and a == 0 and b == 0:
                        pe.wait_ge(jxc.sem, jxc.at(it, g + 1))
                    if n:
                        pe.wait_ge(qs.sem, qs.at(it, n))
                    if n == 3 * LSTEPS:
                        pe.wait_ge(cw.sem, cw.at(it, LSTEPS))
                    w = w_of(n)
                    for h in range(2):
                        pe.matmul(PK[:, h * S:(h + 1) * S], WA[:, w + 1, h * 64:h * 64 + 64],
                                  kv_input(n), start=True, stop=True)
                    pe.matmul(PV, kv_input(n), WA[:, w + 2, :], start=True, stop=True)\
                        .then_inc(pk.sem, 1)

                def proj_q(n):
                    l, g, a, b = stage(n)
                    pe.wait_ge(va.sem, va.at(it, n + 1))
                    if l == 1 and n % LSTEPS >= 2:
                        pe.wait_ge(cw.sem, cw.at(it, n - 2 - N0 + 1))
                    if a == 1:
                        pe.wait_ge(xtc.sem, xtc.at(it, n - GB + 1))
                    w = w_of(n)
                    for h in range(2):
                        mm = pe.matmul(PQ[:, h * S:(h + 1) * S], WA[:, w, h * 64:h * 64 + 64],
                                       q_input(n), start=True, stop=True)
                    mm.then_inc(pq.sem, 1)

                def scores1(n, g):
                    l, gr_, a, b = stage(n)
                    if g == 0:
                        pe.wait_ge(kb.sem, kb.at(it, n + 1))
                        pe.wait_ge(qs.sem, qs.at(it, n + 1))
                        if n == 2 * LSTEPS or n == 3 * LSTEPS:
                            pe.wait_ge(ma.sem, ma.at(it, 2 * gr_ + 2))
                    q = 4 * n + g
                    free = q if n >= LSTEPS else q - 1
                    if free > 0:
                        pe.wait_ge(mx.sem, mx.at(it, free))
                    o = s1_bank(n, g)
                    if l:
                        pe.matmul(o[:], IDB[:],
                                  MA[gr_][:, 2 * a, b:b + 1, :].broadcast_to((128, 4, S)),
                                  start=True, stop=False, skip_group_check=True)
                    pe.matmul(o[:], QS[n % 4][:, g // 2, :], KB[n % 2][:, 4 * g:4 * g + 4, :],
                              start=not l, stop=True, skip_group_check=True).then_inc(s1.sem, 1)

                def shift_rows(n):
                    pe.wait_ge(nm.sem, nm.at(it, n + 1))
                    ph, s = divmod(n, LSTEPS)
                    if s == 0 and ph == 1:
                        pe.wait_ge(xtc.sem, xtc.at(it, n))
                    if s == 0 and ph >= 2:
                        pe.wait_ge(jxc.sem, jxc.at(it, ph - 1))
                    if s == 1:
                        pe.wait_ge(nmc.sem, nmc.at(it, n))
                    if s == 2:
                        pe.wait_ge(atc.sem, atc.at(it, n - 1))
                    if s >= 3:
                        pe.wait_ge(xtc.sem, xtc.at(it, n - 2))
                    for h in range(2):
                        mm = pe.transpose(MB[0:SR, h * S:(h + 1) * S], NM[:, n % 2, h, :], ID[:])
                    mm.then_inc(nmt.sem, 1)

                def scores2(n, g):
                    l, gr_, a, b = stage(n)
                    q = 4 * n + g
                    if g == 0:
                        pe.wait_ge(kx.sem, kx.at(it, n + 1))
                        pe.wait_ge(nmc.sem, nmc.at(it, n + 1))
                    free = q if n >= LSTEPS else q - 1
                    if free > 0:
                        pe.wait_ge(ex.sem, ex.at(it, free))
                    o = s2_bank(n, g)
                    if l:
                        pe.matmul(o[:], IDB[:],
                                  MA[gr_][:, 2 * a + 1, b:b + 1, :].broadcast_to((128, 4, S)),
                                  start=True, stop=False, skip_group_check=True)
                    for j in range(4):
                        mm = pe.matmul(o[:, j * S:(j + 1) * S], KX[n % 3][:, 4 * g + j, :],
                                       Q9[n % 4][:, g // 2, :], start=not l, stop=True,
                                       skip_group_check=True)
                    mm.then_inc(s2.sem, 1)

                def values(n, g):
                    pe.wait_ge(ex.sem, ex.at(it, 4 * n + g + 1))
                    if g == 0:
                        pe.wait_ge(va.sem, va.at(it, n + 1))
                        if n:
                            pe.wait_ge(otc.sem, otc.at(it, n))
                    for j in range(4):
                        mm = pe.matmul(OB[32 * j:32 * j + HD + 1, g * S:(g + 1) * S],
                                       VA[n % 4][:, 4 * g + j, :], PT[:, g, j, :],
                                       start=True, stop=True, skip_group_check=True)
                    mm.then_inc(av.sem, 1)

                def masked_values(n):
                    l, g, a, b = stage(n)
                    if a == 0 and b == 0:
                        pe.wait_ge(mz.sem, mz.at(it, 2 * g + 2))
                    end = (n // LSTEPS + 1) * LSTEPS
                    pe.wait_ge(va.sem, va.at(it, min(n + 3, end)))
                    pe.wait_ge(qs.sem, qs.at(it, min(n + 2, end)))
                    if n > N0:
                        pe.wait_ge(cw.sem, cw.at(it, n - N0))
                    pe.matmul(PB[:, 0:H * (HD + 1)], MZ[g][:, a, b, :],
                              VA[n % 4][:].rearrange("p h d -> p (h d)"), start=True, stop=True)\
                        .then_inc(wz.sem, 1)

                def token_major(n):
                    pe.wait_ge(otc.sem, otc.at(it, n + 1))
                    if n:
                        pe.wait_ge(rr.sem, rr.at(it, n))
                    for g in range(4):
                        mm = pe.transpose(TB[:, g * 128:(g + 1) * 128], OT[:, n % 2, g, :], ID[:])
                    mm.then_inc(ott.sem, 1)

                def heads_back(n):
                    pe.wait_ge(an.sem, an.at(it, n + 1))
                    if (n + 1) % LSTEPS:
                        pe.wait_ge(nmc.sem, nmc.at(it, n + 2))
                    else:
                        pe.wait_ge(xtc.sem, xtc.at(it, n - 1))
                    pe.transpose(MB[:, 0:128], AN[:, n % 2, :], ID[:]).then_inc(ant.sem, 1)

                def out_proj(n):
                    pe.wait_ge(atc.sem, atc.at(it, n + 1))
                    pe.matmul(TB[:, 0:128], AT[:, n % 2, :], WA[:, w_of(n) + 3, :],
                              start=True, stop=True).then_inc(zo.sem, 1)

                def feature_major(n):
                    pe.wait_ge(yn.sem, yn.at(it, n + 1))
                    if (n + 1) % LSTEPS:
                        pe.wait_ge(atc.sem, atc.at(it, n + 2))
                    else:
                        pe.wait_ge(xtc.sem, xtc.at(it, n))
                    pe.transpose(MB[:, 0:128], YN[:, n % 2, :], ID[:]).then_inc(xtt.sem, 1)

                def layer_input(m):
                    pe.wait_ge(jy.sem, jy.at(it, m + 1))
                    pe.wait_ge(xtc.sem, xtc.at(it, (m + 2) * LSTEPS))
                    for b in range(GB):
                        mm = pe.transpose(MB[:, b * 128:(b + 1) * 128], JT[:, b, :], ID[:])
                    mm.then_inc(jxt.sem, 1)

                def logits(m):
                    l, g = divmod(m, 2)
                    if m < 2:
                        pe.wait_ge(moe_w[0].sem, 16 * 2 * E0)
                    else:
                        pe.wait_ge(moe_w[1].sem, 16 * 2 * E1)
                    pe.wait_ge(xtc.sem, xtc.at(it, (m + 1) * LSTEPS))
                    if m == 0:
                        pe.wait_ge(mx.sem, mx.at(it, 4 * LSTEPS))
                        pe.wait_ge(ex.sem, ex.at(it, 4 * LSTEPS))
                    else:
                        pe.wait_ge(acc.sem, acc.at(it, moe_first(m)))
                    for b in range(GB):
                        mm = pe.matmul(bank[7][:, b * NE:(b + 1) * NE], tok(XC[g], b), GW[:, l, :],
                                       start=True, stop=True)
                    mm.then_inc(lgt.sem, 1)
                    if m == 3:
                        pe.wait_ge(mx.sem, mx.at(it, 4 * N))
                        pe.wait_ge(ex.sem, ex.at(it, 4 * N))
                        pe.wait_ge(otc.sem, otc.at(it, N))
                        pe.wait_ge(rr.sem, rr.at(it, N))

                def hidden(m, e, c):
                    l, g = divmod(m, 2)
                    k = HC * e + c
                    back = HC if m == 3 else 1
                    if k >= back:
                        sig_, at = hidden_done(m, k - back + 1)
                        pe.wait_ge(sig_.sem, sig_.at(it, at))
                    pe.matmul(h_bank(m, c)[:], W1[l][:, e, c * 128:(c + 1) * 128], XC[g][:],
                              start=True, stop=True).then_inc(ht.sem, 1)

                def expert_out(m, e, b):
                    l, g = divmod(m, 2)
                    if b == 0:
                        sig_, at = hidden_done(m, HC * (e + 1))
                        pe.wait_ge(sig_.sem, sig_.at(it, at))
                        if e == 0:
                            pe.wait_ge(lg.sem, lg.at(it, m + 1))
                        elif e == 1 and l == 0:
                            pe.wait_ge(xb2.sem, xb2.at(it, m + 1))
                        elif m == 3 and e >= 2:
                            pe.wait_ge(acc.sem, acc.at(it, moe_first(m) + e - 1))
                        elif m < 3:
                            pe.wait_ge(acc.sem, acc.at(it, moe_first(m) + e))
                    for c in range(HC):
                        mm = pe.matmul(y_bank(m, e)[:, b * 128:(b + 1) * 128],
                                       HT[:, e % 2, c, b * 128:(b + 1) * 128],
                                       W2[l][:, e, c, :], start=(c == 0), stop=(c == HC - 1),
                                       skip_group_check=True)
                    if b == GB - 1:
                        mm.then_inc(yt.sem, 1)

                def gates_back(m):
                    pe.wait_ge(gg.sem, gg.at(it, m + 1))
                    pe.wait_ge(acc.sem, acc.at(it, moe_first(m) + 1))
                    for b in range(GB):
                        mm = pe.transpose(bank[7][0:NE, b * 128:(b + 1) * 128], G[:, b, :], ID[:])
                    mm.then_inc(gtt.sem, 1)

                def gates_b2(m):
                    pe.wait_ge(gtc.sem, gtc.at(it, m + 1))
                    for b in range(GB):
                        mm = pe.matmul(bank[7][:, b * 128:(b + 1) * 128], GTT[:, b, :], B2[:],
                                       start=True, stop=True)
                    mm.then_inc(b2t.sem, 1)

                def experts(ps):
                    for m, kind, *at in ps:
                        if kind == "lg":
                            logits(m)
                        elif kind == "h":
                            hidden(m, *at)
                        elif kind == "y":
                            expert_out(m, *at)
                        elif kind == "gt":
                            gates_back(m)
                        elif kind == "b2":
                            gates_b2(m)

                for ph in range(PHASES):
                    n0 = ph * LSTEPS
                    for i, (f, n) in enumerate(((proj_kv, n0), (proj_q, n0), (proj_kv, n0 + 1),
                                                (proj_q, n0 + 1), (proj_kv, n0 + 2))):
                        f(n)
                        experts(pieces(ph, "fill", i))
                    for g in range(4):
                        scores1(n0, g)
                        experts(pieces(ph, "fill", 5 + g))
                    shift_rows(n0)
                    for s in range(LSTEPS + 2):
                        n = n0 + s
                        on, more, last = s < LSTEPS, s < LSTEPS - 1, 1 <= s <= LSTEPS
                        l = n0 // N0
                        if more:
                            scores1(n + 1, 0)
                        if last:
                            token_major(n - 1)
                        if on:
                            scores2(n, 0)
                        if more:
                            scores1(n + 1, 1)
                        experts(pieces(ph, s, 0))
                        if last:
                            heads_back(n - 1)
                        if on:
                            if l:
                                masked_values(n)
                            scores2(n, 1)
                            values(n, 0)
                        if more:
                            scores1(n + 1, 2)
                        experts(pieces(ph, s, 1))
                        if last:
                            out_proj(n - 1)
                        if s >= 2:
                            feature_major(n - 2)
                        if on:
                            scores2(n, 2)
                            values(n, 1)
                        if more:
                            scores1(n + 1, 3)
                        experts(pieces(ph, s, 2))
                        if s + 2 < LSTEPS:
                            proj_q(n + 2)
                        if on:
                            scores2(n, 3)
                            values(n, 2)
                        if s + 3 < LSTEPS:
                            proj_kv(n + 3)
                        experts(pieces(ph, s, 3))
                        if more:
                            shift_rows(n + 1)
                        if on:
                            values(n, 3)
                    if ph in (1, 2):
                        layer_input(ph - 1)
                experts(alone)
                pe.wait_ge(acc.sem, acc.at(it, EX))

        @block.scalar
        def _(act):
            act.wait_ge(w_in.sem, 16 * N_CONST)
            act.wait_ge(c_zero.sem, 1)
            for a in range(2):
                for h in range(2):
                    act.activation(QB[:, 2 * a + h:2 * a + h + 1], C64[:, 4 * a + h:4 * a + h + 1],
                                   ACT.Copy, scale=SCALE).then_inc(c_qb.sem, 1)
            act.activation(CR[:], col("norm1_w"), ACT.Copy, scale=float(D) ** 0.5)\
                .then_inc(c_qb.sem, 1)
            act.wait_ge(c_qb.sem, 5)

            with act.Fori(0, TURNS) as it:
                def queries(n):
                    l, g, a, b = stage(n)
                    act.wait_ge(pq.sem, pq.at(it, n + 1))
                    if l == 0:
                        for h in range(2):
                            i = act.activation(Q9[n % 4][0:64, h, :], PQ[:, h * S:(h + 1) * S],
                                               ACT.Identity, scale=SCALE,
                                               bias=QB[:, 2 * a + h:2 * a + h + 1])
                    else:
                        i = act.activation(Q9[n % 4][0:64, :, :].rearrange("p h t -> p (h t)"), PQ,
                                           ACT.Copy, scale=SCALE)
                    i.then_inc(q9.sem, 1)
                    act.wait_ge(q9.sem, q9.at(it, n + 1))
                    act.activation(QS[n % 4][0:64, :, :], Q9[n % 4][0:64, :, :], ACT.Copy)\
                        .then_inc(qs.sem, 1)

                def exps(n, g):
                    act.wait_ge(s2.sem, s2.at(it, 4 * n + g + 1))
                    act.activation(PT[:, g], s2_bank(n, g)[:], ACT.Exp).then_inc(ex.sem, 1)

                def shift_copy(n):
                    act.wait_ge(nmt.sem, nmt.at(it, n + 1))
                    act.activation(Q9[n % 4][64:96, :, :],
                                   MB[0:SR, 0:2 * S].rearrange("p (h t) -> p h t", h=2),
                                   ACT.Copy).then_inc(nmc.sem, 1)
                    if n >= N0:
                        act.wait_ge(ca.sem, ca.at(it, n - N0 + 1))
                        act.activation(CE[:, n % 2], CA[:, n % 2], ACT.Exp).then_inc(ce.sem, 1)

                def values_copy(n):
                    act.wait_ge(av.sem, av.at(it, 4 * n + 4))
                    act.activation(OT[:, n % 2].rearrange("p g t -> p (g t)"), OB[:],
                                   ACT.Copy).then_inc(otc.sem, 1)

                def heads_copy(n):
                    act.wait_ge(ant.sem, ant.at(it, n + 1))
                    act.activation(AT[:, n % 2, :], MB[:, 0:128], ACT.Copy).then_inc(atc.sem, 1)

                def norm_scale(n):
                    l, g, a, b = stage(n)
                    name = [["n1", "n2"], ["norm2", "norm3"]][l][a]
                    act.wait_ge(xtt.sem, xtt.at(it, n + 1))
                    act.activation(tok((XB, XC[g])[a], b), MB[:, 0:128], ACT.Identity,
                                   scale=col(name + ("_w" if l else "_g")),
                                   bias=0.0 if l else col(name + "_b")).then_inc(xtc.sem, 1)

                def experts(ps):
                    for m, kind, *at in ps:
                        if kind == "le":
                            act.wait_ge(lz.sem, lz.at(it, m + 1))
                            act.activation(LE[:], LZ[:], ACT.Exp).then_inc(le.sem, 1)
                        elif kind == "gt":
                            act.wait_ge(gtt.sem, gtt.at(it, m + 1))
                            act.activation(GTT[:].rearrange("p b t -> p (b t)"), bank[7][0:NE, :],
                                           ACT.Copy).then_inc(gtc.sem, 1)
                        elif kind == "h":
                            e, c = at
                            act.wait_ge(ht.sem, ht.at(it, HC * (moe_first(m) + e) + c + 1))
                            if m < 2:
                                act.activation(HT[:, e % 2, c, :], h_bank(m, c)[:], ACT.Relu,
                                               bias=B1[:, e, c:c + 1]).then_inc(hr.sem, 1)
                            else:
                                act.activation(HT[:, e % 2, c, :], h_bank(m, c)[:], ACT.Tanh,
                                               scale=0.5).then_inc(th.sem, 1)

                for ph in range(PHASES):
                    n0 = ph * LSTEPS
                    for i in range(5):
                        if i in (1, 3):
                            queries(n0 + i // 2)
                        experts(pieces(ph, "fill", i))
                    for g in range(4):
                        experts(pieces(ph, "fill", 5 + g))
                    shift_copy(n0)
                    for s in range(LSTEPS + 2):
                        n = n0 + s
                        on, more, last = s < LSTEPS, s < LSTEPS - 1, 1 <= s <= LSTEPS
                        if last:
                            values_copy(n - 1)
                        if on:
                            exps(n, 0)
                        experts(pieces(ph, s, 0))
                        if last:
                            heads_copy(n - 1)
                        if on:
                            exps(n, 1)
                        experts(pieces(ph, s, 1))
                        if s >= 2:
                            norm_scale(n - 2)
                        if on:
                            exps(n, 2)
                        experts(pieces(ph, s, 2))
                        if s + 2 < LSTEPS:
                            queries(n + 2)
                        if on:
                            exps(n, 3)
                        experts(pieces(ph, s, 3))
                        if more:
                            shift_copy(n + 1)
                    if ph in (1, 2):
                        act.wait_ge(jxt.sem, jxt.at(it, ph))
                        act.activation(XA[:], MB[:], ACT.Copy, scale=CR[:]).then_inc(jxc.sem, 1)
                experts(alone)

        @block.vector
        def _(dve):
            dve.memset(NM[:], 0.0)
            dve.memset(OB[:], 0.0)
            for t in Q9:
                dve.memset(t[64:96], 0.0)
            for t in VA:
                dve.memset(t[:, :, HD:HD + 1], 1.0)
            for t in QS:
                i = dve.memset(t[64:96], 0.0)
            i.then_inc(c_zero.sem, 1)
            dve.wait_ge(kx_ones.sem, 16 * 3)
            for i in range(2):
                dve.tensor_copy(KB[i][64:96], KX[i][64:96]).then_inc(kb_ones.sem, 1)
            dve.wait_ge(w_in.sem, 16 * N_CONST)
            dve.tensor_tensor(BS[:, 0], row("n1_b"), row("ca_bo"), ALU.add).then_inc(c_bs.sem, 1)
            dve.tensor_copy(BS[:, 1], row("n2_b")).then_inc(c_bs.sem, 1)

            with dve.Fori(0, TURNS) as it:
                def keys_values(n):
                    l, g, a, b = stage(n)
                    dve.wait_ge(pk.sem, pk.at(it, n + 1))
                    if n >= 2:
                        dve.wait_ge(kx.sem, kx.at(it, n - 1))
                    if l == 0:
                        for h in range(2):
                            i = dve.tensor_scalar(K9[:, n % 2, h, :], PK[:, h * S:(h + 1) * S],
                                                  C64[:, 4 * a + 2 + h:4 * a + 3 + h], None, ALU.add)
                    else:
                        i = dve.tensor_copy(K9[:, n % 2].rearrange("p h t -> p (h t)"), PK)
                    i.then_inc(k9.sem, 1)
                    v = PV.rearrange("p (h d) -> p h d", h=H)
                    if l == 0:
                        i = dve.tensor_tensor(VA[n % 4][:, :, 0:HD], v,
                                              row(("sa_bv", "ca_bv")[a]).rearrange(
                                                  "p (h d) -> p h d", h=H), ALU.add)
                    else:
                        i = dve.tensor_copy(VA[n % 4][:, :, 0:HD], v)
                    i.then_inc(va.sem, 1)

                def keys_bf16(n):
                    dve.wait_ge(kx.sem, kx.at(it, n + 1))
                    dve.tensor_copy(KB[n % 2][0:64], KX[n % 3][0:64]).then_inc(kb.sem, 1)

                def row_max(n, g):
                    dve.wait_ge(s1.sem, s1.at(it, 4 * n + g + 1))
                    dve.tensor_reduce(MX[:, n % 2, 4 * g:4 * g + 4],
                                      s1_bank(n, g)[:].rearrange("p (j k) -> p j k", j=4),
                                      AX.X, ALU.max).then_inc(mx.sem, 1)

                def shift(n):
                    l, g, a, b = stage(n)
                    dve.wait_ge(mx.sem, mx.at(it, 4 * n + 4))
                    src = MX[:, n % 2].rearrange("p (a h) -> p a h", a=2)
                    dst = NM[:, n % 2, :, 0:HALF]
                    if l == 0:
                        dve.tensor_scalar(dst, src, -1.0, None, ALU.mult).then_inc(nm.sem, 1)
                    else:
                        dve.tensor_scalar(dst, src, MF[:, a, b, 3:4], -1.0, ALU.max, ALU.mult)\
                            .then_inc(nm.sem, 1)
                        dve.wait_ge(nm.sem, nm.at(it, n + 1))
                        dve.tensor_scalar(CA[:, n % 2].rearrange("p (a h) -> p a h", a=2), dst,
                                          NEG, 0.0, ALU.add, ALU.min).then_inc(ca.sem, 1)

                def masked_sum(n):
                    m = n - N0
                    dve.wait_ge(wz.sem, wz.at(it, m + 1))
                    dve.wait_ge(ce.sem, ce.at(it, m + 1))
                    c = CE[:, n % 2].rearrange("p (h o) -> p h o", o=1)\
                        .broadcast_to((128, H, HD + 1))
                    dve.tensor_tensor(CW[:, n % 2],
                                      PB[:, 0:H * (HD + 1)].rearrange("p (h d) -> p h d", h=H),
                                      c, ALU.mult).then_inc(cw.sem, 1)

                def normalise(n):
                    dve.wait_ge(ott.sem, ott.at(it, n + 1))
                    o = TB[:].rearrange("p (h r) -> p h r", h=H)
                    if n >= N0:
                        m = n - N0
                        dve.wait_ge(cw.sem, cw.at(it, m + 1))
                        dve.tensor_tensor(OW[:], o[:, :, 0:HD + 1], CW[:, n % 2], ALU.add)\
                            .then_inc(ow.sem, 1)
                        dve.wait_ge(ow.sem, ow.at(it, m + 1))
                        o = OW[:]
                    dve.reciprocal(RS[:, n % 2].rearrange("p (h o) -> p h o", o=1), o[:, :, HD:HD + 1])\
                        .then_inc(rs.sem, 1)
                    dve.wait_ge(rs.sem, rs.at(it, n + 1))
                    r = RS[:, n % 2].rearrange("p (h o) -> p h o", o=1).broadcast_to((128, H, HD))
                    dve.tensor_tensor(AN[:, n % 2].rearrange("p (h d) -> p h d", h=H),
                                      o[:, :, 0:HD], r, ALU.mult).then_inc(an.sem, 1)

                def residual(n):
                    l, g, a, b = stage(n)
                    dve.wait_ge(zo.sem, zo.at(it, n + 1))
                    if l == 0:
                        if a == 0 and b == 0:
                            dve.wait_ge(x0.sem, x0.at(it, g + 1))
                        if a == 1:
                            dve.wait_ge(xg.sem, xg.at(it, n - GB + 1))
                        slot = n % 2
                        dve.tensor_tensor(RR[:, slot], TB[:, 0:128], X[g][:, b], ALU.add)\
                            .then_inc(rr.sem, 1)
                        dve.wait_ge(rr.sem, rr.at(it, n + 1))
                        dve.bn_stats(BN[:, slot], RR[:, slot]).then_inc(bns.sem, 1)
                        dve.wait_ge(bns.sem, bns.at(it, n + 1))
                        dve.tensor_copy(TICK[:, 1:2], BN[:, slot, 0:1])
                        dve.bn_aggr(MV[:, slot], BN[:, slot]).then_inc(mv.sem, 1)
                    else:
                        dve.tensor_tensor(X[g][:, b], TB[:, 0:128], X[g][:, b], ALU.add)\
                            .then_inc(rr.sem, 1)
                        dve.wait_ge(rr.sem, rr.at(it, n + 1))
                        dve.scalar_tensor_tensor(SQ[:], X[g][:, b], 1.0, X[g][:, b], ALU.mult,
                                                 ALU.mult, accum_out=SS[:, n % 2:n % 2 + 1])\
                            .then_inc(ss.sem, 1)

                def norm_out(n):
                    l, g, a, b = stage(n)
                    dve.wait_ge(rd.sem, rd.at(it, n + 1))
                    if n >= 2:
                        dve.wait_ge(xtt.sem, xtt.at(it, n - 1))
                    if l == 0:
                        dve.tensor_scalar(YN[:, n % 2], RR[:, n % 2], MV[:, n % 2, 0:1],
                                          RD[:, n % 2:n % 2 + 1], ALU.subtract, ALU.mult)\
                            .then_inc(yn.sem, 1)
                    else:
                        dve.tensor_scalar(YN[:, n % 2], X[g][:, b], RD[:, n % 2:n % 2 + 1],
                                          float(D) ** 0.5, ALU.mult, ALU.mult).then_inc(yn.sem, 1)

                def mask_floor(g):
                    for a in range(2):
                        i = dve.tensor_reduce(MF[:, a, :, 0:1].rearrange("p b o -> p (b o)"),
                                              MA[g][:, 2 * a], AX.X, ALU.min)
                    i.then_inc(mf.sem, 1)
                    dve.wait_ge(mf.sem, mf.at(it, 3 * g + 1))
                    dve.tensor_scalar(MF[:, :, :, 1], MF[:, :, :, 0], 0.0, -BIG,
                                      ALU.is_ge, ALU.mult)
                    dve.tensor_scalar(MF[:, :, :, 2], MF[:, :, :, 0], 0.0, NEG,
                                      ALU.is_lt, ALU.mult).then_inc(mf.sem, 1)
                    dve.wait_ge(mf.sem, mf.at(it, 3 * g + 2))
                    dve.tensor_tensor(MF[:, :, :, 3], MF[:, :, :, 1], MF[:, :, :, 2], ALU.add)\
                        .then_inc(mf.sem, 1)
                    dve.wait_ge(mf.sem, mf.at(it, 3 * g + 3))

                def per_batch(t):
                    return t.rearrange("p (b o) -> p b o", o=1).broadcast_to((128, GB, D))

                def junction_stats(m):
                    dve.wait_ge(acc.sem, acc.at(it, moe_first(m + 1)))
                    for b in range(GB):
                        i = dve.bn_stats(JB[:, b], X[m][:, b])
                    i.then_inc(jb.sem, 1)
                    dve.wait_ge(jb.sem, jb.at(it, m + 1))
                    dve.tensor_copy(TICK[:, 2:3], JB[:, 0, 0:1])
                    for b in range(GB):
                        i = dve.bn_aggr(JM[:, b], JB[:, b])
                    i.then_inc(jm.sem, 1)

                def junction_norm(m):
                    dve.wait_ge(jd.sem, jd.at(it, 2 * m + 1))
                    for b in range(GB):
                        i = dve.tensor_scalar(JT[:, b], X[m][:, b], JM[:, b, 0:1],
                                              JD[:, 0, b:b + 1], ALU.subtract, ALU.mult)
                    i.then_inc(jt.sem, 1)
                    dve.wait_ge(jt.sem, jt.at(it, 4 * m + 1))
                    for step, (dst, a, b, op) in enumerate((
                            (JT, JT, "n3_g", ALU.mult), (X[m], JT, "n3_b", ALU.add),
                            (JT, X[m], None, ALU.mult))):
                        b = X[m][:] if b is None else row(b).rearrange("p (o d) -> p o d", o=1)\
                            .broadcast_to((128, GB, D))
                        dve.tensor_tensor(dst[:], a[:], b, op).then_inc(jt.sem, 1)
                        dve.wait_ge(jt.sem, jt.at(it, 4 * m + step + 2))
                    dve.tensor_reduce(JS[:], JT[:], AX.X, ALU.add).then_inc(js.sem, 1)

                def junction_rms(m):
                    dve.wait_ge(jd.sem, jd.at(it, 2 * m + 2))
                    dve.wait_ge(js.sem, js.at(it, m + 1))
                    dve.tensor_tensor(JT[:], X[m][:], per_batch(JD[:, 1]), ALU.mult)\
                        .then_inc(jy.sem, 1)

                def rank(m):
                    dve.wait_ge(lgt.sem, lgt.at(it, m + 1))
                    lgp = bank[7][:, 0:GB * NE].rearrange("p (b e) -> p b e", b=GB)
                    if m < 2:
                        rb = RV[:, len(ROWS) * D:].rearrange("p (o e) -> p o e", o=1)
                        i = dve.tensor_tensor(LG[:], lgp, rb.broadcast_to((128, GB, NE)), ALU.add)
                    else:
                        i = dve.tensor_copy(LG[:], lgp)
                    i.then_inc(lg.sem, 1)
                    dve.wait_ge(lg.sem, lg.at(it, m + 1))
                    dve.tensor_reduce(LM[:], LG[:], AX.X, ALU.max).then_inc(lm.sem, 1)
                    for b in range(GB):
                        other = LG[:, b:b + 1, :].broadcast_to((128, NE, NE))
                        own = LG[:, b, :].rearrange("p (i o) -> p i o", o=1)\
                            .broadcast_to((128, NE, NE))
                        dve.tensor_tensor(GT[:, b], other, own, ALU.is_gt)
                        i = dve.tensor_tensor(EQ[:, b], other, own, ALU.is_equal)
                    i.then_inc(lgr.sem, 1)
                    dve.wait_ge(lm.sem, lm.at(it, m + 1))
                    lmb = LM[:].rearrange("p (b o) -> p b o", o=1).broadcast_to((128, GB, NE))
                    dve.tensor_tensor(LZ[:], LG[:], lmb, ALU.subtract).then_inc(lz.sem, 1)
                    dve.wait_ge(lgr.sem, lgr.at(it, 4 * m + 1))
                    bef = BEF[:].rearrange("p i j -> p (i j)").rearrange("p (o k) -> p o k", o=1)
                    eq = EQ[:].rearrange("p b i j -> p b (i j)")
                    dve.tensor_tensor(eq, eq, bef.broadcast_to((128, GB, NE * NE)), ALU.mult)\
                        .then_inc(lgr.sem, 1)
                    dve.wait_ge(lgr.sem, lgr.at(it, 4 * m + 2))
                    dve.tensor_tensor(GT[:], GT[:], EQ[:], ALU.add).then_inc(lgr.sem, 1)
                    dve.wait_ge(lgr.sem, lgr.at(it, 4 * m + 3))
                    dve.tensor_reduce(RK[:], GT[:], AX.X, ALU.add).then_inc(lgr.sem, 1)

                def gates(m):
                    dve.wait_ge(lgr.sem, lgr.at(it, 4 * m + 4))
                    dve.wait_ge(le.sem, le.at(it, m + 1))
                    dve.scalar_tensor_tensor(GE[:], RK[:], 1.5, LE[:], ALU.is_lt, ALU.mult)\
                        .then_inc(ge.sem, 1)
                    dve.wait_ge(ge.sem, ge.at(it, m + 1))
                    dve.tensor_reduce(GS[:], GE[:], AX.X, ALU.add).then_inc(gs.sem, 1)
                    dve.wait_ge(gs.sem, gs.at(it, m + 1))
                    dve.reciprocal(GR[:], GS[:]).then_inc(gr.sem, 1)
                    dve.wait_ge(gr.sem, gr.at(it, m + 1))
                    grb = GR[:].rearrange("p (b o) -> p b o", o=1).broadcast_to((128, GB, NE))
                    dve.scalar_tensor_tensor(G[:], GE[:], (1.0, 0.5)[m // 2], grb, ALU.mult,
                                             ALU.mult).then_inc(gg.sem, 1)

                def add_expert(m, e):
                    g, x = m % 2, moe_first(m) + e
                    y = y_bank(m, e)
                    dve.wait_ge(yt.sem, yt.at(it, x + 1))
                    if e == 0:
                        dve.wait_ge(gg.sem, gg.at(it, m + 1))
                        if m < 2:
                            dve.wait_ge(xg.sem, xg.at(it, (m + 1) * LSTEPS))
                    else:
                        dve.wait_ge(acc.sem, acc.at(it, x))
                    if e == NE:
                        dve.scalar_tensor_tensor(X[g][:].rearrange("p b d -> p (b d)"), y[:], 0.5,
                                                 X[g][:].rearrange("p b d -> p (b d)"), ALU.mult,
                                                 ALU.add).then_inc(acc.sem, 1)
                        return
                    for b in range(GB):
                        i = dve.scalar_tensor_tensor(
                            X[g][:, b], y[:, b * 128:(b + 1) * 128], G[:, b, e:e + 1],
                            X[g][:, b], ALU.mult, ALU.add)
                    i.then_inc(acc.sem, 1)

                def experts(ps):
                    for m, kind, *at in ps:
                        if kind == "lg":
                            rank(m)
                        elif kind == "le":
                            gates(m)
                        elif kind == "h" and m >= 2:
                            e, c = at
                            k = HC * (E1 * (m % 2) + e) + c + 1
                            dve.wait_ge(th.sem, th.at(it, k))
                            dve.scalar_tensor_tensor(HT[:, e % 2, c, :], HT[:, e % 2, c, :], 1.0,
                                                     h_bank(m, c)[:], ALU.add, ALU.mult)\
                                .then_inc(hs.sem, 1)
                        elif kind == "y" and at[1] == GB - 1:
                            add_expert(m, at[0])
                        elif kind == "b2":
                            dve.wait_ge(b2t.sem, b2t.at(it, m + 1))
                            dve.wait_ge(acc.sem, acc.at(it, moe_first(m) + 1))
                            x = X[m][:].rearrange("p b d -> p (b d)")
                            dve.tensor_tensor(x, bank[7][:], x, ALU.add).then_inc(xb2.sem, 1)
                            dve.wait_ge(xb2.sem, xb2.at(it, m + 1))

                for ph in range(PHASES):
                    n0 = ph * LSTEPS
                    l, grp = divmod(ph, 2)
                    if l:
                        dve.wait_ge(ma.sem, ma.at(it, 2 * grp + 2))
                        mask_floor(grp)
                    keys_values(n0)
                    experts(pieces(ph, "fill", 0))
                    experts(pieces(ph, "fill", 1))
                    keys_values(n0 + 1)
                    experts(pieces(ph, "fill", 2))
                    experts(pieces(ph, "fill", 3))
                    keys_bf16(n0)
                    keys_values(n0 + 2)
                    experts(pieces(ph, "fill", 4))
                    for g in range(4):
                        row_max(n0, g)
                        experts(pieces(ph, "fill", 5 + g))
                    shift(n0)
                    keys_bf16(n0 + 1)
                    for s in range(LSTEPS + 2):
                        n = n0 + s
                        on, more, last = s < LSTEPS, s < LSTEPS - 1, 1 <= s <= LSTEPS
                        if more:
                            row_max(n + 1, 0)
                        if last:
                            normalise(n - 1)
                        if more:
                            row_max(n + 1, 1)
                        experts(pieces(ph, s, 0))
                        if on and l:
                            masked_sum(n)
                        if s >= 2:
                            norm_out(n - 2)
                        if more:
                            row_max(n + 1, 2)
                        experts(pieces(ph, s, 1))
                        if last:
                            residual(n - 1)
                        if more:
                            row_max(n + 1, 3)
                            shift(n + 1)
                        experts(pieces(ph, s, 2))
                        if s + 3 < LSTEPS:
                            keys_values(n + 3)
                        if s + 2 < LSTEPS:
                            keys_bf16(n + 2)
                        experts(pieces(ph, s, 3))
                        if ph in (1, 2) and s >= LSTEPS - 1:
                            (junction_stats, junction_norm, junction_rms)[s - LSTEPS + 1](ph - 1)
                experts(alone)

        @block.gpsimd
        def _(pool):
            pool.memset(EXPN[:, 0:1], -0.5)
            pool.memset(EXPN[:, 1:2], EPS)
            pool.memset(EXPN[:, 2:3], D * EPS).then_inc(c_bs.sem, 1)
            pool.wait_ge(w_in.sem, 16 * N_CONST)
            pool.wait_ge(c_bs.sem, 3)

            with pool.Fori(0, TURNS) as it:
                def spread(n):
                    pool.wait_ge(k9.sem, k9.at(it, n + 1))
                    if n >= 3:
                        pool.wait_ge(s2.sem, s2.at(it, 4 * (n - 2)))
                        pool.wait_ge(kb.sem, kb.at(it, n - 2))
                    dst = KX[n % 3][0:64].rearrange("p (a h) t -> p a h t", a=2)
                    pool.tensor_tensor(dst[:, :, 0, :], K9[:, n % 2],
                                       HM[:, 0:1].rearrange("p (a o) -> p a o", a=1)
                                       .broadcast_to((64, 2, S)), ALU.mult)
                    for h in range(1, HALF):
                        i = pool.tensor_scalar(dst[:, :, h, :], K9[:, n % 2], HM[:, h:h + 1], 1.0,
                                               ALU.mult, ALU.mult)
                    i.then_inc(kx.sem, 1)

                def inverse_root(src, eps, n):
                    slot = n % 2
                    pool.tensor_tensor(RE[:, slot:slot + 1], src, EXPN[:, eps:eps + 1], ALU.add)\
                        .then_inc(re.sem, 1)
                    pool.wait_ge(re.sem, re.at(it, n + 1))
                    pool.tensor_tensor(RD[:, slot:slot + 1], RE[:, slot:slot + 1], EXPN[:, 0:1],
                                       ALU.pow).then_inc(rd.sem, 1)

                def junction_root(src, eps, m, k):
                    pool.tensor_tensor(JE[:], src, EXPN[:, eps:eps + 1].broadcast_to((128, GB)),
                                       ALU.add).then_inc(je.sem, 1)
                    pool.wait_ge(je.sem, je.at(it, 2 * m + k + 1))
                    pool.tensor_tensor(JD[:, k], JE[:], EXPN[:, 0:1].broadcast_to((128, GB)),
                                       ALU.pow).then_inc(jd.sem, 1)

                def affine(n):
                    l, g, a, b = stage(n)
                    pool.wait_ge(yn.sem, yn.at(it, n + 1))
                    pool.tensor_tensor(YG[:], YN[:, n % 2], row(("n1_g", "n2_g")[a]), ALU.mult)\
                        .then_inc(yg.sem, 1)
                    pool.wait_ge(yg.sem, yg.at(it, n + 1))
                    pool.tensor_tensor(X[g][:, b], YG[:], BS[:, a], ALU.add).then_inc(xg.sem, 1)

                def group_masks(g, a):
                    pool.wait_ge(m_in.sem, m_in.at(it, 32 * (2 * g + a + 1)))
                    pool.tensor_tensor(TICK[:, 0:1], EXPN[:, 0:1], EXPN[:, 0:1], ALU.mult)
                    pool.tensor_scalar(MA[g][:, 2 * a:2 * a + 2].rearrange("p m b t -> p (m b t)"),
                                       MI[:].rearrange("p m b t -> p (m b t)"), 0.0, -BIG,
                                       ALU.is_equal, ALU.mult).then_inc(ma.sem, 1)
                    pool.tensor_scalar(MZ[g][:, a], MI[:, 1], 0.0, 1.0,
                                       ALU.is_equal, ALU.mult).then_inc(mz.sem, 1)

                bo = row("sa_bo").rearrange("p (o d) -> p o d", o=1).broadcast_to((128, GB, D))
                for ph in range(PHASES):
                    n0 = ph * LSTEPS
                    l, grp = divmod(ph, 2)
                    spread(n0)
                    if l == 0:
                        pool.wait_ge(x_in.sem, x_in.at(it, 16 * (grp + 1)))
                        pool.wait_ge(out_done[grp].sem, out_done[grp].at(it, 16))
                        pool.tensor_tensor(X[grp][:], Xin[:], bo, ALU.add).then_inc(x0.sem, 1)
                    spread(n0 + 1)
                    for s in range(LSTEPS + 2):
                        n = n0 + s
                        if s == LSTEPS and ph in (1, 2):
                            pool.wait_ge(jm.sem, jm.at(it, ph))
                            junction_root(JM[:, :, 1], 1, ph - 1, 0)
                        if s + 2 < LSTEPS:
                            spread(n + 2)
                        if l == 0 and s >= 2:
                            affine(n - 2)
                        if 1 <= s <= LSTEPS:
                            m = n - 1
                            if l == 0:
                                pool.wait_ge(mv.sem, mv.at(it, m + 1))
                                inverse_root(MV[:, m % 2, 1:2], 1, m)
                            else:
                                pool.wait_ge(ss.sem, ss.at(it, m - N0 + 1))
                                inverse_root(SS[:, m % 2:m % 2 + 1], 2, m)
                        if s == LSTEPS and ph in (1, 2):
                            pool.wait_ge(js.sem, js.at(it, ph))
                            junction_root(JS[:], 2, ph - 1, 1)
                        if s in (GB, GB + 2) and l == 0:
                            group_masks(grp, (s - GB) // 2)


def kernel(**inputs):
    import ml_dtypes
    import numpy as np
    import concourse.bacc as bacc
    from concourse.bass_utils import run_bass_kernel_spmd as run

    a = {k: np.asarray(v) for k, v in inputs.items()}
    p0 = lambda k: a["L0_xattn_" + k]
    p1 = lambda k: a["L1_xattn_" + k]
    c = np.ascontiguousarray
    x, ctx = a["x"], a["ctx_1024"]
    ms, mc = a["mask_BxSxS_ik0"], a["mask_BxSxS2_if1"]
    att = [p0(f"{s}_w{m}") for s in ("sa", "ca") for m in "qkvo"]
    att += [p1(f"{s}_w{m}").T for s in ("sa", "ca") for m in "qkvo"]
    w1_1 = np.concatenate([p1("exp_w1"), p1("sh_w1")[None]])
    w2_1 = np.concatenate([p1("exp_w2"), p1("sh_w2")[None]])
    half = lambda v: v.reshape(2, 64).T
    eye = np.eye(128, dtype=np.float32)
    ones = np.zeros((SR, H, S), np.float32)
    for h in range(H):
        ones[h % HALF, h] = 1.0
    head = np.zeros((64, HALF), np.float32)
    for h in range(HALF):
        head[h * HD:(h + 1) * HD, h] = 1.0
    arrays = {
        "x_tok": x.transpose(1, 0, 2),
        "x_feat": x.transpose(2, 0, 1).reshape(D, B * S),
        "ctx_feat": ctx.transpose(2, 0, 1).reshape(D, B * S),
        "m_self": ms.transpose(1, 0, 2), "m_selfT": ms.transpose(2, 0, 1),
        "m_cross": mc.transpose(1, 0, 2), "m_crossT": mc.transpose(2, 0, 1),
        "att_w": np.stack(att, 1),
        "w1_0": p0("e_w1").transpose(1, 0, 2),
        "w2_0": p0("e_w2").reshape(E0, HC, 128, D).transpose(2, 0, 1, 3),
        "w1_1": w1_1.transpose(2, 0, 1),
        "w2_1": w2_1.reshape(E1, D, HC, 128).transpose(3, 0, 2, 1),
        "gate_w": np.stack([p0("r_w"), p1("gate_w").T], 1),
        "rows": np.concatenate([p0(r) for r in ROWS] + [p0("r_b")])[None],
        "cols": np.stack([p0(v) for v in COLS[:4]] + [p1(v) for v in COLS[4:]], 1),
        "cols64": np.concatenate([half(p0(f"{s}_b{m}")) for s in ("sa", "ca") for m in "qk"], 1),
        "b1c": p0("e_b1").reshape(E0, HC, 128).transpose(2, 0, 1),
        "b2": p0("e_b2"),
        "ident": eye, "identb": eye.astype(ml_dtypes.bfloat16),
        "hmask": head, "shift_ones": ones,
        "before": np.tril(np.ones((NE, NE), np.float32), -1).reshape(1, NE * NE),
    }
    nc = bacc.Bacc("TRN2", target_bir_lowering=False, num_devices=1)
    feed, args = {}, []
    for name, v in arrays.items():
        v = c(v)
        feed[name] = v
        args.append(nc.dram_tensor(name, v.shape, mybir.dt.from_np(v.dtype),
                                   kind="ExternalInput").ap())
    out = nc.dram_tensor("out", (S, B, D), F32, kind="ExternalOutput").ap()
    two_layers(nc, *args, out)
    r = run(nc, [feed], core_ids=[0])
    return r.results[0]["out"].transpose(1, 0, 2)
```

```python
from contextlib import ExitStack

import concourse.bass as bass
from concourse import mybir

F32 = mybir.dt.float32
F32R = mybir.dt.float32r
BF16 = mybir.dt.bfloat16
I32 = mybir.dt.int32
ALU = mybir.AluOpType
ACT = mybir.ActivationFunctionType
AX = mybir.AxisListType

B, S, D = 16, 128, 128
H, HD = 16, 8
E0, E1, HID = 8, 9, 512
NE = 8
GB = 4
GROUPS = B // GB
T = GB * S
HC = HID // 128
HALF = H // 2
SR = 32
KR = HALF * HD + SR
LSTEPS = 2 * GB
PHASES = 4
STEPS = PHASES * LSTEPS
TURNS = GROUPS // 2
SLOTS = 4
JSLOTS = (0, 1, 2, 3, 6)
L0_SLOTS = 10
SCALE = float(HD) ** -0.5
EPS = 1e-5
NEG = -65504.0
BIG = 1e30

ROWS = ["sa_bv", "ca_bv", "sa_bo", "ca_bo", "n1_g", "n1_b", "n2_g", "n2_b", "n3_g", "n3_b"]
COLS = ["n1_g", "n1_b", "n2_g", "n2_b", "norm1_w", "norm2_w", "norm3_w"]


class Signal:

    def __init__(self, sem, per):
        self.sem, self.per = sem, per

    def at(self, turn, k):
        return turn * self.per + k


def moe_first(m):
    return sum((E0, E1)[j // 2] for j in range(m))


def moe_pieces(l):
    n = (E0, E1)[l]
    out = [("h", 0, c) for c in range(HC)]
    for e in range(1, n):
        h, y = [("h", e, c) for c in range(HC)], [("y", e - 1, b) for b in range(GB)]
        if l == 0 and e == 2:
            out += [h[0], ("gt",), h[1], ("b2",), h[2], y[0], h[3], *y[1:]]
        else:
            out += [p for pair in zip(h, y) for p in pair]
    return out + [("y", n - 1, b) for b in range(GB)]


def moe_slots(m):
    first = SLOTS * (LSTEPS * (m + 1) + 1) + SLOTS - 1
    return first, (L0_SLOTS if m < 2 else SLOTS * (STEPS + 2) - first)


def moe_plan():
    plan = {}
    for m in range(3):
        ps = moe_pieces(m // 2)
        first, count = moe_slots(m)
        for i in range(count):
            lo, hi = (len(ps) * j // count for j in (i, i + 1))
            own = [("lg",)] * (i == 0) + [("le",)] * (i == 1) + ps[lo:hi]
            plan[first + i] = [(m, *x) for x in own]
    return plan


def two_layers(nc, x_tok, x_feat, ctx_feat, m_self, m_selfT, m_cross, m_crossT, att_w, w1_0, w2_0,
               w1_1, w2_1, gate_w, rows, cols, cols64, b1c, b2, ident, identb, hmask, shift_ones,
               before, out):
    ctx = ExitStack()
    with ctx:
        def sb(name, shape, dt=F32):
            return ctx.enter_context(nc.sbuf_tensor(name, shape, dt))

        def sig(name, per):
            return Signal(ctx.enter_context(nc.semaphore(name)), per)

        WA = sb("WA", [128, 16, 128])
        W1 = [sb("W1a", [128, E0, HID]), sb("W1b", [128, E1, HID])]
        W2 = [sb("W2a", [128, E0, HC, D]), sb("W2b", [128, E1, HC, D])]
        GW = sb("GW", [128, 2, NE])
        RV = sb("RV", [128, len(ROWS) * D + NE])
        CV = sb("CV", [128, len(COLS)])
        CR = sb("CR", [128, 1])
        C64 = sb("C64", [64, 8])
        QB = sb("QB", [64, 4])
        B1 = sb("B1", [128, E0, HC])
        B2 = sb("B2", [NE, D])
        ID = sb("ID", [128, 128])
        IDB = sb("IDB", [128, 128], BF16)
        HM = sb("HM", [64, HALF])
        BEF = sb("BEF", [128, NE, NE])
        BS = sb("BS", [128, 2, D])
        EXPN = sb("EXPN", [128, 3])
        TICK = sb("TICK", [128, 7])
        Xin = sb("Xin", [128, GB, D])
        XFin = sb("XFin", [128, T])
        CF = [sb(f"CF{i}", [128, T]) for i in range(2)]
        X = [sb(f"X{i}", [128, GB, D]) for i in range(2)]
        XA = sb("XA", [128, T])
        XB = sb("XB", [128, T])
        XH = [sb(f"XH{i}", [128, T], F32R) for i in range(2)]
        XL = [sb(f"XL{i}", [128, T], F32R) for i in range(2)]
        XT = sb("XT", [128, 2, D])
        MI = sb("MI", [128, 2, GB, S], I32)
        MA = [sb(f"MA{i}", [128, 4, GB, S], BF16) for i in range(2)]
        MZ = sb("MZ", [128, 2, S])
        MF = sb("MF", [128, 2, GB, 4])
        K9 = sb("K9", [64, 2, 2, S])
        KX = [sb(f"KX{i}", [KR, H, S]) for i in range(3)]
        KB = sb("KB", [KR, H, S], BF16)
        Q9 = [sb(f"Q9{i}", [KR, 2, S]) for i in range(4)]
        QS = [sb(f"QS{i}", [KR, 2, S], BF16) for i in range(4)]
        VA = [sb(f"VA{i}", [128, H, HD + 1]) for i in range(4)]
        MX = sb("MX", [128, 2, H])
        SM = sb("SM", [128, 2, 4, S], BF16)
        NM = sb("NM", [128, 2, 2, SR])
        PT = sb("PT", [128, 2, 4, S])
        CA = sb("CA", [128, 2, H])
        CE = sb("CE", [128, 2, H])
        OT = sb("OT", [128, 2, 4, S])
        CW = sb("CW", [128, 2, H, HD + 1])
        OW = sb("OW", [128, H, HD + 1])
        RS = sb("RS", [128, 2, H])
        AN = sb("AN", [128, 2, D])
        AT = sb("AT", [128, 2, S])
        RR = sb("RR", [128, 2, D])
        BN = sb("BN", [128, 2, 6])
        MV = sb("MV", [128, 2, 2])
        SQ = sb("SQ", [128, D])
        SS = sb("SS", [128, 2])
        RE = sb("RE", [128, 2])
        RD = sb("RD", [128, 2])
        YN = sb("YN", [128, 2, D])
        YG = sb("YG", [128, D])
        JB = sb("JB", [128, GB, 6])
        JM = sb("JM", [128, GB, 2])
        JS = sb("JS", [128, GB])
        JE = sb("JE", [128, GB])
        JD = sb("JD", [128, 2, GB])
        JT = sb("JT", [128, GB, D])
        WH = sb("WH", [128, 2, HID], F32R)
        WL = sb("WL", [128, 2, HID], F32R)
        HT = sb("HT", [128, 2, HC, T])
        LG = sb("LG", [128, GB, NE])
        LM = sb("LM", [128, GB])
        LZ = sb("LZ", [128, GB, NE])
        LE = sb("LE", [128, GB, NE])
        GT = sb("GT", [128, GB, NE, NE])
        EQ = sb("EQ", [128, GB, NE, NE])
        RK = sb("RK", [128, GB, NE])
        GE = sb("GE", [128, GB, NE])
        GS = sb("GS", [128, GB])
        GR = sb("GR", [128, GB])
        G = sb("G", [128, GB, NE])
        GTT = JT[0:NE]

        bank = [ctx.enter_context(nc.psum_tensor(f"bank{i}", [128, 512], F32)) for i in range(8)]
        OB, TB, MB, PB = bank[2:6]
        PK, PV = PB[0:64, 0:256], PB[:, 256:384]

        def q_bank(n):
            return (MB if n < 2 else PB)[0:64, 0:256]

        S2_TWO = LSTEPS + 1

        def s1_two(n):
            return n < LSTEPS + 2 or any(moe_slots(m)[0] + moe_slots(m)[1] < SLOTS * (n - 1) and
                                         SLOTS * n < moe_slots(m + 1)[0] for m in range(2))

        def s1_bank(n, g):
            return bank[(0, 7)[g % 2]] if s1_two(n) else bank[0]

        def s2_bank(n, g):
            return bank[(1, 6)[g % 2]] if n < S2_TWO else bank[1]

        def h_bank(m, e, c):
            if m == 3:
                return bank[(6, 0, 1, 2)[c]]
            if m == 2 and e >= LAST_TWO:
                return bank[(6, 0)[c % 2]]
            return bank[(6, 7)[c % 2] if e == 0 else 6]

        LAST_TWO = 7

        def lg_bank(m):
            return bank[5] if m == 3 else bank[7]

        def y_bank(m, e):
            return bank[(7, 3)[e % 2]] if m == 3 else bank[7]

        w_first = sig("w_first", 0)
        w_in = sig("w_in", 0)
        moe_w = [sig("moe_w0", 0), sig("moe_w1", 0)]
        x_in = sig("x_in", 32)
        xf_in = sig("xf_in", 32)
        c_in = [sig("c_in0", 16), sig("c_in1", 16)]
        m_in = sig("m_in", 128)
        out_done = [sig("out_done0", 16), sig("out_done1", 16)]
        c_zero = sig("c_zero", 0)
        c_qb = sig("c_qb", 0)
        c_bs = sig("c_bs", 0)
        kx_ones = sig("kx_ones", 0)
        kb_ones = sig("kb_ones", 0)
        N, N0 = STEPS, STEPS // 2
        EX = moe_first(4)
        pk = sig("pk", N)
        pq = sig("pq", N)
        s1 = sig("s1", 4 * N)
        nmt = sig("nmt", N)
        s2 = sig("s2", 4 * N)
        av = sig("av", 4 * N)
        wz = sig("wz", N0)
        ott = sig("ott", N)
        ant = sig("ant", N)
        zo = sig("zo", N)
        xtt = sig("xtt", N)
        lgt = sig("lgt", 4)
        gtt = sig("gtt", 2)
        b2t = sig("b2t", 2)
        ht = sig("ht", HC * EX)
        yt = sig("yt", EX)
        jxt = sig("jxt", 2)
        k9 = sig("k9", N)
        va = sig("va", N)
        kb = sig("kb", N)
        mx = sig("mx", 4 * N)
        nm = sig("nm", N)
        ca = sig("ca", N0)
        cw = sig("cw", N0)
        ow = sig("ow", N0)
        rs = sig("rs", N)
        an = sig("an", N)
        rr = sig("rr", N)
        bns = sig("bns", N0)
        mv = sig("mv", N0)
        ss = sig("ss", N0)
        yn = sig("yn", N)
        lg = sig("lg", 4)
        lm = sig("lm", 4)
        lz = sig("lz", 4)
        lgr = sig("lgr", 16)
        ge = sig("ge", 4)
        gs = sig("gs", 4)
        gr = sig("gr", 4)
        gg = sig("gg", 4)
        xb2 = sig("xb2", 2)
        hs = sig("hs", HC * 2 * E1)
        acc = sig("acc", EX)
        mf = sig("mf", 6)
        mz = sig("mz", N0)
        jb = sig("jb", 2)
        jm = sig("jm", 2)
        jt = sig("jt", 6)
        js = sig("js", 2)
        jy = sig("jy", 2)
        q9 = sig("q9", N)
        qs = sig("qs", N)
        nmc = sig("nmc", N)
        ce = sig("ce", N0)
        ex = sig("ex", 4 * N)
        otc = sig("otc", N)
        atc = sig("atc", N)
        xtc = sig("xtc", N)
        le = sig("le", 4)
        gtc = sig("gtc", 2)
        hr = sig("hr", HC * 2 * E0)
        th = sig("th", HC * 2 * E1)
        jxc = sig("jxc", 2)
        wh = sig("wh", EX)
        x0 = sig("x0", 2)
        ma = sig("ma", 4)
        xl = sig("xl", N0)
        wl = sig("wl", EX)
        kx = sig("kx", N)
        re = sig("re", N)
        rd = sig("rd", N)
        yg = sig("yg", N0)
        xg = sig("xg", N0)
        je = sig("je", 4)
        jd = sig("jd", 4)

        def row(name):
            i = ROWS.index(name)
            return RV[:, i * D:(i + 1) * D]

        def col(name):
            i = COLS.index(name)
            return CV[:, i:i + 1]

        def stage(n):
            ph, s = divmod(n, LSTEPS)
            return ph // 2, ph % 2, s // GB, s % GB

        def tok(t, b):
            return t[:, b * S:(b + 1) * S]

        def q_input(n):
            l, g, a, b = stage(n)
            return tok([[XFin, XB], [XA, XB]][l][a], b)

        def kv_input(n):
            l, g, a, b = stage(n)
            return tok(CF[g] if a else [XFin, XA][l], b)

        def hidden_done(m, k):
            return (hr, HC * E0 * (m % 2) + k) if m < 2 else (hs, HC * E1 * (m % 2) + k)

        plan = moe_plan()

        def pieces(n, g):
            return plan.get(SLOTS * n + g, ())

        def after(n, g, slots):
            return [m for m in range(2) if sum(moe_slots(m)) - 1 + slots == SLOTS * n + g]

        J_STATS, J_NORM, J_SQUARES, J_RMS, J_INPUT = JSLOTS

        alone = [(3, "lg"), (3, *moe_pieces(1)[0]), (3, *moe_pieces(1)[1]), (3, "le"),
                 *((3, *p) for p in moe_pieces(1)[2:])]

        block = ctx.enter_context(nc.Block())

        @block.sync
        def _(sp):
            for g in range(2):
                sp.sem_inc(out_done[g].sem, 16)

            def x_load(g):
                sp.dma_start(Xin[:], x_tok[:, bass.ds(g * GB, GB), :]).then_inc(x_in.sem, 16)

            def xf_load(g):
                sp.dma_start(XFin[:], x_feat[:, bass.ds(g * T, T)]).then_inc(xf_in.sem, 16)

            def c_load(g, half):
                sp.dma_start(CF[half][:], ctx_feat[:, bass.ds(g * T, T)])\
                    .then_inc(c_in[half].sem, 16)

            def m_load(g, a):
                for i, m in enumerate(((m_self, m_selfT), (m_cross, m_crossT))[a]):
                    sp.dma_start(MI[:, i], m[:, bass.ds(g * GB, GB), :]).then_inc(m_in.sem, 16)

            xf_load(0)
            for tile, src in ((C64[:], cols64), (HM[:], hmask), (CV[:], cols),
                              (RV[:], bass.AP(rows.tensor, 0, [[0, 128], [1, rows.shape[1]]]))):
                sp.dma_start(tile, src).then_inc(w_first.sem, 16)
            for tile, src in ((ID, ident), (IDB, identb), (GW, gate_w), (B1, b1c), (B2, b2)):
                sp.dma_start(tile[:], src).then_inc(w_in.sem, 16)
            sp.dma_start(BEF[:].rearrange("p i j -> p (i j)"),
                         bass.AP(before.tensor, 0, [[0, 128], [1, before.shape[1]]]))\
                .then_inc(w_in.sem, 16)
            c_load(0, 0)
            x_load(0)
            m_load(0, 0)
            for l, (a, b) in enumerate(((w1_0, w2_0), (w1_1, w2_1))):
                for e in range((E0, E1)[l]):
                    sp.dma_start(W1[l][:, e], a[:, e]).then_inc(moe_w[l].sem, 16)
                    sp.dma_start(W2[l][:, e], b[:, e]).then_inc(moe_w[l].sem, 16)
                if l == 0:
                    c_load(1, 1)

            def turn(it, more):
                group = 2 * it
                sp.wait_ge(x0.sem, x0.at(it, 1))
                x_load(group + 1)
                sp.wait_ge(pk.sem, pk.at(it, GB))
                sp.wait_ge(pq.sem, pq.at(it, GB))
                xf_load(group + 1)
                sp.wait_ge(ma.sem, ma.at(it, 1))
                m_load(group, 1)
                sp.wait_ge(ma.sem, ma.at(it, 2))
                m_load(group + 1, 0)
                if more:
                    sp.wait_ge(x0.sem, x0.at(it, 2))
                    x_load(group + 2)
                sp.wait_ge(ma.sem, ma.at(it, 3))
                m_load(group + 1, 1)
                if more:
                    sp.wait_ge(pk.sem, pk.at(it, LSTEPS + GB))
                    sp.wait_ge(pq.sem, pq.at(it, LSTEPS + GB))
                    xf_load(group + 2)
                    sp.wait_ge(ma.sem, ma.at(it, 4))
                    m_load(group + 2, 0)
                    sp.wait_ge(pk.sem, pk.at(it, 3 * LSTEPS))
                    c_load(group + 2, 0)
                    sp.wait_ge(pk.sem, pk.at(it, 4 * LSTEPS))
                    c_load(group + 3, 1)
                for g in range(2):
                    sp.wait_ge(acc.sem, acc.at(it, moe_first(3 + g)))
                    sp.dma_start(out[:, bass.ds((group + g) * GB, GB), :], X[g][:])\
                        .then_inc(out_done[g].sem, 16)

            with sp.Fori(0, TURNS - 1) as it:
                turn(it, True)
            turn(TURNS - 1, False)
            for g in range(2):
                sp.wait_ge(out_done[g].sem, out_done[g].at(TURNS, 16))

        N_FIRST, N_CONST = 5, 7

        @block.tensor
        def _(pe):
            pe.wait_ge(w_first.sem, 16 * N_FIRST)
            pe.wait_ge(c_zero.sem, 1)

            with pe.Fori(0, TURNS) as it:
                def w_of(n):
                    l, g, a, b = stage(n)
                    return (2 * l + a) * 4

                def proj_kv(n):
                    l, g, a, b = stage(n)
                    if l == 0 and a == 0 and b == 0:
                        pe.wait_ge(xf_in.sem, xf_in.at(it, 16 * (g + 1)))
                    if l == 0 and a == 1 and b == 0:
                        pe.wait_ge(c_in[g].sem, c_in[g].at(it, 16))
                    if l == 1 and a == 0 and b == 0:
                        pe.wait_ge(jxc.sem, jxc.at(it, g + 1))
                    if n >= 3:
                        pe.wait_ge(qs.sem, qs.at(it, n))
                    elif n:
                        pe.wait_ge(va.sem, va.at(it, n))
                    w = w_of(n)
                    for h in range(2):
                        pe.matmul(PK[:, h * S:(h + 1) * S], WA[:, w + 1, h * 64:h * 64 + 64],
                                  kv_input(n), start=True, stop=True)
                    pe.matmul(PV, kv_input(n), WA[:, w + 2, :], start=True, stop=True)\
                        .then_inc(pk.sem, 1)

                def proj_q(n):
                    l, g, a, b = stage(n)
                    if n >= 2:
                        pe.wait_ge(va.sem, va.at(it, n + 1))
                    elif n:
                        pe.wait_ge(qs.sem, qs.at(it, n))
                    if n - 2 >= N0:
                        pe.wait_ge(cw.sem, cw.at(it, n - 2 - N0 + 1))
                    if a == 1:
                        pe.wait_ge(xtc.sem, xtc.at(it, n - GB + 1))
                    w = w_of(n)
                    for h in range(2):
                        mm = pe.matmul(q_bank(n)[:, h * S:(h + 1) * S], WA[:, w, h * 64:h * 64 + 64],
                                       q_input(n), start=True, stop=True)
                    mm.then_inc(pq.sem, 1)

                def scores1(n, g):
                    _, grp, _, _ = stage(n)
                    if g == 0:
                        pe.wait_ge(kb.sem, kb.at(it, n + 1))
                        pe.wait_ge(qs.sem, qs.at(it, n + 1))
                        if n == 2 * LSTEPS or n == 3 * LSTEPS:
                            pe.wait_ge(ma.sem, ma.at(it, 2 * grp + 2))
                    q = 4 * n + g
                    if s1_two(n) and n and not s1_two(n - 1) and g < 2:
                        if g == 0:
                            pe.wait_ge(mx.sem, mx.at(it, q))
                        else:
                            pe.wait_ge(acc.sem, acc.at(it, moe_first(n // LSTEPS)))
                    elif s1_two(n) and q > 1:
                        pe.wait_ge(mx.sem, mx.at(it, q - 1))
                    elif not s1_two(n):
                        pe.wait_ge(mx.sem, mx.at(it, q))
                    o = s1_bank(n, g)
                    pe.matmul(o[:], QS[n % 4][:, g // 2, :], KB[:, 4 * g:4 * g + 4, :],
                              start=True, stop=True).then_inc(s1.sem, 1)

                def shift_rows(n):
                    pe.wait_ge(nm.sem, nm.at(it, n + 1))
                    if n == 0:
                        pe.wait_ge(qs.sem, qs.at(it, 2))
                    if n == 1:
                        pe.wait_ge(nmc.sem, nmc.at(it, 1))
                    if n == 2:
                        pe.wait_ge(atc.sem, atc.at(it, 1))
                    if n >= 3:
                        pe.wait_ge(xtc.sem, xtc.at(it, n - 2))
                    for h in range(2):
                        mm = pe.transpose(MB[0:SR, h * S:(h + 1) * S], NM[:, n % 2, h, :], ID[:])
                    mm.then_inc(nmt.sem, 1)

                def scores2(n, g):
                    l, grp, a, b = stage(n)
                    q = 4 * n + g
                    if g == 0:
                        pe.wait_ge(kx.sem, kx.at(it, n + 1))
                        pe.wait_ge(nmc.sem, nmc.at(it, n + 1))
                    free = q if n >= S2_TWO else q - 1
                    if free > 0:
                        pe.wait_ge(ex.sem, ex.at(it, free))
                    o = s2_bank(n, g)
                    if l:
                        pe.matmul(o[:], IDB[:],
                                  MA[grp][:, 2 * a + 1, b:b + 1, :].broadcast_to((128, 4, S)),
                                  start=True, stop=False, skip_group_check=True)
                    for j in range(4):
                        mm = pe.matmul(o[:, j * S:(j + 1) * S], KX[n % 3][:, 4 * g + j, :],
                                       Q9[n % 4][:, g // 2, :], start=not l, stop=True,
                                       skip_group_check=True)
                    mm.then_inc(s2.sem, 1)

                def values(n, g):
                    pe.wait_ge(ex.sem, ex.at(it, 4 * n + g + 1))
                    if g == 0:
                        pe.wait_ge(va.sem, va.at(it, n + 1))
                        if n:
                            pe.wait_ge(otc.sem, otc.at(it, n))
                    for j in range(4):
                        mm = pe.matmul(OB[32 * j:32 * j + HD + 1, g * S:(g + 1) * S],
                                       VA[n % 4][:, 4 * g + j, :], PT[:, g % 2, j, :],
                                       start=True, stop=True, skip_group_check=True)
                    mm.then_inc(av.sem, 1)

                def masked_values(n):
                    l, g, a, b = stage(n)
                    pe.wait_ge(mz.sem, mz.at(it, n - N0 + 1))
                    pe.wait_ge(va.sem, va.at(it, min(n + 3, N)))
                    pe.wait_ge(qs.sem, qs.at(it, min(n + 2, N)))
                    if n > N0:
                        pe.wait_ge(cw.sem, cw.at(it, n - N0))
                    pe.matmul(PB[:, 0:H * (HD + 1)], MZ[:, n % 2, :],
                              VA[n % 4][:].rearrange("p h d -> p (h d)"), start=True, stop=True)\
                        .then_inc(wz.sem, 1)

                def token_major(n):
                    pe.wait_ge(otc.sem, otc.at(it, n + 1))
                    if n:
                        pe.wait_ge(rr.sem, rr.at(it, n))
                    for g in range(4):
                        mm = pe.transpose(TB[:, g * 128:(g + 1) * 128], OT[:, n % 2, g, :], ID[:])
                    mm.then_inc(ott.sem, 1)

                def heads_back(n):
                    pe.wait_ge(an.sem, an.at(it, n + 1))
                    if n + 1 < N:
                        pe.wait_ge(nmc.sem, nmc.at(it, n + 2))
                    else:
                        pe.wait_ge(xtc.sem, xtc.at(it, n - 1))
                    pe.transpose(MB[:, 0:128], AN[:, n % 2, :], ID[:]).then_inc(ant.sem, 1)

                def out_proj(n):
                    pe.wait_ge(atc.sem, atc.at(it, n + 1))
                    pe.matmul(TB[:, 0:128], AT[:, n % 2, :], WA[:, w_of(n) + 3, :],
                              start=True, stop=True).then_inc(zo.sem, 1)

                def feature_major(n):
                    pe.wait_ge(yn.sem, yn.at(it, n + 1))
                    if n + 1 < N:
                        pe.wait_ge(atc.sem, atc.at(it, n + 2))
                    else:
                        pe.wait_ge(xtc.sem, xtc.at(it, n))
                    pe.transpose(MB[:, 0:128], YN[:, n % 2, :], ID[:]).then_inc(xtt.sem, 1)

                def layer_input(m):
                    pe.wait_ge(jy.sem, jy.at(it, m + 1))
                    for b in range(GB):
                        mm = pe.transpose(bank[6][:, b * 128:(b + 1) * 128], JT[:, b, :], ID[:])
                    mm.then_inc(jxt.sem, 1)

                def logits(m):
                    l, g = divmod(m, 2)
                    pe.wait_ge(xl.sem, xl.at(it, (m + 1) * GB))
                    if m == 0:
                        pe.wait_ge(mx.sem, mx.at(it, 4 * (LSTEPS + 2)))
                        pe.wait_ge(ex.sem, ex.at(it, 4 * S2_TWO))
                    elif m < 3:
                        pe.wait_ge(acc.sem, acc.at(it, moe_first(m)))
                        pe.wait_ge(mx.sem, mx.at(it, 4 * (moe_slots(m)[0] // SLOTS + 1)))
                    else:
                        pe.wait_ge(cw.sem, cw.at(it, N0))
                    if m in (1, 2):
                        pe.wait_ge(jxc.sem, jxc.at(it, m))
                    for b in range(GB):
                        for x in (XH, XL):
                            mm = pe.matmul(lg_bank(m)[:, b * NE:(b + 1) * NE],
                                           tok(x[g], b).bitcast(F32), GW[:, l, :],
                                           start=x is XH, stop=x is XL)
                    mm.then_inc(lgt.sem, 1)
                    if m == 3:
                        pe.wait_ge(mx.sem, mx.at(it, 4 * N))
                        pe.wait_ge(ex.sem, ex.at(it, 4 * N))
                        pe.wait_ge(otc.sem, otc.at(it, N))
                        pe.wait_ge(rr.sem, rr.at(it, N))

                def hidden(m, e, c):
                    l, g = divmod(m, 2)
                    k = HC * e + c
                    back = HC if m == 3 else 2 if k <= HC or (m == 2 and k > HC * LAST_TWO) else 1
                    if m == 2 and e == LAST_TWO and c == 1:
                        pe.wait_ge(mx.sem, mx.at(it, 4 * N))
                    if m < 3 and k == 1:
                        pe.wait_ge(lg.sem, lg.at(it, m + 1))
                    if k >= back:
                        sig_, at = hidden_done(m, k - back + 1)
                        pe.wait_ge(sig_.sem, sig_.at(it, at))
                    if c == 0:
                        pe.wait_ge(wl.sem, wl.at(it, moe_first(m) + e + 1))
                    slot = (moe_first(m) + e) % 2
                    for i, (w, x) in enumerate(((WH, XH), (WH, XL), (WL, XH))):
                        mm = pe.matmul(h_bank(m, e, c)[:], w[:, slot, c * 128:(c + 1) * 128],
                                       x[g][:], start=i == 0, stop=i == 2)
                    mm.then_inc(ht.sem, 1)

                def expert_out(m, e, b):
                    l, g = divmod(m, 2)
                    if b == 0:
                        sig_, at = hidden_done(m, HC * (e + 1))
                        pe.wait_ge(sig_.sem, sig_.at(it, at))
                        if e == 0 and m == 3:
                            pe.wait_ge(acc.sem, acc.at(it, moe_first(3)))
                        elif e == 0:
                            pe.wait_ge(lg.sem, lg.at(it, m + 1))
                        elif e == 1 and l == 0:
                            pe.wait_ge(xb2.sem, xb2.at(it, m + 1))
                        elif m == 3 and e >= 2:
                            pe.wait_ge(acc.sem, acc.at(it, moe_first(m) + e - 1))
                        elif m < 3:
                            pe.wait_ge(acc.sem, acc.at(it, moe_first(m) + e))
                    for c in range(HC):
                        mm = pe.matmul(y_bank(m, e)[:, b * 128:(b + 1) * 128],
                                       HT[:, e % 2, c, b * 128:(b + 1) * 128],
                                       W2[l][:, e, c, :], start=(c == 0), stop=(c == HC - 1),
                                       skip_group_check=True)
                    if b == GB - 1:
                        mm.then_inc(yt.sem, 1)

                def gates_back(m):
                    pe.wait_ge(gg.sem, gg.at(it, m + 1))
                    pe.wait_ge(acc.sem, acc.at(it, moe_first(m) + 1))
                    for b in range(GB):
                        mm = pe.transpose(bank[7][0:NE, b * 128:(b + 1) * 128], G[:, b, :], ID[:])
                    mm.then_inc(gtt.sem, 1)

                def gates_b2(m):
                    pe.wait_ge(gtc.sem, gtc.at(it, m + 1))
                    for b in range(GB):
                        mm = pe.matmul(bank[7][:, b * 128:(b + 1) * 128], GTT[:, b, :], B2[:],
                                       start=True, stop=True)
                    mm.then_inc(b2t.sem, 1)

                def experts(ps):
                    for m, kind, *at in ps:
                        if kind == "lg":
                            logits(m)
                        elif kind == "h":
                            hidden(m, *at)
                        elif kind == "y":
                            expert_out(m, *at)
                        elif kind == "gt":
                            gates_back(m)
                        elif kind == "b2":
                            gates_b2(m)

                proj_kv(0)
                proj_q(0)
                proj_kv(1)
                proj_q(1)
                proj_kv(2)
                pe.wait_ge(w_in.sem, 16 * N_CONST)
                pe.wait_ge(kx_ones.sem, 16 * 3)
                pe.wait_ge(kb_ones.sem, 1)
                for g in range(4):
                    scores1(0, g)
                shift_rows(0)
                for n in range(N + 2):
                    on, more, last = n < N, n + 1 < N, 1 <= n <= N
                    if more:
                        scores1(n + 1, 0)
                    if on:
                        scores2(n, 0)
                    if last:
                        token_major(n - 1)
                    if more:
                        scores1(n + 1, 1)
                    experts(pieces(n, 0))
                    if on:
                        if n >= N0:
                            masked_values(n)
                        scores2(n, 1)
                        values(n, 0)
                    if last:
                        heads_back(n - 1)
                    if more:
                        scores1(n + 1, 2)
                    experts(pieces(n, 1))
                    if n >= 2:
                        feature_major(n - 2)
                    if last:
                        out_proj(n - 1)
                    if on:
                        scores2(n, 2)
                        values(n, 1)
                    if n + 2 < N:
                        proj_q(n + 2)
                    if more:
                        scores1(n + 1, 3)
                    experts(pieces(n, 2))
                    for m in after(n, 2, J_INPUT):
                        layer_input(m)
                    if on:
                        scores2(n, 3)
                        values(n, 2)
                    if more:
                        shift_rows(n + 1)
                    if n + 3 < N:
                        proj_kv(n + 3)
                    experts(pieces(n, 3))
                    if on:
                        values(n, 3)
                experts(alone)
                pe.wait_ge(acc.sem, acc.at(it, EX))

        @block.scalar
        def _(act):
            act.dma_start(WA[:, 0:4], att_w[:, 0:4]).then_inc(w_first.sem, 16)
            for t in KX:
                act.dma_start(t[KR - SR:KR], shift_ones).then_inc(kx_ones.sem, 16)
            act.dma_start(WA[:, 4:], att_w[:, 4:]).then_inc(w_in.sem, 16)
            act.wait_ge(w_first.sem, 16 * N_FIRST)
            act.wait_ge(c_zero.sem, 1)
            for a in range(2):
                for h in range(2):
                    act.activation(QB[:, 2 * a + h:2 * a + h + 1], C64[:, 4 * a + h:4 * a + h + 1],
                                   ACT.Copy, scale=SCALE).then_inc(c_qb.sem, 1)
            act.activation(CR[:], col("norm1_w"), ACT.Copy, scale=float(D) ** 0.5)\
                .then_inc(c_qb.sem, 1)
            act.wait_ge(c_qb.sem, 5)

            with act.Fori(0, TURNS) as it:
                def queries(n):
                    l, g, a, b = stage(n)
                    act.wait_ge(pq.sem, pq.at(it, n + 1))
                    if l == 0:
                        for h in range(2):
                            i = act.activation(Q9[n % 4][0:64, h, :], q_bank(n)[:, h * S:(h + 1) * S],
                                               ACT.Identity, scale=SCALE,
                                               bias=QB[:, 2 * a + h:2 * a + h + 1])
                    else:
                        i = act.activation(Q9[n % 4][0:64, :, :].rearrange("p h t -> p (h t)"), q_bank(n),
                                           ACT.Copy, scale=SCALE)
                    i.then_inc(q9.sem, 1)
                    act.wait_ge(q9.sem, q9.at(it, n + 1))
                    act.activation(QS[n % 4][0:64, :, :], Q9[n % 4][0:64, :, :], ACT.Copy)\
                        .then_inc(qs.sem, 1)

                def exps(n, g):
                    act.wait_ge(s2.sem, s2.at(it, 4 * n + g + 1))
                    act.activation(PT[:, g % 2], s2_bank(n, g)[:], ACT.Exp).then_inc(ex.sem, 1)

                def shift_copy(n):
                    act.wait_ge(nmt.sem, nmt.at(it, n + 1))
                    act.activation(Q9[n % 4][64:96, :, :],
                                   MB[0:SR, 0:2 * S].rearrange("p (h t) -> p h t", h=2),
                                   ACT.Copy).then_inc(nmc.sem, 1)
                    if n >= N0:
                        act.wait_ge(ca.sem, ca.at(it, n - N0 + 1))
                        act.activation(CE[:, n % 2], CA[:, n % 2], ACT.Exp).then_inc(ce.sem, 1)

                def values_copy(n):
                    act.wait_ge(av.sem, av.at(it, 4 * n + 4))
                    act.activation(OT[:, n % 2].rearrange("p g t -> p (g t)"), OB[:],
                                   ACT.Copy).then_inc(otc.sem, 1)

                def heads_copy(n):
                    act.wait_ge(ant.sem, ant.at(it, n + 1))
                    act.activation(AT[:, n % 2, :], MB[:, 0:128], ACT.Copy).then_inc(atc.sem, 1)

                def norm_scale(n):
                    l, g, a, b = stage(n)
                    name = [["n1", "n2"], ["norm2", "norm3"]][l][a]
                    act.wait_ge(xtt.sem, xtt.at(it, n + 1))
                    if a == 1 and n > GB + 1:
                        act.wait_ge(xl.sem, xl.at(it, (n // LSTEPS) * GB + b - 1))
                    for dst in ((tok(XB, b),), (XT[:, n % 2], tok(XH[g], b)))[a]:
                        i = act.activation(dst, MB[:, 0:128], ACT.Identity,
                                           scale=col(name + ("_w" if l else "_g")),
                                           bias=0.0 if l else col(name + "_b"))
                    i.then_inc(xtc.sem, 1)

                def split_weights(x):
                    m = max(j for j in range(4) if moe_first(j) <= x)
                    if x == moe_first(m) and m in (0, 2):
                        act.wait_ge(moe_w[m // 2].sem, 16 * 2 * (E0, E1)[m // 2])
                    if x >= 2:
                        act.wait_ge(ht.sem, ht.at(it, HC * (x - 1)))
                    act.activation(WH[:, x % 2], W1[m // 2][:, x - moe_first(m)], ACT.Copy)\
                        .then_inc(wh.sem, 1)

                def experts(ps):
                    for m, kind, *at in ps:
                        if kind == "lg" and m == 0:
                            act.wait_ge(w_in.sem, 16 * N_CONST)
                        if kind == "le":
                            act.wait_ge(lz.sem, lz.at(it, m + 1))
                            act.activation(LE[:], LZ[:], ACT.Exp).then_inc(le.sem, 1)
                        elif kind == "gt":
                            act.wait_ge(gtt.sem, gtt.at(it, m + 1))
                            act.activation(GTT[:].rearrange("p b t -> p (b t)"), bank[7][0:NE, :],
                                           ACT.Copy).then_inc(gtc.sem, 1)
                        elif kind == "h":
                            e, c = at
                            act.wait_ge(ht.sem, ht.at(it, HC * (moe_first(m) + e) + c + 1))
                            if m < 2:
                                act.activation(HT[:, e % 2, c, :], h_bank(m, e, c)[:], ACT.Relu,
                                               bias=B1[:, e, c:c + 1]).then_inc(hr.sem, 1)
                            else:
                                act.activation(HT[:, e % 2, c, :], h_bank(m, e, c)[:], ACT.Tanh,
                                               scale=0.5).then_inc(th.sem, 1)
                            if c == 0 and moe_first(m) + e + 1 < EX:
                                split_weights(moe_first(m) + e + 1)

                queries(0)
                queries(1)
                shift_copy(0)
                for n in range(N + 2):
                    if n == GB:
                        split_weights(0)
                    on, more, last = n < N, n + 1 < N, 1 <= n <= N
                    if last:
                        values_copy(n - 1)
                    if on:
                        exps(n, 0)
                    experts(pieces(n, 0))
                    if last:
                        heads_copy(n - 1)
                    if on:
                        exps(n, 1)
                    experts(pieces(n, 1))
                    if n >= 2:
                        norm_scale(n - 2)
                    if on:
                        exps(n, 2)
                    experts(pieces(n, 2))
                    for m in after(n, 2, J_INPUT):
                        act.wait_ge(jxt.sem, jxt.at(it, m + 1))
                        act.activation(XA[:], bank[6][:], ACT.Copy, scale=CR[:])\
                            .then_inc(jxc.sem, 1)
                    if n + 2 < N:
                        queries(n + 2)
                    if on:
                        exps(n, 3)
                    if more:
                        shift_copy(n + 1)
                    experts(pieces(n, 3))
                experts(alone)

        @block.vector
        def _(dve):
            dve.memset(NM[:], 0.0)
            dve.memset(OB[:], 0.0)
            for t in Q9:
                dve.memset(t[64:96], 0.0)
            for t in VA:
                dve.memset(t[:, :, HD:HD + 1], 1.0)
            for t in QS:
                i = dve.memset(t[64:96], 0.0)
            i.then_inc(c_zero.sem, 1)
            dve.wait_ge(w_first.sem, 16 * N_FIRST)
            dve.tensor_tensor(BS[:, 0], row("n1_b"), row("ca_bo"), ALU.add).then_inc(c_bs.sem, 1)
            dve.tensor_copy(BS[:, 1], row("n2_b")).then_inc(c_bs.sem, 1)
            dve.wait_ge(kx_ones.sem, 16 * 3)
            dve.tensor_copy(KB[64:96], KX[0][64:96]).then_inc(kb_ones.sem, 1)

            with dve.Fori(0, TURNS) as it:
                def keys_values(n):
                    l, g, a, b = stage(n)
                    dve.wait_ge(pk.sem, pk.at(it, n + 1))
                    if n >= 2:
                        dve.wait_ge(kx.sem, kx.at(it, n - 1))
                    if l == 0:
                        for h in range(2):
                            i = dve.tensor_scalar(K9[:, n % 2, h, :], PK[:, h * S:(h + 1) * S],
                                                  C64[:, 4 * a + 2 + h:4 * a + 3 + h], None, ALU.add)
                    else:
                        i = dve.tensor_copy(K9[:, n % 2].rearrange("p h t -> p (h t)"), PK)
                    i.then_inc(k9.sem, 1)
                    v = PV.rearrange("p (h d) -> p h d", h=H)
                    if l == 0:
                        i = dve.tensor_tensor(VA[n % 4][:, :, 0:HD], v,
                                              row(("sa_bv", "ca_bv")[a]).rearrange(
                                                  "p (h d) -> p h d", h=H), ALU.add)
                    else:
                        i = dve.tensor_copy(VA[n % 4][:, :, 0:HD], v)
                    i.then_inc(va.sem, 1)

                def keys_bf16(n):
                    dve.wait_ge(kx.sem, kx.at(it, n + 1))
                    dve.tensor_copy(KB[0:64], KX[n % 3][0:64]).then_inc(kb.sem, 1)

                def row_max(n, g):
                    dve.wait_ge(s1.sem, s1.at(it, 4 * n + g + 1))
                    l, grp, a, b = stage(n)
                    if l == 0:
                        i = dve.tensor_reduce(MX[:, n % 2, 4 * g:4 * g + 4],
                                              s1_bank(n, g)[:].rearrange("p (j k) -> p j k", j=4),
                                              AX.X, ALU.max)
                    else:
                        dve.tensor_copy(TICK[:, 3 + g:4 + g], CV[:, 0:1])
                        for j in range(4):
                            h = 4 * g + j
                            i = dve.tensor_tensor_reduce(SM[:, g % 2, j], s1_bank(n, g)[:, j * S:(j + 1) * S],
                                                         MA[grp][:, 2 * a, b], 1.0, -BIG, ALU.add,
                                                         ALU.max, accum_out=MX[:, n % 2, h:h + 1])
                    i.then_inc(mx.sem, 1)

                def shift(n):
                    l, g, a, b = stage(n)
                    dve.wait_ge(mx.sem, mx.at(it, 4 * n + 4))
                    src = MX[:, n % 2].rearrange("p (a h) -> p a h", a=2)
                    dst = NM[:, n % 2, :, 0:HALF]
                    if l == 0:
                        dve.tensor_scalar(dst, src, -1.0, None, ALU.mult).then_inc(nm.sem, 1)
                    else:
                        dve.tensor_scalar(dst, src, MF[:, a, b, 3:4], -1.0, ALU.max, ALU.mult)\
                            .then_inc(nm.sem, 1)
                        dve.wait_ge(nm.sem, nm.at(it, n + 1))
                        dve.tensor_scalar(CA[:, n % 2].rearrange("p (a h) -> p a h", a=2), dst,
                                          NEG, 0.0, ALU.add, ALU.min).then_inc(ca.sem, 1)

                def mask_ones(n):
                    l, g, a, b = stage(n)
                    dve.tensor_scalar(MZ[:, n % 2], MA[g][:, 2 * a + 1, b], 0.0, None, ALU.is_lt)\
                        .then_inc(mz.sem, 1)

                def masked_sum(n):
                    m = n - N0
                    dve.wait_ge(wz.sem, wz.at(it, m + 1))
                    dve.wait_ge(ce.sem, ce.at(it, m + 1))
                    c = CE[:, n % 2].rearrange("p (h o) -> p h o", o=1)\
                        .broadcast_to((128, H, HD + 1))
                    dve.tensor_tensor(CW[:, n % 2],
                                      PB[:, 0:H * (HD + 1)].rearrange("p (h d) -> p h d", h=H),
                                      c, ALU.mult).then_inc(cw.sem, 1)

                def normalise(n):
                    dve.wait_ge(ott.sem, ott.at(it, n + 1))
                    o = TB[:].rearrange("p (h r) -> p h r", h=H)
                    if n >= N0:
                        m = n - N0
                        dve.wait_ge(cw.sem, cw.at(it, m + 1))
                        dve.tensor_tensor(OW[:], o[:, :, 0:HD + 1], CW[:, n % 2], ALU.add)\
                            .then_inc(ow.sem, 1)
                        dve.wait_ge(ow.sem, ow.at(it, m + 1))
                        o = OW[:]
                    dve.reciprocal(RS[:, n % 2].rearrange("p (h o) -> p h o", o=1), o[:, :, HD:HD + 1])\
                        .then_inc(rs.sem, 1)
                    dve.wait_ge(rs.sem, rs.at(it, n + 1))
                    r = RS[:, n % 2].rearrange("p (h o) -> p h o", o=1).broadcast_to((128, H, HD))
                    dve.tensor_tensor(AN[:, n % 2].rearrange("p (h d) -> p h d", h=H),
                                      o[:, :, 0:HD], r, ALU.mult).then_inc(an.sem, 1)

                def residual(n):
                    l, g, a, b = stage(n)
                    dve.wait_ge(zo.sem, zo.at(it, n + 1))
                    if l == 0:
                        if a == 0 and b == 0:
                            dve.wait_ge(x0.sem, x0.at(it, g + 1))
                        if a == 1:
                            dve.wait_ge(xg.sem, xg.at(it, n - GB + 1))
                        slot = n % 2
                        dve.tensor_tensor(RR[:, slot], TB[:, 0:128], X[g][:, b], ALU.add)\
                            .then_inc(rr.sem, 1)
                        dve.wait_ge(rr.sem, rr.at(it, n + 1))
                        dve.bn_stats(BN[:, slot], RR[:, slot]).then_inc(bns.sem, 1)
                        dve.wait_ge(bns.sem, bns.at(it, n + 1))
                        dve.tensor_copy(TICK[:, 1:2], BN[:, slot, 0:1])
                        dve.bn_aggr(MV[:, slot], BN[:, slot]).then_inc(mv.sem, 1)
                    else:
                        dve.tensor_tensor(X[g][:, b], TB[:, 0:128], X[g][:, b], ALU.add)\
                            .then_inc(rr.sem, 1)
                        dve.wait_ge(rr.sem, rr.at(it, n + 1))
                        dve.scalar_tensor_tensor(SQ[:], X[g][:, b], 1.0, X[g][:, b], ALU.mult,
                                                 ALU.mult, accum_out=SS[:, n % 2:n % 2 + 1])\
                            .then_inc(ss.sem, 1)

                def norm_out(n):
                    l, g, a, b = stage(n)
                    dve.wait_ge(rd.sem, rd.at(it, n + 1))
                    if n >= 2:
                        dve.wait_ge(xtt.sem, xtt.at(it, n - 1))
                    if l == 0:
                        dve.tensor_scalar(YN[:, n % 2], RR[:, n % 2], MV[:, n % 2, 0:1],
                                          RD[:, n % 2:n % 2 + 1], ALU.subtract, ALU.mult)\
                            .then_inc(yn.sem, 1)
                    else:
                        dve.tensor_scalar(YN[:, n % 2], X[g][:, b], RD[:, n % 2:n % 2 + 1],
                                          float(D) ** 0.5, ALU.mult, ALU.mult).then_inc(yn.sem, 1)

                def mask_floor(g):
                    for a in range(2):
                        i = dve.tensor_reduce(MF[:, a, :, 0:1].rearrange("p b o -> p (b o)"),
                                              MA[g][:, 2 * a], AX.X, ALU.min)
                    i.then_inc(mf.sem, 1)
                    dve.wait_ge(mf.sem, mf.at(it, 3 * g + 1))
                    dve.tensor_scalar(MF[:, :, :, 1], MF[:, :, :, 0], 0.0, -BIG,
                                      ALU.is_ge, ALU.mult)
                    dve.tensor_scalar(MF[:, :, :, 2], MF[:, :, :, 0], 0.0, NEG,
                                      ALU.is_lt, ALU.mult).then_inc(mf.sem, 1)
                    dve.wait_ge(mf.sem, mf.at(it, 3 * g + 2))
                    dve.tensor_tensor(MF[:, :, :, 3], MF[:, :, :, 1], MF[:, :, :, 2], ALU.add)\
                        .then_inc(mf.sem, 1)
                    dve.wait_ge(mf.sem, mf.at(it, 3 * g + 3))

                def per_batch(t):
                    return t.rearrange("p (b o) -> p b o", o=1).broadcast_to((128, GB, D))

                def junction_stats(m):
                    dve.wait_ge(acc.sem, acc.at(it, moe_first(m + 1)))
                    for b in range(GB):
                        i = dve.bn_stats(JB[:, b], X[m][:, b])
                    i.then_inc(jb.sem, 1)
                    dve.wait_ge(jb.sem, jb.at(it, m + 1))
                    dve.tensor_copy(TICK[:, 2:3], JB[:, 0, 0:1])
                    for b in range(GB):
                        i = dve.bn_aggr(JM[:, b], JB[:, b])
                    i.then_inc(jm.sem, 1)

                def junction_norm(m):
                    dve.wait_ge(jd.sem, jd.at(it, 2 * m + 1))
                    for b in range(GB):
                        i = dve.tensor_scalar(JT[:, b], X[m][:, b], JM[:, b, 0:1],
                                              JD[:, 0, b:b + 1], ALU.subtract, ALU.mult)
                    i.then_inc(jt.sem, 1)
                    dve.wait_ge(jt.sem, jt.at(it, 3 * m + 1))
                    g3 = row("n3_g").rearrange("p (o d) -> p o d", o=1).broadcast_to((128, GB, D))
                    dve.tensor_tensor(JT[:], JT[:], g3, ALU.mult).then_inc(jt.sem, 1)

                def junction_squares(m):
                    dve.wait_ge(jt.sem, jt.at(it, 3 * m + 2))
                    b3 = row("n3_b").rearrange("p (o d) -> p o d", o=1).broadcast_to((128, GB, D))
                    dve.tensor_tensor(X[m][:], JT[:], b3, ALU.add).then_inc(jt.sem, 1)
                    dve.wait_ge(jt.sem, jt.at(it, 3 * m + 3))
                    for b in range(GB):
                        i = dve.scalar_tensor_tensor(JT[:, b], X[m][:, b], 1.0, X[m][:, b],
                                                     ALU.mult, ALU.mult, accum_out=JS[:, b:b + 1])
                    i.then_inc(js.sem, 1)

                def junction_rms(m):
                    dve.wait_ge(jd.sem, jd.at(it, 2 * m + 2))
                    dve.wait_ge(js.sem, js.at(it, m + 1))
                    dve.tensor_tensor(JT[:], X[m][:], per_batch(JD[:, 1]), ALU.mult)\
                        .then_inc(jy.sem, 1)

                def junction(n, g):
                    for slots, stage_ in ((J_STATS, junction_stats), (J_NORM, junction_norm),
                                          (J_SQUARES, junction_squares), (J_RMS, junction_rms)):
                        for m in after(n, g, slots):
                            stage_(m)

                def rank(m):
                    dve.wait_ge(w_in.sem, 16 * N_CONST)
                    dve.wait_ge(lgt.sem, lgt.at(it, m + 1))
                    lgp = lg_bank(m)[:, 0:GB * NE].rearrange("p (b e) -> p b e", b=GB)
                    if m < 2:
                        rb = RV[:, len(ROWS) * D:].rearrange("p (o e) -> p o e", o=1)
                        i = dve.tensor_tensor(LG[:], lgp, rb.broadcast_to((128, GB, NE)), ALU.add)
                    else:
                        i = dve.tensor_copy(LG[:], lgp)
                    i.then_inc(lg.sem, 1)
                    dve.wait_ge(lg.sem, lg.at(it, m + 1))
                    dve.tensor_reduce(LM[:], LG[:], AX.X, ALU.max).then_inc(lm.sem, 1)
                    shape = (128, GB, NE, NE)
                    other = LG[:].rearrange("p b (o j) -> p b o j", o=1).broadcast_to(shape)
                    own = LG[:].rearrange("p b (i o) -> p b i o", o=1).broadcast_to(shape)
                    dve.tensor_tensor(GT[:], other, own, ALU.is_gt)
                    i = dve.tensor_tensor(EQ[:], other, own, ALU.is_equal)
                    i.then_inc(lgr.sem, 1)
                    dve.wait_ge(lm.sem, lm.at(it, m + 1))
                    lmb = LM[:].rearrange("p (b o) -> p b o", o=1).broadcast_to((128, GB, NE))
                    dve.tensor_tensor(LZ[:], LG[:], lmb, ALU.subtract).then_inc(lz.sem, 1)
                    dve.wait_ge(lgr.sem, lgr.at(it, 4 * m + 1))
                    bef = BEF[:].rearrange("p i j -> p (i j)").rearrange("p (o k) -> p o k", o=1)
                    eq = EQ[:].rearrange("p b i j -> p b (i j)")
                    dve.tensor_tensor(eq, eq, bef.broadcast_to((128, GB, NE * NE)), ALU.mult)\
                        .then_inc(lgr.sem, 1)
                    dve.wait_ge(lgr.sem, lgr.at(it, 4 * m + 2))
                    dve.tensor_tensor(GT[:], GT[:], EQ[:], ALU.add).then_inc(lgr.sem, 1)
                    dve.wait_ge(lgr.sem, lgr.at(it, 4 * m + 3))
                    dve.tensor_reduce(RK[:], GT[:], AX.X, ALU.add).then_inc(lgr.sem, 1)

                def gates(m):
                    dve.wait_ge(lgr.sem, lgr.at(it, 4 * m + 4))
                    dve.wait_ge(le.sem, le.at(it, m + 1))
                    dve.scalar_tensor_tensor(GE[:], RK[:], 1.5, LE[:], ALU.is_lt, ALU.mult)\
                        .then_inc(ge.sem, 1)
                    dve.wait_ge(ge.sem, ge.at(it, m + 1))
                    dve.tensor_reduce(GS[:], GE[:], AX.X, ALU.add).then_inc(gs.sem, 1)
                    dve.wait_ge(gs.sem, gs.at(it, m + 1))
                    dve.reciprocal(GR[:], GS[:]).then_inc(gr.sem, 1)
                    dve.wait_ge(gr.sem, gr.at(it, m + 1))
                    grb = GR[:].rearrange("p (b o) -> p b o", o=1).broadcast_to((128, GB, NE))
                    dve.scalar_tensor_tensor(G[:], GE[:], (1.0, 0.5)[m // 2], grb, ALU.mult,
                                             ALU.mult).then_inc(gg.sem, 1)

                def add_expert(m, e):
                    g, x = m % 2, moe_first(m) + e
                    y = y_bank(m, e)
                    dve.wait_ge(yt.sem, yt.at(it, x + 1))
                    if e == 0:
                        dve.wait_ge(gg.sem, gg.at(it, m + 1))
                        if m < 2:
                            dve.wait_ge(xg.sem, xg.at(it, (m + 1) * LSTEPS))
                    else:
                        dve.wait_ge(acc.sem, acc.at(it, x))
                    if e == NE:
                        dve.scalar_tensor_tensor(X[g][:].rearrange("p b d -> p (b d)"), y[:], 0.5,
                                                 X[g][:].rearrange("p b d -> p (b d)"), ALU.mult,
                                                 ALU.add).then_inc(acc.sem, 1)
                        return
                    for b in range(GB):
                        i = dve.scalar_tensor_tensor(
                            X[g][:, b], y[:, b * 128:(b + 1) * 128], G[:, b, e:e + 1],
                            X[g][:, b], ALU.mult, ALU.add)
                    i.then_inc(acc.sem, 1)

                def experts(ps):
                    for m, kind, *at in ps:
                        if kind == "lg":
                            rank(m)
                        elif kind == "le":
                            gates(m)
                        elif kind == "h" and m >= 2:
                            e, c = at
                            k = HC * (E1 * (m % 2) + e) + c + 1
                            dve.wait_ge(th.sem, th.at(it, k))
                            dve.scalar_tensor_tensor(HT[:, e % 2, c, :], HT[:, e % 2, c, :], 1.0,
                                                     h_bank(m, e, c)[:], ALU.add, ALU.mult)\
                                .then_inc(hs.sem, 1)
                        elif kind == "y" and at[1] == GB - 1:
                            add_expert(m, at[0])
                        elif kind == "b2":
                            dve.wait_ge(b2t.sem, b2t.at(it, m + 1))
                            dve.wait_ge(acc.sem, acc.at(it, moe_first(m) + 1))
                            x = X[m][:].rearrange("p b d -> p (b d)")
                            dve.tensor_tensor(x, bank[7][:], x, ALU.add).then_inc(xb2.sem, 1)
                            dve.wait_ge(xb2.sem, xb2.at(it, m + 1))

                keys_values(0)
                keys_values(1)
                keys_bf16(0)
                keys_values(2)
                for g in range(4):
                    row_max(0, g)
                shift(0)
                keys_bf16(1)
                for n in range(N + 2):
                    on, more, last = n < N, n + 1 < N, 1 <= n <= N
                    if more:
                        row_max(n + 1, 0)
                    if last:
                        normalise(n - 1)
                    if more:
                        row_max(n + 1, 1)
                    experts(pieces(n, 0))
                    junction(n, 0)
                    if N0 <= n < N:
                        masked_sum(n)
                    if n >= 2:
                        norm_out(n - 2)
                    if more:
                        row_max(n + 1, 2)
                    experts(pieces(n, 1))
                    junction(n, 1)
                    if last:
                        residual(n - 1)
                    if more:
                        row_max(n + 1, 3)
                        if n + 1 in (2 * LSTEPS, 3 * LSTEPS):
                            grp = (n + 1) // LSTEPS % 2
                            dve.wait_ge(ma.sem, ma.at(it, 2 * grp + 2))
                            mask_floor(grp)
                        shift(n + 1)
                        if n + 1 >= N0:
                            mask_ones(n + 1)
                    experts(pieces(n, 2))
                    junction(n, 2)
                    if n + 2 < N:
                        keys_bf16(n + 2)
                    if n + 3 < N:
                        keys_values(n + 3)
                    experts(pieces(n, 3))
                    junction(n, 3)
                experts(alone)

        @block.gpsimd
        def _(pool):
            pool.memset(EXPN[:, 0:1], -0.5)
            pool.memset(EXPN[:, 1:2], EPS)
            pool.memset(EXPN[:, 2:3], D * EPS).then_inc(c_bs.sem, 1)
            pool.wait_ge(w_first.sem, 16 * N_FIRST)
            pool.wait_ge(c_bs.sem, 3)

            with pool.Fori(0, TURNS) as it:
                def spread(n):
                    pool.wait_ge(k9.sem, k9.at(it, n + 1))
                    if n >= 3:
                        pool.wait_ge(s2.sem, s2.at(it, 4 * (n - 2)))
                        pool.wait_ge(kb.sem, kb.at(it, n - 2))
                    dst = KX[n % 3][0:64].rearrange("p (a h) t -> p a h t", a=2)
                    pool.tensor_tensor(dst[:, :, 0, :], K9[:, n % 2],
                                       HM[:, 0:1].rearrange("p (a o) -> p a o", a=1)
                                       .broadcast_to((64, 2, S)), ALU.mult)
                    for h in range(1, HALF):
                        i = pool.tensor_scalar(dst[:, :, h, :], K9[:, n % 2], HM[:, h:h + 1], 1.0,
                                               ALU.mult, ALU.mult)
                    i.then_inc(kx.sem, 1)

                def inverse_root(src, eps, n):
                    slot = n % 2
                    pool.tensor_tensor(RE[:, slot:slot + 1], src, EXPN[:, eps:eps + 1], ALU.add)\
                        .then_inc(re.sem, 1)
                    pool.wait_ge(re.sem, re.at(it, n + 1))
                    pool.tensor_tensor(RD[:, slot:slot + 1], RE[:, slot:slot + 1], EXPN[:, 0:1],
                                       ALU.pow).then_inc(rd.sem, 1)

                def junction_root(src, eps, m, k):
                    pool.tensor_tensor(JE[:], src, EXPN[:, eps:eps + 1].broadcast_to((128, GB)),
                                       ALU.add).then_inc(je.sem, 1)
                    pool.wait_ge(je.sem, je.at(it, 2 * m + k + 1))
                    pool.tensor_tensor(JD[:, k], JE[:], EXPN[:, 0:1].broadcast_to((128, GB)),
                                       ALU.pow).then_inc(jd.sem, 1)

                def junction(n, g):
                    for m in after(n, g, J_STATS):
                        pool.wait_ge(jm.sem, jm.at(it, m + 1))
                        junction_root(JM[:, :, 1], 1, m, 0)
                    for m in after(n, g, J_SQUARES):
                        pool.wait_ge(js.sem, js.at(it, m + 1))
                        junction_root(JS[:], 2, m, 1)

                def affine(n):
                    l, g, a, b = stage(n)
                    pool.wait_ge(yn.sem, yn.at(it, n + 1))
                    pool.tensor_tensor(YG[:], YN[:, n % 2], row(("n1_g", "n2_g")[a]), ALU.mult)\
                        .then_inc(yg.sem, 1)
                    pool.wait_ge(yg.sem, yg.at(it, n + 1))
                    pool.tensor_tensor(X[g][:, b], YG[:], BS[:, a], ALU.add).then_inc(xg.sem, 1)

                def low_input(n):
                    l, g, a, b = stage(n)
                    pool.wait_ge(xtc.sem, xtc.at(it, n + 1))
                    pool.tensor_tensor(tok(XL[g], b), XT[:, n % 2], tok(XH[g], b).bitcast(F32),
                                       ALU.subtract).then_inc(xl.sem, 1)

                def low_weights(x):
                    m = max(j for j in range(4) if moe_first(j) <= x)
                    pool.wait_ge(wh.sem, wh.at(it, x + 1))
                    pool.tensor_tensor(WL[:, x % 2], W1[m // 2][:, x - moe_first(m)],
                                       WH[:, x % 2].bitcast(F32), ALU.subtract)\
                        .then_inc(wl.sem, 1)

                def experts(ps):
                    for m, kind, *at in ps:
                        x = moe_first(m) + at[0] + 1 if kind == "h" and at[1] == 0 else EX
                        if x < EX:
                            low_weights(x)

                def group_masks(g, a):
                    pool.wait_ge(m_in.sem, m_in.at(it, 32 * (2 * g + a + 1)))
                    pool.tensor_tensor(TICK[:, 0:1], EXPN[:, 0:1], EXPN[:, 0:1], ALU.mult)
                    pool.tensor_scalar(MA[g][:, 2 * a:2 * a + 2].rearrange("p m b t -> p (m b t)"),
                                       MI[:].rearrange("p m b t -> p (m b t)"), 0.0, -BIG,
                                       ALU.is_equal, ALU.mult).then_inc(ma.sem, 1)

                bo = row("sa_bo").rearrange("p (o d) -> p o d", o=1).broadcast_to((128, GB, D))
                def layer0_input(g):
                    pool.wait_ge(x_in.sem, x_in.at(it, 16 * (g + 1)))
                    pool.wait_ge(out_done[g].sem, out_done[g].at(it, 16))
                    pool.tensor_tensor(X[g][:], Xin[:], bo, ALU.add).then_inc(x0.sem, 1)

                spread(0)
                spread(1)
                layer0_input(0)
                for n in range(N + 2):
                    if n + 2 < N:
                        spread(n + 2)
                    if n == GB:
                        low_weights(0)
                    experts(pieces(n, 0))
                    junction(n, 0)
                    if 2 <= n < N0 + 2:
                        affine(n - 2)
                    experts(pieces(n, 1))
                    junction(n, 1)
                    if n >= 2 and stage(n - 2)[2] == 1:
                        low_input(n - 2)
                    if 1 <= n <= N:
                        k = n - 1
                        if k < N0:
                            pool.wait_ge(mv.sem, mv.at(it, k + 1))
                            inverse_root(MV[:, k % 2, 1:2], 1, k)
                        else:
                            pool.wait_ge(ss.sem, ss.at(it, k - N0 + 1))
                            inverse_root(SS[:, k % 2:k % 2 + 1], 2, k)
                    if n in (2, 4):
                        group_masks(0, n // 2 - 1)
                    if n == 5:
                        layer0_input(1)
                    if n in (8, 10):
                        group_masks(1, n // 2 - 4)
                    experts(pieces(n, 2))
                    junction(n, 2)
                    experts(pieces(n, 3))
                    junction(n, 3)
                experts(alone)


def kernel(**inputs):
    import ml_dtypes
    import numpy as np
    import concourse.bacc as bacc
    from concourse.bass_utils import run_bass_kernel_spmd as run

    a = {k: np.asarray(v) for k, v in inputs.items()}
    p0 = lambda k: a["L0_xattn_" + k]
    p1 = lambda k: a["L1_xattn_" + k]
    c = np.ascontiguousarray
    x, ctx = a["x"], a["ctx_1024"]
    ms, mc = a["mask_BxSxS_ik0"], a["mask_BxSxS2_if1"]
    att = [p0(f"{s}_w{m}") for s in ("sa", "ca") for m in "qkvo"]
    att += [p1(f"{s}_w{m}").T for s in ("sa", "ca") for m in "qkvo"]
    w1_1 = np.concatenate([p1("exp_w1"), p1("sh_w1")[None]])
    w2_1 = np.concatenate([p1("exp_w2"), p1("sh_w2")[None]])
    half = lambda v: v.reshape(2, 64).T
    eye = np.eye(128, dtype=np.float32)
    ones = np.zeros((SR, H, S), np.float32)
    for h in range(H):
        ones[h % HALF, h] = 1.0
    head = np.zeros((64, HALF), np.float32)
    for h in range(HALF):
        head[h * HD:(h + 1) * HD, h] = 1.0
    arrays = {
        "x_tok": x.transpose(1, 0, 2),
        "x_feat": x.transpose(2, 0, 1).reshape(D, B * S),
        "ctx_feat": ctx.transpose(2, 0, 1).reshape(D, B * S),
        "m_self": ms.transpose(1, 0, 2), "m_selfT": ms.transpose(2, 0, 1),
        "m_cross": mc.transpose(1, 0, 2), "m_crossT": mc.transpose(2, 0, 1),
        "att_w": np.stack(att, 1),
        "w1_0": p0("e_w1").transpose(1, 0, 2),
        "w2_0": p0("e_w2").reshape(E0, HC, 128, D).transpose(2, 0, 1, 3),
        "w1_1": w1_1.transpose(2, 0, 1),
        "w2_1": w2_1.reshape(E1, D, HC, 128).transpose(3, 0, 2, 1),
        "gate_w": np.stack([p0("r_w"), p1("gate_w").T], 1),
        "rows": np.concatenate([p0(r) for r in ROWS] + [p0("r_b")])[None],
        "cols": np.stack([p0(v) for v in COLS[:4]] + [p1(v) for v in COLS[4:]], 1),
        "cols64": np.concatenate([half(p0(f"{s}_b{m}")) for s in ("sa", "ca") for m in "qk"], 1),
        "b1c": p0("e_b1").reshape(E0, HC, 128).transpose(2, 0, 1),
        "b2": p0("e_b2"),
        "ident": eye, "identb": eye.astype(ml_dtypes.bfloat16),
        "hmask": head, "shift_ones": ones,
        "before": np.tril(np.ones((NE, NE), np.float32), -1).reshape(1, NE * NE),
    }
    nc = bacc.Bacc("TRN2", target_bir_lowering=False, num_devices=1)
    feed, args = {}, []
    for name, v in arrays.items():
        v = c(v)
        feed[name] = v
        args.append(nc.dram_tensor(name, v.shape, mybir.dt.from_np(v.dtype),
                                   kind="ExternalInput").ap())
    out = nc.dram_tensor("out", (S, B, D), F32, kind="ExternalOutput").ap()
    two_layers(nc, *args, out)
    r = run(nc, [feed], core_ids=[0])
    return r.results[0]["out"].transpose(1, 0, 2)
```
